# Optimizing a Trainium2 kernel written in Bass

```python
import numpy as np
import jax
import jax.numpy as jnp

def _softmax(x, axis=-1):
    return jax.nn.softmax(x, axis=axis)

def _gelu(x):
    return jax.nn.gelu(x, approximate=True)

def _silu(x):
    return jax.nn.silu(x)

def _sigmoid(x):
    return jax.nn.sigmoid(x)

def _layernorm(x, axis=-1, eps=1e-05):
    m = jnp.mean(x, axis=axis, keepdims=True)
    v = jnp.var(x, axis=axis, keepdims=True)
    return (x - m) / jnp.sqrt(v + eps)

def _scatter_add(tgt, idx, src, axis=0):
    return tgt.at[idx].add(src)

def _segment_sum(src, seg, n):
    return jax.ops.segment_sum(src, seg, n)
kernel_name = 'mk_adaln_attn_ffn_d2_seqx_r8_0bf00c'

def setup_inputs(seed: int=0):
    np.random.seed(seed)
    _w = jnp.asarray

    def _rec_inputs():
        import jax
        import jax.numpy as jnp
        _rk = jax.random.key(seed)
        x = -0.0003929 + 0.9999 * jax.random.normal(jax.random.fold_in(_rk, 1), (2, 512, 128), jnp.float32)
        _lenS = 512 - jax.random.randint(jax.random.fold_in(_rk, 7), (2,), 0, max(1, 512 // 4) + 1, jnp.int32)
        _lenS2 = 512 - jax.random.randint(jax.random.fold_in(_rk, 8), (2,), 0, max(1, 512 // 4) + 1, jnp.int32)
        itok_B_0_7 = jax.random.randint(jax.random.fold_in(_rk, 11), (2,), 0, 8, jnp.int32)
        itok_B_0_6 = jax.random.randint(jax.random.fold_in(_rk, 12), (2,), 0, 7, jnp.int32)
        itok_B_0_8 = jax.random.randint(jax.random.fold_in(_rk, 13), (2,), 0, 9, jnp.int32)
        return (x, itok_B_0_7, itok_B_0_6, itok_B_0_8)
    x, itok_B_0_7, itok_B_0_6, itok_B_0_8 = _rec_inputs()

    def _L0_cond_setup():
        import jax, jax.numpy as jnp
        import numpy as np
        S, O, H = (8, 128, 128)
        B, N = (32, 64)
        key = jax.random.key(seed)
        k1, k2, k3, k4 = jax.random.split(key, 4)
        x = jax.random.normal(k1, (B, N, H), dtype=jnp.float32)
        subject_id = jax.random.randint(k2, (B,), 0, S)
        wbound = jnp.sqrt(2.0 / 6.0) * jnp.sqrt(3.0 / H)
        weight = jax.random.uniform(k3, (S, O, H), minval=-wbound, maxval=wbound, dtype=jnp.float32)
        bbound = 1.0 / jnp.sqrt(H)
        bias = jax.random.uniform(k4, (S, O), minval=-bbound, maxval=bbound, dtype=jnp.float32)
        return {'x': x, 'subject_id': subject_id, 'weight': weight, 'bias': bias}
    _L0_cond_all = _L0_cond_setup()
    _L0_cond_in = {k: v for k, v in _L0_cond_all.items() if k in ('weight', 'bias')}
    del _L0_cond_all

    def _L0_attn_setup():
        import jax, jax.numpy as jnp
        import numpy as np
        import math
        NUM_HEADS = 16

        def rotate_half(x):
            x1 = x[..., ::2]
            x2 = x[..., 1::2]
            return jnp.concatenate((-x2, x1), axis=-1)

        def rotary_tables(seq_len, head_dim, dtype):
            inv_freq = 1.0 / 10000.0 ** (jnp.arange(0, head_dim, 2, dtype=jnp.float32) / head_dim)
            t = jnp.arange(seq_len, dtype=jnp.float32)
            freqs = t[:, None] * inv_freq[None, :]
            emb = jnp.concatenate((freqs, freqs), axis=-1)
            cos = jnp.cos(emb)[None, None, :, :].astype(dtype)
            sin = jnp.sin(emb)[None, None, :, :].astype(dtype)
            return (cos, sin)
        key = jax.random.key(seed)
        k1, k2, k3, k4 = jax.random.split(key, 4)
        B, T, D = (2, 256, 128)
        scale = 1.0 / math.sqrt(D)
        x = jax.random.normal(k1, (B, T, D), dtype=jnp.float32)
        w_qkv = jax.random.normal(k2, (3 * D, D), dtype=jnp.float32) * scale
        w_out = jax.random.normal(k3, (D, D), dtype=jnp.float32) * scale
        b_out = jax.random.normal(k4, (D,), dtype=jnp.float32) * scale
        return {'x': x, 'w_qkv': w_qkv, 'w_out': w_out, 'b_out': b_out}
    _L0_attn_all = _L0_attn_setup()
    _L0_attn_in = {k: v for k, v in _L0_attn_all.items() if k in ('w_qkv', 'w_out', 'b_out')}
    del _L0_attn_all

    def _L0_cond2_setup():
        import jax, jax.numpy as jnp
        import numpy as np
        N_PROFILES = 8
        HIDDEN = 128
        BOTTLENECK = 128
        EPS = 1e-05
        key = jax.random.key(seed)
        ks = jax.random.split(key, 8)
        B, S, H, K, P = (16, 256, HIDDEN, BOTTLENECK, N_PROFILES)
        down_w = jax.random.normal(ks[0], (P, H, K), dtype=jnp.float32) * (1.0 / np.sqrt(H))
        down_b = jax.random.normal(ks[1], (P, K), dtype=jnp.float32) * 0.01
        up_w = jax.random.normal(ks[2], (P, K, H), dtype=jnp.float32) * (1.0 / np.sqrt(K))
        up_b = jax.random.normal(ks[3], (P, H), dtype=jnp.float32) * 0.01
        ln_g = jnp.ones((P, H), dtype=jnp.float32)
        ln_b = jnp.zeros((P, H), dtype=jnp.float32)
        hidden = jax.random.normal(ks[4], (B, S, H), dtype=jnp.float32)
        profile_ids = jax.random.randint(ks[5], (B,), 0, P)
        return {'hidden': hidden, 'profile_ids': profile_ids, 'down_w': down_w, 'down_b': down_b, 'up_w': up_w, 'up_b': up_b, 'ln_g': ln_g, 'ln_b': ln_b}
    _L0_cond2_all = _L0_cond2_setup()
    _L0_cond2_in = {k: v for k, v in _L0_cond2_all.items() if k in ('down_w', 'down_b', 'up_w', 'up_b', 'ln_g', 'ln_b')}
    del _L0_cond2_all

    def _L0_ffn_setup():
        import jax, jax.numpy as jnp
        import numpy as np
        TOP_K = 4
        key = jax.random.key(seed)
        ks = jax.random.split(key, 5)
        B, T, D = (2, 128, 128)
        P, PD = (32, 32)
        return {'x': jax.random.normal(ks[0], (B, T, D), dtype=jnp.float32), 'hasher_w': jax.random.normal(ks[1], (PD, D), dtype=jnp.float32) * 0.03, 'keys': jax.random.normal(ks[2], (P, PD), dtype=jnp.float32) * 0.1, 'values_down': jax.random.normal(ks[3], (P, D, PD), dtype=jnp.float32) * 0.01, 'values_up': jax.random.normal(ks[4], (P, PD, D), dtype=jnp.float32) * 0.01, 'scale': jnp.full((1,), 0.1, dtype=jnp.float32)}
    _L0_ffn_all = _L0_ffn_setup()
    _L0_ffn_in = {k: v for k, v in _L0_ffn_all.items() if k in ('hasher_w', 'keys', 'values_down', 'values_up', 'scale')}
    del _L0_ffn_all

    def _L1_cond_setup():
        import jax, jax.numpy as jnp
        import numpy as np
        IN, HID, OUT, PART, E = (128, 512, 128, 32, 8)
        B, N = (16, 256)
        key = jax.random.key(seed)
        ks = jax.random.split(key, 8)
        s1 = 1.0 / np.sqrt(IN)
        s2 = 1.0 / np.sqrt(HID)
        return {'x': jax.random.normal(ks[0], (B, N, IN), dtype=jnp.float32), 'indices': jax.random.randint(ks[1], (B,), 0, E, dtype=jnp.int64), 'W1': jax.random.uniform(ks[2], (IN, HID), jnp.float32, -s1, s1), 'b1': jax.random.uniform(ks[3], (HID,), jnp.float32, -s1, s1), 'W2': jax.random.uniform(ks[4], (HID, OUT - PART), jnp.float32, -s2, s2), 'b2': jax.random.uniform(ks[5], (OUT - PART,), jnp.float32, -s2, s2), 'We': jax.random.uniform(ks[6], (E, HID, PART), jnp.float32, -s2, s2), 'be': jax.random.uniform(ks[7], (E, PART), jnp.float32, -s2, s2)}
    _L1_cond_all = _L1_cond_setup()
    _L1_cond_in = {k: v for k, v in _L1_cond_all.items() if k in ('W1', 'b1', 'W2', 'b2', 'We', 'be')}
    del _L1_cond_all

    def _L1_attn_setup():
        import math
        import jax, jax.numpy as jnp
        import numpy as np
        B, L, D_MODEL, N_HEADS = (4, 512, 128, 16)
        HEAD_DIM = D_MODEL // N_HEADS
        NUM_LANDMARKS = 128

        def _split_heads(t):
            b, l, _ = t.shape
            return t.reshape(b, l, N_HEADS, HEAD_DIM).transpose(0, 2, 1, 3)

        def _iterative_inv(mat, n_iter=6):
            I = jnp.eye(mat.shape[-1], dtype=mat.dtype)
            K = mat
            V = K.swapaxes(-1, -2) / jnp.max(jnp.sum(K, axis=-2))
            for _ in range(n_iter):
                KV = jnp.matmul(K, V)
                V = jnp.matmul(0.25 * V, 13.0 * I - jnp.matmul(KV, 15.0 * I - jnp.matmul(KV, 7.0 * I - KV)))
            return V
        key = jax.random.key(seed)
        ks = jax.random.split(key, 7)
        s = 1.0 / math.sqrt(D_MODEL)
        return {'x': jax.random.normal(ks[0], (B, L, D_MODEL), dtype=jnp.float32), 'Wq': jax.random.uniform(ks[1], (D_MODEL, D_MODEL), jnp.float32, -s, s), 'bq': jax.random.uniform(ks[2], (D_MODEL,), jnp.float32, -s, s), 'Wk': jax.random.uniform(ks[3], (D_MODEL, D_MODEL), jnp.float32, -s, s), 'bk': jax.random.uniform(ks[4], (D_MODEL,), jnp.float32, -s, s), 'Wv': jax.random.uniform(ks[5], (D_MODEL, D_MODEL), jnp.float32, -s, s), 'bv': jax.random.uniform(ks[6], (D_MODEL,), jnp.float32, -s, s)}
    _L1_attn_all = _L1_attn_setup()
    _L1_attn_in = {k: v for k, v in _L1_attn_all.items() if k in ('Wq', 'bq', 'Wk', 'bk', 'Wv', 'bv')}
    del _L1_attn_all

    def _L1_cond2_setup():
        import jax, jax.numpy as jnp
        import numpy as np
        LN_EPS = 1e-05
        key = jax.random.key(seed)
        ks = jax.random.split(key, 8)
        B, S, H, A, L = (32, 256, 128, 32, 10)
        return {'hidden_states': jax.random.normal(ks[0], (B, S, H), dtype=jnp.float32), 'language_ids': jax.random.randint(ks[1], (B,), 0, L, dtype=jnp.int64), 'W1': jax.random.normal(ks[2], (L, H, A), dtype=jnp.float32) * (1.0 / np.sqrt(H)), 'b1': jnp.zeros((L, A), dtype=jnp.float32), 'W2': jax.random.normal(ks[3], (L, A, H), dtype=jnp.float32) * (1.0 / np.sqrt(A)), 'b2': jnp.zeros((L, H), dtype=jnp.float32), 'gamma': jnp.ones((L, H), dtype=jnp.float32), 'beta': jnp.zeros((L, H), dtype=jnp.float32)}
    _L1_cond2_all = _L1_cond2_setup()
    _L1_cond2_in = {k: v for k, v in _L1_cond2_all.items() if k in ('W1', 'b1', 'W2', 'b2', 'gamma', 'beta')}
    del _L1_cond2_all

    def _L1_ffn_setup():
        import jax, jax.numpy as jnp
        import numpy as np
        E = 8
        TOP_K = 2
        H = 128
        I = 64
        SI = 64
        B, S = (4, 512)
        key = jax.random.key(seed)
        ks = jax.random.split(key, 8)
        sc_h = 1.0 / np.sqrt(H)
        sc_i = 1.0 / np.sqrt(I)
        return {'hidden_states': jax.random.normal(ks[0], (B, S, H), jnp.float32), 'gate_w': jax.random.normal(ks[1], (E, H), jnp.float32) * sc_h, 'Wg': jax.random.normal(ks[2], (E, H, I), jnp.float32) * sc_h, 'Wu': jax.random.normal(ks[3], (E, H, I), jnp.float32) * sc_h, 'Wd': jax.random.normal(ks[4], (E, I, H), jnp.float32) * sc_i, 'sWg': jax.random.normal(ks[5], (H, SI), jnp.float32) * sc_h, 'sWu': jax.random.normal(ks[6], (H, SI), jnp.float32) * sc_h, 'sWd': jax.random.normal(ks[7], (SI, H), jnp.float32) * sc_i}
    _L1_ffn_all = _L1_ffn_setup()
    _L1_ffn_in = {k: v for k, v in _L1_ffn_all.items() if k in ('gate_w', 'Wg', 'Wu', 'Wd', 'sWg', 'sWu', 'sWd')}
    del _L1_ffn_all
    return {'x': x, 'itok_B_0_7': itok_B_0_7, 'itok_B_0_6': itok_B_0_6, 'itok_B_0_8': itok_B_0_8, 'L0_cond_weight': _L0_cond_in['weight'], 'L0_cond_bias': _L0_cond_in['bias'], 'L0_attn_w_qkv': _L0_attn_in['w_qkv'], 'L0_attn_w_out': _L0_attn_in['w_out'], 'L0_attn_b_out': _L0_attn_in['b_out'], 'L0_cond2_down_w': _L0_cond2_in['down_w'], 'L0_cond2_down_b': _L0_cond2_in['down_b'], 'L0_cond2_up_w': _L0_cond2_in['up_w'], 'L0_cond2_up_b': _L0_cond2_in['up_b'], 'L0_cond2_ln_g': _L0_cond2_in['ln_g'], 'L0_cond2_ln_b': _L0_cond2_in['ln_b'], 'L0_ffn_hasher_w': _L0_ffn_in['hasher_w'], 'L0_ffn_keys': _L0_ffn_in['keys'], 'L0_ffn_values_down': _L0_ffn_in['values_down'], 'L0_ffn_values_up': _L0_ffn_in['values_up'], 'L0_ffn_scale': _L0_ffn_in['scale'], 'L1_cond_W1': _L1_cond_in['W1'], 'L1_cond_b1': _L1_cond_in['b1'], 'L1_cond_W2': _L1_cond_in['W2'], 'L1_cond_b2': _L1_cond_in['b2'], 'L1_cond_We': _L1_cond_in['We'], 'L1_cond_be': _L1_cond_in['be'], 'L1_attn_Wq': _L1_attn_in['Wq'], 'L1_attn_bq': _L1_attn_in['bq'], 'L1_attn_Wk': _L1_attn_in['Wk'], 'L1_attn_bk': _L1_attn_in['bk'], 'L1_attn_Wv': _L1_attn_in['Wv'], 'L1_attn_bv': _L1_attn_in['bv'], 'L1_cond2_W1': _L1_cond2_in['W1'], 'L1_cond2_b1': _L1_cond2_in['b1'], 'L1_cond2_W2': _L1_cond2_in['W2'], 'L1_cond2_b2': _L1_cond2_in['b2'], 'L1_cond2_gamma': _L1_cond2_in['gamma'], 'L1_cond2_beta': _L1_cond2_in['beta'], 'L1_ffn_gate_w': _L1_ffn_in['gate_w'], 'L1_ffn_Wg': _L1_ffn_in['Wg'], 'L1_ffn_Wu': _L1_ffn_in['Wu'], 'L1_ffn_Wd': _L1_ffn_in['Wd'], 'L1_ffn_sWg': _L1_ffn_in['sWg'], 'L1_ffn_sWu': _L1_ffn_in['sWu'], 'L1_ffn_sWd': _L1_ffn_in['sWd']}

def reference(x, itok_B_0_7, itok_B_0_6, itok_B_0_8, L0_cond_weight, L0_cond_bias, L0_attn_w_qkv, L0_attn_w_out, L0_attn_b_out, L0_cond2_down_w, L0_cond2_down_b, L0_cond2_up_w, L0_cond2_up_b, L0_cond2_ln_g, L0_cond2_ln_b, L0_ffn_hasher_w, L0_ffn_keys, L0_ffn_values_down, L0_ffn_values_up, L0_ffn_scale, L1_cond_W1, L1_cond_b1, L1_cond_W2, L1_cond_b2, L1_cond_We, L1_cond_be, L1_attn_Wq, L1_attn_bq, L1_attn_Wk, L1_attn_bk, L1_attn_Wv, L1_attn_bv, L1_cond2_W1, L1_cond2_b1, L1_cond2_W2, L1_cond2_b2, L1_cond2_gamma, L1_cond2_beta, L1_ffn_gate_w, L1_ffn_Wg, L1_ffn_Wu, L1_ffn_Wd, L1_ffn_sWg, L1_ffn_sWu, L1_ffn_sWd):
    import jax
    import jax.numpy as jnp

    def _L0_cond_ref(x, subject_id, weight, bias):
        import jax, jax.numpy as jnp
        import numpy as np
        S, O, H = (8, 128, 128)
        B, N = (32, 64)
        W = weight[subject_id]
        b = bias[subject_id]
        y = jnp.einsum('bnh,boh->bno', x, W) + b[:, None, :]
        return y

    def _L0_attn_ref(x, w_qkv, w_out, b_out):
        import jax, jax.numpy as jnp
        import numpy as np
        import math
        NUM_HEADS = 16

        def rotate_half(x):
            x1 = x[..., ::2]
            x2 = x[..., 1::2]
            return jnp.concatenate((-x2, x1), axis=-1)

        def rotary_tables(seq_len, head_dim, dtype):
            inv_freq = 1.0 / 10000.0 ** (jnp.arange(0, head_dim, 2, dtype=jnp.float32) / head_dim)
            t = jnp.arange(seq_len, dtype=jnp.float32)
            freqs = t[:, None] * inv_freq[None, :]
            emb = jnp.concatenate((freqs, freqs), axis=-1)
            cos = jnp.cos(emb)[None, None, :, :].astype(dtype)
            sin = jnp.sin(emb)[None, None, :, :].astype(dtype)
            return (cos, sin)
        B, T, D = x.shape
        H = NUM_HEADS
        hd = D // H
        qkv = x @ w_qkv.T
        q, k, v = jnp.split(qkv, 3, axis=-1)

        def to_heads(a):
            return a.reshape(B, T, H, hd).transpose(0, 2, 1, 3)
        q, k, v = (to_heads(q), to_heads(k), to_heads(v))
        cos, sin = rotary_tables(T, hd, x.dtype)
        q = q * cos + rotate_half(q) * sin
        k = k * cos + rotate_half(k) * sin
        attn = jnp.einsum('bhqd,bhkd->bhqk', q, k) / math.sqrt(hd)
        attn = jax.nn.softmax(attn, axis=-1)
        out = jnp.einsum('bhqk,bhkd->bhqd', attn, v)
        out = out.transpose(0, 2, 1, 3).reshape(B, T, D)
        return out @ w_out.T + b_out

    def _L0_cond2_ref(hidden, profile_ids, down_w, down_b, up_w, up_b, ln_g, ln_b):
        import jax, jax.numpy as jnp
        import numpy as np
        N_PROFILES = 8
        HIDDEN = 128
        BOTTLENECK = 128
        EPS = 1e-05
        Wd = down_w[profile_ids]
        bd = down_b[profile_ids][:, None]
        Wu = up_w[profile_ids]
        bu = up_b[profile_ids][:, None]
        g = ln_g[profile_ids][:, None]
        b = ln_b[profile_ids][:, None]
        z = jax.nn.relu(jnp.einsum('bsh,bhk->bsk', hidden, Wd) + bd)
        y = hidden + jnp.einsum('bsk,bkh->bsh', z, Wu) + bu
        mu = jnp.mean(y, axis=-1, keepdims=True)
        var = jnp.mean(jnp.square(y - mu), axis=-1, keepdims=True)
        return (y - mu) * jax.lax.rsqrt(var + EPS) * g + b

    def _L0_ffn_ref(x, hasher_w, keys, values_down, values_up, scale):
        import jax, jax.numpy as jnp
        import numpy as np
        TOP_K = 4
        h = jnp.einsum('btd,pd->btp', x, hasher_w)
        sim = jnp.einsum('btp,np->btn', h, keys)
        vals, idx = jax.lax.top_k(sim, TOP_K)
        w = jax.nn.softmax(vals, axis=-1)
        out = jnp.zeros_like(x)
        for k in range(TOP_K):
            ik = idx[..., k]
            vd = values_down[ik]
            vu = values_up[ik]
            proj = jax.nn.silu(jnp.einsum('btd,btdp->btp', x, vd))
            o = jnp.einsum('btp,btpd->btd', proj, vu)
            out = out + o * w[..., k:k + 1]
        return x + out * scale

    def _L1_cond_ref(x, indices, W1, b1, W2, b2, We, be):
        import jax, jax.numpy as jnp
        import numpy as np
        IN, HID, OUT, PART, E = (128, 512, 128, 32, 8)
        B, N = (16, 256)
        h = jax.nn.gelu(jnp.einsum('bni,ih->bnh', x, W1) + b1, approximate=False)
        shared_x = jnp.einsum('bnh,ho->bno', h, W2) + b2
        We_sel = We[indices]
        be_sel = be[indices]
        expert_x = jnp.einsum('bnh,bhp->bnp', h, We_sel) + be_sel[:, None, :]
        return jnp.concatenate([shared_x, expert_x], axis=-1)

    def _L1_attn_ref(x, Wq, bq, Wk, bk, Wv, bv):
        import math
        import jax, jax.numpy as jnp
        import numpy as np
        B, L, D_MODEL, N_HEADS = (4, 512, 128, 16)
        HEAD_DIM = D_MODEL // N_HEADS
        NUM_LANDMARKS = 128

        def _split_heads(t):
            b, l, _ = t.shape
            return t.reshape(b, l, N_HEADS, HEAD_DIM).transpose(0, 2, 1, 3)

        def _iterative_inv(mat, n_iter=6):
            I = jnp.eye(mat.shape[-1], dtype=mat.dtype)
            K = mat
            V = K.swapaxes(-1, -2) / jnp.max(jnp.sum(K, axis=-2))
            for _ in range(n_iter):
                KV = jnp.matmul(K, V)
                V = jnp.matmul(0.25 * V, 13.0 * I - jnp.matmul(KV, 15.0 * I - jnp.matmul(KV, 7.0 * I - KV)))
            return V
        Q = _split_heads(x @ Wq.T + bq)
        K = _split_heads(x @ Wk.T + bk)
        V = _split_heads(x @ Wv.T + bv)
        b, h, l, d = Q.shape
        scale = 1.0 / math.sqrt(math.sqrt(HEAD_DIM))
        Q = Q * scale
        K = K * scale
        seg = l // NUM_LANDMARKS
        Q_lm = Q.reshape(b, h, NUM_LANDMARKS, seg, d).mean(axis=-2)
        K_lm = K.reshape(b, h, NUM_LANDMARKS, seg, d).mean(axis=-2)
        kernel_1 = jax.nn.softmax(jnp.einsum('bhld,bhmd->bhlm', Q, K_lm), axis=-1)
        kernel_2 = jax.nn.softmax(jnp.einsum('bhmd,bhnd->bhmn', Q_lm, K_lm), axis=-1)
        kernel_3 = jax.nn.softmax(jnp.einsum('bhmd,bhld->bhml', Q_lm, K), axis=-1)
        X = jnp.matmul(jnp.matmul(kernel_1, _iterative_inv(kernel_2)), jnp.matmul(kernel_3, V))
        out = X.transpose(0, 2, 1, 3).reshape(b, l, h * d)
        return out

    def _L1_cond2_ref(hidden_states, language_ids, W1, b1, W2, b2, gamma, beta):
        import jax, jax.numpy as jnp
        import numpy as np
        LN_EPS = 1e-05
        w1 = W1[language_ids]
        w2 = W2[language_ids]
        h = jnp.einsum('bsh,bha->bsa', hidden_states, w1) + b1[language_ids][:, None, :]
        h = jax.nn.relu(h)
        adapted = jnp.einsum('bsa,bah->bsh', h, w2) + b2[language_ids][:, None, :]
        x = hidden_states + adapted
        mean = jnp.mean(x, axis=-1, keepdims=True)
        var = jnp.mean(jnp.square(x - mean), axis=-1, keepdims=True)
        normed = (x - mean) * jax.lax.rsqrt(var + LN_EPS)
        return normed * gamma[language_ids][:, None, :] + beta[language_ids][:, None, :]

    def _L1_ffn_ref(hidden_states, gate_w, Wg, Wu, Wd, sWg, sWu, sWd):
        import jax, jax.numpy as jnp
        import numpy as np
        E = 8
        TOP_K = 2
        H = 128
        I = 64
        SI = 64
        B, S = (4, 512)
        b, s, h = hidden_states.shape
        x = hidden_states.reshape(-1, h)
        logits = x.astype(jnp.float32) @ gate_w.T
        scores = jax.nn.softmax(logits, axis=-1)
        topk_w, topk_idx = jax.lax.top_k(scores, TOP_K)
        topk_w = topk_w / (topk_w.sum(-1, keepdims=True) + 1e-20)
        cw = (jax.nn.one_hot(topk_idx, E, dtype=topk_w.dtype) * topk_w[..., None]).sum(1)
        g = jnp.einsum('th,ehi->tei', x, Wg)
        u = jnp.einsum('th,ehi->tei', x, Wu)
        inter = jax.nn.gelu(g, approximate=False) * u
        y = jnp.einsum('tei,te,eih->th', inter, cw.astype(x.dtype), Wd)
        sh = jax.nn.gelu(x @ sWg, approximate=False) * (x @ sWu) @ sWd
        return (y + sh).reshape(b, s, h)
    x = x + _L0_attn_ref(_L0_cond_ref(x, itok_B_0_7, L0_cond_weight, L0_cond_bias), L0_attn_w_qkv, L0_attn_w_out, L0_attn_b_out)
    x = x + _L0_ffn_ref(_L0_cond2_ref(x, itok_B_0_6, L0_cond2_down_w, L0_cond2_down_b, L0_cond2_up_w, L0_cond2_up_b, L0_cond2_ln_g, L0_cond2_ln_b), L0_ffn_hasher_w, L0_ffn_keys, L0_ffn_values_down, L0_ffn_values_up, L0_ffn_scale)
    x = x + _L1_attn_ref(_L1_cond_ref(x, itok_B_0_7, L1_cond_W1, L1_cond_b1, L1_cond_W2, L1_cond_b2, L1_cond_We, L1_cond_be), L1_attn_Wq, L1_attn_bq, L1_attn_Wk, L1_attn_bk, L1_attn_Wv, L1_attn_bv)
    x = x + _L1_ffn_ref(_L1_cond2_ref(x, itok_B_0_8, L1_cond2_W1, L1_cond2_b1, L1_cond2_W2, L1_cond2_b2, L1_cond2_gamma, L1_cond2_beta), L1_ffn_gate_w, L1_ffn_Wg, L1_ffn_Wu, L1_ffn_Wd, L1_ffn_sWg, L1_ffn_sWu, L1_ffn_sWd)
    return x

_drawn_inputs = setup_inputs


def setup_inputs(seed=0):
    import zlib

    import numpy as np

    out = dict(_drawn_inputs(seed))
    spreads = {'L0_cond2_ln_g': (1.0, 0.2),
     'L0_cond2_ln_b': (0.0, 0.1),
     'L1_cond2_b1': (0.0, 0.1),
     'L1_cond2_b2': (0.0, 0.1),
     'L1_cond2_gamma': (1.0, 0.2),
     'L1_cond2_beta': (0.0, 0.1)}
    factors = {'L0_cond2_down_b': 6.13,
     'L0_cond2_up_b': 4.979,
     'L0_ffn_hasher_w': 8.0,
     'L0_ffn_keys': 22.552,
     'L0_ffn_values_down': 8.0,
     'L0_ffn_values_up': 22.168,
     'L1_cond_b1': 6.562,
     'L1_cond_b2': 3.215,
     'L1_cond_be': 5.572,
     'L1_attn_Wq': 8.0,
     'L1_attn_bq': 8.0,
     'L1_attn_Wk': 8.0,
     'L1_attn_bk': 64.0}
    for name, (base, spread) in spreads.items():
        noise = np.random.default_rng([zlib.crc32(name.encode()), seed]).standard_normal(out[name].shape)
        drawn = base * np.exp(spread * noise) if base else spread * noise
        out[name] = jnp.asarray(drawn.astype(out[name].dtype))
    for name, factor in factors.items():
        out[name] = (out[name] * factor).astype(out[name].dtype)
    return out
```

```python
from contextlib import ExitStack

import numpy as np

import concourse.bass as bass
from concourse import mybir

F32 = mybir.dt.float32
BF16 = mybir.dt.bfloat16
I32 = mybir.dt.int32
U16 = mybir.dt.uint16
ALU = mybir.AluOpType
ACT = mybir.ActivationFunctionType
AX = mybir.AxisListType

P = 128
B, T = 2, 512
NT = T // P
H, HD = 16, 8
GH = 4
NG = H // GH
G = B * NG
PARTS = 3
PROD = PARTS * PARTS * HD
KROWS = PROD + PARTS
LM = 128
SEG = T // LM
LW = T + LM
ITERS = 6
VW = 2 * HD
WA = P + HD
E0, PD, TOP0 = 32, 32, 4
C0 = E0 * PD // P
HC = 4
AD = 32
E1, I1, TOP1 = 8, 64, 2
C1 = E1 // 2
EPS = 1e-5
LOW = -3.0e38
HIGH = 3.0e38

SEMAPHORES = """ld_ids ld_in ld_qkv ld_res ld_c0 ld_f0 ld_c1 ld_l1 ld_ad ld_f1
mv_ready rstd_ready const_ready step_dve stored
y0_ps y0_ready qk_ps v_ps rot_cos rot_done part_a res_a part_b part_c parts_out stacks_in_0 stacks_in_1 ones_rows vaug_ready
smax_ps smax_done negT_ps neg_split neg_rows_0 neg_rows_1 st_ps exp_done av_ps outT_ready otr_ps o_ready
oT_ps oT_ready proj_ps x1_ready xbias_ready
t0_ps t0_ready t1_ps t1_ready z0_ps z0_ready z1_ps z1_ready u0_ps u1_ps n0_ready n1_ready base0_ready base1_ready
xn0_ps xn0_ready xn1_ps xn1_ready
hash_ps hash_ready sim_ps cwp_ready cwT_ps cwT_ready up_proj_ps silu_ready sel_ps hid_ready down_ps x3_ready x12_ready
x3T_ps x3T_ready h1_ps h1_ready y1_ps y1_ready
l1q_ps l1k_ps l1v_ps l1q_ready l1k_ready lm_ready v1_ready l1_parts l1_parts_out l1_stacks
k2_ps k2_max k2_exp a_ready col_ps col_done m_ps m_done n_ps n_split n_rows_0 n_rows_1 k3_ps k3_exp yv_ps yv_sb ytr_ps y_ready
rc_ready rcb_ps rcb_ready
sq_ps w_ready mm1_ps w2_ready f_ready d_ready mm2_ps wn_ready k1_ps k1_exp gaug_ready x_ps xo_sb xtr_ps xo_ready x4_ready gaug_ones
gate_ps sc_sub sc_exp cw1_ready cw1T_ps cw1T_ready g_ps gelu_ready uu_ps gu_ready cs_ps hid1_ready fin_ps out_ready"""


def build(nc, a, out):
    ctx = ExitStack()
    with ctx:
        def sb(name, shape, dt=F32):
            return ctx.enter_context(nc.sbuf_tensor(name, shape, dt))

        S = {}
        for n in SEMAPHORES.split():
            S[n] = ctx.enter_context(nc.semaphore(n))

        S["stacks_in"] = (S["stacks_in_0"], S["stacks_in_1"])
        S["neg_rows"] = (S["neg_rows_0"], S["neg_rows_1"])
        S["n_rows"] = (S["n_rows_0"], S["n_rows_1"])

        ids = sb("ids", [1, 8], I32)
        ident = sb("ident", [P, P])
        identb = sb("identb", [P, P], BF16)
        ones = sb("ones", [P, P])
        x = sb("x", [P, B, NT, P])
        xT = sb("xT", [P, B, T])
        w0T = sb("w0T", [P, B, P])
        b0 = sb("b0", [P, B])
        y0T = sb("y0T", [P, B, T])
        wqk = sb("wqk", [P, 4, P])
        wv = sb("wv", [P, P])
        QS = sb("QS", [P, B, H * LW], BF16)
        KS = sb("KS", [P, B, H * LW], BF16)
        V = sb("V", [P, B, NT, H, VW])
        woutT = sb("woutT", [P, P])
        boutb = sb("boutb", [P, P])
        negm = sb("negm", [P, 2, 20])
        negT = sb("negT", [32, 2, PARTS, P], BF16)
        negR = sb("negR", [32, P])
        outT = sb("outT", [P, T])
        rden = sb("rden", [P, NT, GH])
        O = sb("O", [P, B, NT, P])
        featT = sb("featT", [P, B, T])
        stats = sb("stats", [P, B, NT, 6])
        mv = sb("mv", [P, B, NT, 2])
        rstd = sb("rstd", [P, B, NT])
        veps = sb("veps", [P, B, NT])
        rinv = sb("rinv", [P, B, NT])
        root = sb("root", [P, B, NT])
        wdn = sb("wdn", [P, B, P])
        bdn = sb("bdn", [P, B])
        wup = sb("wup", [P, B, P])
        rows0 = sb("rows0", [P, B, 3, P])
        rows1 = sb("rows1", [P, B, 3, P])
        hashT = sb("hashT", [P, PD])
        keysT = sb("keysT", [PD, E0])
        scale = sb("scale", [P, 1])
        sel0 = sb("sel0", [PARTS * E0, C0, P], BF16)
        sel1 = sb("sel1", [PARTS * E1, C1, P], BF16)
        sim = sb("sim", [P, B, NT, E0 + 8])
        took = sb("took", [P, B, NT, E0 + 8])
        best = sb("best", [P, B, NT, 8])
        pick = sb("pick", [P, B, NT, 8])
        ex = sb("ex", [P, B, NT, E0])
        ex2 = sb("ex2", [P, B, NT, E0])
        tot = sb("tot", [P, B, NT])
        totr = sb("totr", [P, B, NT])
        cw = sb("cw", [P, B, NT, E0])
        cwr = sb("cwr", [P, B, NT, E0])
        cwp = sb("cwp", [P, B, NT, PARTS, E0], BF16)
        cwT = sb("cwT", [PARTS * E0, B, T], BF16)
        sim1 = sim[:, :, :, 0:16]
        took1 = took[:, :, :, 0:16]
        cwp1 = sb("cwp1", [P, B, NT, PARTS, E1], BF16)
        b1 = sb("b1", [P, HC])
        b2 = sb("b2", [P, B])
        wl1 = sb("wl1", [P, 3, P])
        bl1 = sb("bl1", [P, 2])
        bvb = sb("bvb", [P, P])
        sums = sb("sums", [P, GH])
        rsum = sb("rsum", [P, GH])
        cmax = sb("cmax", [1, G])
        rc = sb("rc", [1, 2])
        rcb = sb("rcb", [P, 1])
        Gaug = sb("Gaug", [P, 2, GH, VW])
        gateT = sb("gateT", [P, E1])
        a1 = sb("a1", [P, B, AD])
        ab1 = sb("ab1", [AD, B])
        a2 = sb("a2", [AD, B, P])

        PT = sb("PT", [P, 8, T])
        early = sb("early", [P, 6400])
        late = sb("late", [P, 5440])

        def view(buf, at, *shape):
            n = int(np.prod(shape))
            ap = buf[:, at:at + n]
            names = " ".join("abcd"[:len(shape)])
            return ap.rearrange(f"p ({names}) -> p {names}", **dict(zip("abcd", shape))) if len(shape) > 1 else ap

        PW = PARTS * LW * 4 // 2
        parts = early[:, 0:PW].bitcast(BF16).rearrange("p (n i t) -> p n i t", n=4, i=PARTS)
        qk = view(early, PW, 2, LW)
        res = view(early, PW + 2 * LW, 2, LW)
        vd = view(early, 0, E0 * PD)
        vu = view(early, 1024, C0, P)
        act_sb = view(early, 2048, 2, T)
        gu_sb = view(early, 3072, 2, T)
        w1 = view(early, 4096, HC, P)
        w2 = view(early, 4608, B, HC, P)
        AY = view(early, 0, B * H, WA)
        wg = view(early, 4352, E1 * I1)
        wu = view(early, 4864, E1 * I1)
        wd = view(early, 5376, C1, P)
        swg = view(early, 5888, I1)
        swu = view(early, 5952, I1)
        swd = early[0:I1, 6016:6016 + P]
        x1 = view(late, 0, B, NT, P)
        base = view(late, 1024, B, NT, P)
        y = view(late, 2048, B, NT, P)
        x2 = view(late, 3072, B, NT, P)
        zT = view(late, 4096, B, T)
        hT = late[0:PD, 4096:5120].rearrange("p (b t) -> p b t", b=B)
        Wb = view(late, 0, 2 * 2, GH, WA)
        W2 = view(late, 2176, 2, GH, WA)
        Fb = view(late, 3264, 2, GH, WA)
        Db = view(late, 4352, 2, GH, WA)
        cos, sin, rot = PT[:, 0, :], PT[:, 1, :], PT[:, 2:4, :]
        ek2 = featT[:, 0, :].rearrange("p (h m) -> p h m", h=GH)
        ysb = featT[:, 1, 0:P]
        neg2 = sb("neg2", [P, GH])
        x3 = x
        xnT = y0T
        y1T = xT
        x4 = O
        hid = PT

        ps = ctx.enter_context(nc.psum_tensor("ps", [P, 8, T], F32))
        bank = lambda i: ps[:, i, :]

        parts_dram = [nc.dram_tensor(f"parts_layer{n}", [4, PARTS, HD, H, width], BF16, kind="Internal").ap()
                      for n, width in enumerate((T, LW))]

        QS0 = [QS[:, b, 0:H * T].rearrange("p (h t) -> p h t", h=H) for b in range(B)]
        KS0 = [KS[:, b, 0:H * T].rearrange("p (h t) -> p h t", h=H) for b in range(B)]
        QS1 = [QS[:, b, :].rearrange("p (h t) -> p h t", h=H) for b in range(B)]
        KS1 = [KS[:, b, :].rearrange("p (h t) -> p h t", h=H) for b in range(B)]
        MAPS = 0.5 ** 0.5 * 0.5
        QSCALE = float(1.0 / np.sqrt(np.sqrt(np.float64(HD))))

        block = ctx.enter_context(nc.Block())
        tile = lambda t: slice(t * P, (t + 1) * P)

        @block.sync
        def _(sp):
            def load(dst, src, sem):
                sp.dma_start(dst, src).then_inc(sem, 16)

            load(ids[0:1, 0:6], a["ids"], S["ld_ids"])
            load(xT[:], a["xT"].rearrange("b h t -> h b t"), S["ld_in"])
            sp.wait_ge(S["ld_ids"], 16)
            subj = [sp.value_load(ids[0:1, b:b + 1], min_val=0, max_val=7) for b in range(B)]
            prof = [sp.value_load(ids[0:1, 2 + b:3 + b], min_val=0, max_val=7) for b in range(B)]
            lang = [sp.value_load(ids[0:1, 4 + b:5 + b], min_val=0, max_val=9) for b in range(B)]
            one = lambda ap, i: ap[bass.ds(i, 1)]
            for b in range(B):
                load(w0T[:, b, :], one(a["w0T"], subj[b]).rearrange("s h o -> (s h) o"), S["ld_in"])
                load(b0[:, b:b + 1], one(a["b0"], subj[b]).rearrange("s h -> h s"), S["ld_in"])
            load(wqk[:], a["wqkT"].rearrange("n h o -> h n o"), S["ld_qkv"])
            load(wv[:], a["wvT"], S["ld_qkv"])
            load(cos[:], a["cos"], S["ld_qkv"])
            load(sin[:], a["sin"], S["ld_qkv"])
            load(ident[:], a["ident"], S["ld_qkv"])
            load(identb[:].bitcast(U16), a["identb"], S["ld_qkv"])
            for b in range(B):
                load(x[:, b], a["x"][b].rearrange("(n p) f -> p n f", p=P), S["ld_res"])
            load(boutb[:], a["bout"].to_broadcast([P, P]), S["ld_res"])
            load(woutT[:], a["woutT"], S["ld_res"])

            def stacks(n, sem_parts, sem_out, sem_in, width, first):
                b = n // 2
                sp.wait_ge(sem_parts, n + 1)
                if not first:
                    sp.wait_ge(S["st_ps"], 8 * NG * (b + 1))
                d = parts_dram[0 if first else 1][n]
                for i in range(PARTS):
                    sp.dma_start(d[i].rearrange("d h t -> (d h) t"),
                                 parts[:, n, i, 0:width]).then_inc(sem_out, 16)
                sp.wait_ge(sem_out, 16 * PARTS * (n + 1))
                for i in range(PARTS):
                    for j in range(PARTS):
                        r = (i * PARTS + j) * HD
                        dst = (QS if n % 2 == 0 else KS)[r:r + HD, b, 0:H * width]
                        src = d[i if n % 2 == 0 else j].rearrange("d h t -> d (h t)")
                        sp.dma_start(dst, src).then_inc(sem_in[b], 16)

            sp.wait_ge(S["ones_rows"], 1)
            for n in range(4):
                stacks(n, S["part_c"], S["parts_out"], S["stacks_in"], T, True)

            for b in range(B):
                load(wdn[:, b, :], one(a["down"], prof[b]).rearrange("s h o -> (s h) o"), S["ld_c0"])
                load(bdn[:, b:b + 1], one(a["bd"], prof[b]).rearrange("s h -> h s"), S["ld_c0"])
                load(wup[:, b, :], one(a["up"], prof[b]).rearrange("s h o -> (s h) o"), S["ld_c0"])
                for k, n in enumerate(("bu", "ln_g", "ln_b")):
                    load(rows0[:, b, k, :], one(a[n], prof[b]).to_broadcast([P, P]), S["ld_c0"])
            load(hashT[:], a["hashT"], S["ld_f0"])
            load(keysT[:], a["keysT"], S["ld_f0"])
            load(vd[:].rearrange("p (e q) -> p e q", e=E0), a["vd"].rearrange("e d q -> d e q"), S["ld_f0"])
            load(vu[:], a["vu"].rearrange("e q d -> (e q) d").rearrange("(c p) d -> p c d", p=P), S["ld_f0"])
            load(scale[:], a["scale"].to_broadcast([P, 1]), S["ld_f0"])
            load(sel0[:].bitcast(U16), a["sel0"], S["ld_f0"])
            load(sel1[:].bitcast(U16), a["sel1"], S["ld_f0"])

            def neg_rows(g):
                sp.wait_ge(S["neg_split"], g + 1)
                b, h0 = g // NG, g % NG * GH
                for i in range(PARTS):
                    dst = QS0[b][PROD + i:PROD + i + 1, h0:h0 + GH, :].rearrange("p h (n t) -> p (h n) t", t=P)
                    sp.dma_start(dst, negT[0:GH * NT, g % 2, i, :]).then_inc(S["neg_rows"][g % 2], 16)

            for g in range(2):
                neg_rows(g)
            load(w1[:], a["w1"].rearrange("h (c n) -> h c n", c=HC), S["ld_c1"])
            load(b1[:], a["b1"], S["ld_c1"])
            PO = P - 32
            for b in range(B):
                load(w2[:, b, :, 0:PO], a["w2"].rearrange("(c n) o -> n c o", c=HC), S["ld_c1"])
                load(w2[:, b, :, PO:P], one(a["we"], subj[b]).rearrange("s (c n) o -> (s n) c o", c=HC), S["ld_c1"])
                load(b2[0:PO, b:b + 1], a["b2"].rearrange("(o s) -> o s", s=1), S["ld_c1"])
                load(b2[PO:P, b:b + 1], one(a["be"], subj[b]).rearrange("s o -> o s"), S["ld_c1"])
            for g in range(2, G):
                neg_rows(g)
            load(wl1[:], a["wl1T"].rearrange("n h o -> h n o"), S["ld_l1"])
            load(bl1[:], a["bl1"], S["ld_l1"])
            load(bvb[:], a["bv"].to_broadcast([P, P]), S["ld_l1"])
            for b in range(B):
                load(a1[:, b, :], one(a["a1"], lang[b]).rearrange("s h o -> (s h) o"), S["ld_ad"])
                load(ab1[:, b:b + 1], one(a["ab1"], lang[b]).rearrange("s h -> h s"), S["ld_ad"])
                load(a2[:, b, :], one(a["a2"], lang[b]).rearrange("s h o -> (s h) o"), S["ld_ad"])
                for k, n in enumerate(("ab2", "gamma", "beta")):
                    load(rows1[:, b, k, :], one(a[n], lang[b]).to_broadcast([P, P]), S["ld_ad"])
            load(gateT[:], a["gateT"], S["ld_f1"])
            for n in range(4):
                stacks(n, S["l1_parts"], S["l1_parts_out"], (S["l1_stacks"], S["l1_stacks"]), LW, False)
            load(wg[:].rearrange("p (e i) -> p e i", e=E1), a["wg"].rearrange("e h i -> h e i"), S["ld_f1"])
            load(wu[:].rearrange("p (e i) -> p e i", e=E1), a["wu"].rearrange("e h i -> h e i"), S["ld_f1"])
            load(wd[:], a["wd"].rearrange("e i h -> (e i) h").rearrange("(c p) h -> p c h", p=P), S["ld_f1"])
            load(swg[:], a["swg"], S["ld_f1"])
            load(swu[:], a["swu"], S["ld_f1"])
            load(swd[:], a["swd"], S["ld_f1"])

            for g in range(G):
                sp.wait_ge(S["n_split"], g + 1)
                b, h0 = g // NG, g % NG * GH
                for i in range(PARTS):
                    dst = QS1[b][PROD + i:PROD + i + 1, h0:h0 + GH, :].rearrange("p h (n t) -> p (h n) t", t=P)
                    sp.dma_start(dst, negT[0:20, g % 2, i, :]).then_inc(S["n_rows"][g % 2], 16)

            for b in range(B):
                sp.wait_ge(S["out_ready"], b + 1)
                sp.dma_start(out[b].rearrange("(n p) f -> p n f", p=P), y[:, b]).then_inc(S["stored"], 16)
            sp.wait_ge(S["stored"], 16 * B)
            sp.wait_ge(S["parts_out"], 16 * PARTS * 4)
            sp.wait_ge(S["l1_parts_out"], 16 * PARTS * 4)

        @block.tensor
        def _(pe):
            mm = nc.tensor.matmul

            pe.wait_ge(S["ld_in"], 80)
            for b in range(B):
                mm(bank(5 + b), w0T[:, b, :], xT[:, b, :], start=True, stop=True).then_inc(S["y0_ps"], 1)
            pe.wait_ge(S["ld_qkv"], 96)
            for b in range(B):
                pe.wait_ge(S["y0_ready"], b + 1)
                for n in range(4):
                    if 5 * b + n == 8:
                        pe.wait_ge(S["rot_cos"], 2)
                    mm(bank((5 * b + n) % 8), wqk[:, n, :], y0T[:, b, :], start=True, stop=True).then_inc(S["qk_ps"], 1)
                if b == 1:
                    pe.wait_ge(S["rot_cos"], 2)
                for t in range(NT):
                    r = mm(ps[:, (5 * b + 4) % 8, tile(t)], y0T[:, b, tile(t)], wv[:], start=True, stop=True)
                r.then_inc(S["v_ps"], 1)

            def s_max(g, u):
                b, h, n = g // NG, g % NG * GH + u // NT, GH * NT * g + u
                if u == 0:
                    pe.wait_ge(S["stacks_in"][b], 9 * 16 * 2)
                if n == 0:
                    pe.wait_ge(S["rot_cos"], 8)
                    pe.wait_ge(S["vaug_ready"], B)
                if n >= 2:
                    pe.wait_ge(S["smax_done"], n - 1)
                mm(bank(n % 2), QS0[b][0:PROD, h, tile(u % NT)], KS0[b][0:PROD, h, :],
                   start=True, stop=True).then_inc(S["smax_ps"], 1)

            def neg_t(g):
                pe.wait_ge(S["smax_done"], GH * NT * (g + 1))
                if g >= 1:
                    pe.wait_ge(S["neg_split"], g)
                if g >= 3:
                    pe.wait_ge(S["o_ready"], g - 2)
                nc.tensor.transpose(ps[0:GH * NT, 7, 0:P], negm[:, g % 2, 0:GH * NT], ident[:]).then_inc(S["negT_ps"], 1)

            def scores(g, p):
                b, n = g // NG, 8 * g + p
                if p == 0:
                    pe.wait_ge(S["neg_rows"][g % 2], 16 * PARTS * (g // 2 + 1))
                if n >= 2:
                    pe.wait_ge(S["exp_done"], n - 1)
                for k in range(2):
                    h = g % NG * GH + p % 2 * 2 + k
                    r = mm(bank(2 + p % 2 * 2 + k), KS0[b][0:KROWS, h, tile(p // 2)], QS0[b][0:KROWS, h, :],
                           start=True, stop=True)
                r.then_inc(S["st_ps"], 1)

            def av(g, kb):
                b = g // NG
                pe.wait_ge(S["exp_done"], 8 * g + 2 * kb + 2)
                if kb == 0 and g >= 1:
                    pe.wait_ge(S["outT_ready"], g)
                for j in range(GH):
                    r = mm(ps[32 * j:32 * j + VW, 6, :], V[:, b, kb, g % NG * GH + j, :],
                           PT[:, kb % 2 * 4 + j, :], start=(kb == 0), stop=(kb == NT - 1))
                r.then_inc(S["av_ps"], 1)

            def out_t(g):
                pe.wait_ge(S["outT_ready"], g + 1)
                pe.wait_ge(S["neg_split"], min(g + 3, G))
                if g >= 1:
                    pe.wait_ge(S["o_ready"], g)
                for t in range(NT):
                    r = nc.tensor.transpose(ps[:, 7, tile(t)], outT[:, tile(t)], ident[:])
                r.then_inc(S["otr_ps"], 1)

            pe.wait_ge(S["ld_qkv"], 96)
            for g in range(2):
                for u in range(GH * NT):
                    s_max(g, u)
                if g == 0:
                    neg_t(0)
            for g in range(G):
                for p in range(8):
                    scores(g, p)
                    if g + 2 < G:
                        for u in (2 * p, 2 * p + 1):
                            s_max(g + 2, u)
                    if p == 1:
                        if g + 1 < G:
                            neg_t(g + 1)
                        if g >= 1:
                            out_t(g - 1)
                    if p % 2 == 0 and p >= 2:
                        av(g, p // 2 - 1)
                av(g, NT - 1)
            out_t(G - 1)

            def turn(bk, src, done):
                for t in range(NT):
                    r = nc.tensor.transpose(ps[:, bk, tile(t)], src[:, t, :], ident[:])
                r.then_inc(done, 1)

            def token_mm(bk, lhs, rhs, done):
                for t in range(NT):
                    r = mm(ps[:, bk, tile(t)], lhs[:, tile(t)], rhs, start=True, stop=True)
                r.then_inc(done, 1)

            pe.wait_ge(S["o_ready"], G)
            for b in range(B):
                turn(4 * b, O[:, b], S["oT_ps"])
            pe.wait_ge(S["ld_res"], 64)
            for b in range(B):
                pe.wait_ge(S["oT_ready"], b + 1)
                token_mm(4 * b + 1, featT[:, b, :], woutT[:], S["proj_ps"])

            def adapter(ready, t_ps, t_ready, z_ps, z_ready, u_ps, src, wz, wu_, rows, loads):
                for b in range(B):
                    pe.wait_ge(ready, b + 1)
                    turn(4 * b + 2, src[:, b], t_ps)
                pe.wait_ge(*loads)
                for b in range(B):
                    pe.wait_ge(t_ready, b + 1)
                    mm(ps[0:rows, 4 * b + 3, :], wz[:, b, :], featT[:, b, :], start=True, stop=True).then_inc(z_ps, 1)
                for b in range(B):
                    pe.wait_ge(z_ready, b + 1)
                    token_mm(4 * b, zT[0:rows, b, :], wu_[:, b, :], u_ps)

            pe.wait_ge(S["ld_c0"], 192)
            adapter(S["x1_ready"], S["t0_ps"], S["t0_ready"], S["z0_ps"], S["z0_ready"], S["u0_ps"], x1, wdn, wup, P, (S["ld_c0"], 192))

            for b in range(B):
                pe.wait_ge(S["n0_ready"], b + 1)
                turn(4 * b + 1, x2[:, b], S["xn0_ps"])
            pe.wait_ge(S["ld_f0"], 112)
            for b in range(B):
                pe.wait_ge(S["xn0_ready"], b + 1)
                mm(ps[0:PD, 4 * b + 2, :], hashT[:], xnT[:, b, :], start=True, stop=True).then_inc(S["hash_ps"], 1)
            for b in range(B):
                pe.wait_ge(S["hash_ready"], b + 1)
                for t in range(NT):
                    r = mm(ps[:, 4 * b + 3, t * E0:(t + 1) * E0], hT[:, b, tile(t)], keysT[:], start=True, stop=True)
                r.then_inc(S["sim_ps"], 1)
            pe.wait_ge(S["ld_f0"], 112)
            for b in range(B):
                for c in range(C0):
                    n = b * C0 + c
                    if n >= 2:
                        pe.wait_ge(S["silu_ready"], n - 1)
                    if n == 0:
                        pe.wait_ge(S["n0_ready"], B)
                        pe.wait_ge(S["xn0_ready"], B)
                        pe.wait_ge(S["hash_ready"], B)
                    mm(bank(n % 2), vd[:, tile(c)], xnT[:, b, :], start=True, stop=True).then_inc(S["up_proj_ps"], 1)
                    if c == 0:
                        pe.wait_ge(S["cwp_ready"], b + 1)
                        for t in range(NT):
                            r = nc.tensor.transpose(ps[0:PARTS * E0, 4, :].bitcast(BF16)[:, tile(t)],
                                                    cwp[:, b, t].rearrange("p i e -> p (i e)"), identb[:])
                        r.then_inc(S["cwT_ps"], 1)
                        pe.wait_ge(S["cwT_ready"], b + 1)
                    if n == 0:
                        pe.wait_ge(S["cwp_ready"], B)
                    if n >= 2:
                        pe.wait_ge(S["hid_ready"], n - 1)
                    mm(bank(2 + n % 2), sel0[:, c, :], cwT[:, b, :], start=True, stop=True).then_inc(S["sel_ps"], 1)
                if b >= 1:
                    pe.wait_ge(S["x3_ready"], b)
                pe.wait_ge(S["hid_ready"], C0 * (b + 1))
                for t in range(NT):
                    for c in range(C0):
                        r = mm(ps[:, 5, tile(t)], hid[:, c, tile(t)], vu[:, c, :], start=(c == 0), stop=(c == C0 - 1))
                r.then_inc(S["down_ps"], 1)

            for b in range(B):
                pe.wait_ge(S["x3_ready"], b + 1)
                turn(6 + b, x3[:, b], S["x3T_ps"])
            pe.wait_ge(S["ld_c1"], 160)
            for b in range(B):
                pe.wait_ge(S["x3T_ready"], b + 1)
                for c in range(HC):
                    n = b * HC + c
                    if n >= 4:
                        pe.wait_ge(S["h1_ready"], n - 3)
                    mm(bank(n % 4), w1[:, c, :], featT[:, b, :], start=True, stop=True).then_inc(S["h1_ps"], 1)
            for b in range(B):
                pe.wait_ge(S["h1_ready"], HC * (b + 1))
                for c in range(HC):
                    r = mm(bank(4 + b), w2[:, b, c, :], hid[:, HC * b + c, :], start=(c == 0), stop=(c == HC - 1))
                r.then_inc(S["y1_ps"], 1)
            pe.wait_ge(S["ld_l1"], 48)
            for b in range(B):
                pe.wait_ge(S["y1_ready"], b + 1)
                mm(bank(b), wl1[:, 0, :], y1T[:, b, :], start=True, stop=True).then_inc(S["l1q_ps"], 1)
                mm(bank(2 + b), wl1[:, 1, :], y1T[:, b, :], start=True, stop=True).then_inc(S["l1k_ps"], 1)
                token_mm(6 + b, y1T[:, b, :], wl1[:, 2, :], S["l1v_ps"])

            QL = lambda b, h, k: QS1[b][0:k, h, T:LW]
            KL = lambda b, h, k: KS1[b][0:k, h, T:LW]

            def maxima(g):
                b, h0 = g // NG, g % NG * GH
                pe.wait_ge(S["l1_stacks"], 9 * 16 * 2 * B)
                if g == 0:
                    pe.wait_ge(S["l1q_ready"], B)
                    pe.wait_ge(S["l1k_ready"], B)
                    pe.wait_ge(S["v1_ready"], B)
                if g >= 1:
                    pe.wait_ge(S["k2_exp"], GH * g)
                for j in range(GH):
                    r = mm(ps[:, 6, tile(j)], QL(b, h0 + j, PROD), KL(b, h0 + j, PROD), start=True, stop=True)
                r.then_inc(S["k2_ps"], 1)
                for u in range(2 * GH):
                    n = 2 * GH * g + u
                    h = h0 + u // 2
                    if n >= 2:
                        pe.wait_ge(S["m_done"], n - 1)
                    if u % 2 == 0:
                        r = mm(bank(n % 2), QL(b, h, PROD), KS1[b][0:PROD, h, 0:T], start=True, stop=True)
                    else:
                        for t in range(NT):
                            r = mm(ps[:, n % 2, tile(t)], QS1[b][0:PROD, h, tile(t)], KL(b, h, PROD),
                                   start=True, stop=True)
                    r.then_inc(S["m_ps"], 1)

            def turn_maxima(g):
                pe.wait_ge(S["m_done"], 2 * GH * (g + 1))
                if g >= 1:
                    pe.wait_ge(S["n_split"], g)
                if g >= 2:
                    pe.wait_ge(S["y_ready"], g - 1)
                nc.tensor.transpose(ps[0:20, 5, 0:P], negm[:, g % 2, :], ident[:]).then_inc(S["n_ps"], 1)

            def landmark_values(g):
                b, h0 = g // NG, g % NG * GH
                pe.wait_ge(S["n_rows"][g % 2], 16 * PARTS * (g // 2 + 1))
                for j in range(GH):
                    n = GH * g + j
                    if n >= 2:
                        pe.wait_ge(S["k3_exp"], n - 1)
                    for kb in range(NT):
                        r = mm(ps[:, 2 + n % 2, tile(kb)], KS1[b][0:KROWS, h0 + j, tile(kb)], QL(b, h0 + j, KROWS),
                               start=True, stop=True)
                    r.then_inc(S["k3_ps"], 1)
                if g >= 1:
                    pe.wait_ge(S["yv_sb"], g)
                pe.wait_ge(S["k3_exp"], GH * (g + 1))
                for kb in range(NT):
                    for j in range(GH):
                        r = mm(ps[32 * j:32 * j + VW, 4, 0:P], V[:, b, kb, h0 + j, :],
                               PT[:, g % 2 * 4 + j, tile(kb)], start=(kb == 0), stop=(kb == NT - 1))
                r.then_inc(S["yv_ps"], 1)
                pe.wait_ge(S["a_ready"], g + 1)
                if g >= 1:
                    pe.wait_ge(S["col_done"], g)
                mm(ps[0:32, 7, :], ones[:, 0:32], AY[:, GH * g:GH * g + GH, 0:P], start=True, stop=True).then_inc(S["col_ps"], 1)
                pe.wait_ge(S["yv_sb"], g + 1)
                pe.wait_ge(S["n_split"], min(g + 2, G))
                if g >= 1:
                    pe.wait_ge(S["y_ready"], g)
                nc.tensor.transpose(ps[:, 5, 0:P], ysb[:], ident[:]).then_inc(S["ytr_ps"], 1)

            maxima(0)
            turn_maxima(0)
            for g in range(G):
                if g + 1 < G:
                    maxima(g + 1)
                    turn_maxima(g + 1)
                landmark_values(g)

            pe.wait_ge(S["rc_ready"], 1)
            mm(ps[:, 7, 0:1], ones[0:1, :], rc[:, 1:2], start=True, stop=True).then_inc(S["rcb_ps"], 1)
            pe.wait_ge(S["y_ready"], G)

            def heads_mm(s, done, lhs, rhs):
                for j in range(GH):
                    r = mm(ps[:, 2 * s + j // 2, j % 2 * WA:(j % 2 + 1) * WA], lhs(j), rhs(j), start=True, stop=True)
                r.then_inc(done, 1)

            def k1_scores(g, j):
                b, h, n = g // NG, g % NG * GH + j, GH * g + j
                if n >= 2:
                    pe.wait_ge(S["k1_exp"], n - 1)
                mm(bank(4 + n % 2), KL(b, h, KROWS), QS1[b][0:KROWS, h, 0:T], start=True, stop=True).then_inc(S["k1_ps"], 1)

            for q in range(G // 2):
                for s in range(2):
                    g = 2 * q + s
                    if g >= 2:
                        pe.wait_ge(S["wn_ready"], ITERS * (g - 1))
                    heads_mm(s, S["sq_ps"], lambda j: AY[:, GH * g + j, 0:P], lambda j: AY[:, GH * g + j, :])
                units = [(2 * q + k // GH, k % GH) for k in range(2 * GH)]
                for it in range(ITERS):
                    for s in range(2):
                        n = (q * ITERS + it) * 2 + s
                        if it == 0:
                            pe.wait_ge(S["w_ready"], 2 * q + s + 1)
                        else:
                            pe.wait_ge(S["wn_ready"], n - 1)
                        W = Wb[:, 2 * s + it % 2]
                        heads_mm(s, S["mm1_ps"], lambda j: W[:, j, 0:P], lambda j: W[:, j, :])
                    if units:
                        k1_scores(*units.pop(0))
                    for s in range(2):
                        n = (q * ITERS + it) * 2 + s
                        pe.wait_ge(S["d_ready"], n + 1)
                        heads_mm(s, S["mm2_ps"], lambda j: W2[:, s, j, 0:P], lambda j: Db[:, s, j, :])
                    if units:
                        k1_scores(*units.pop(0))
                for s in range(2):
                    g = 2 * q + s
                    pe.wait_ge(S["gaug_ready"], g + 1)
                    pe.wait_ge(S["k1_exp"], GH * (g + 1))
                    if g >= 1:
                        pe.wait_ge(S["xo_sb"], g)
                    for j in range(GH):
                        r = mm(ps[32 * j:32 * j + VW, 6, :], Gaug[:, s, j, :], PT[:, s * 4 + j, :], start=True, stop=True)
                    r.then_inc(S["x_ps"], 1)
                    pe.wait_ge(S["xo_sb"], g + 1)
                    if g >= 1:
                        pe.wait_ge(S["xo_ready"], g)
                    if g == 0:
                        pe.wait_ge(S["rcb_ready"], 1)
                    for t in range(NT):
                        r = nc.tensor.transpose(ps[:, 7, tile(t)], outT[:, tile(t)], ident[:])
                    r.then_inc(S["xtr_ps"], 1)

            pe.wait_ge(S["ld_ad"], 192)
            adapter(S["x4_ready"], S["t1_ps"], S["t1_ready"], S["z1_ps"], S["z1_ready"], S["u1_ps"], x4, a1, a2, AD, (S["ld_ad"], 192))
            for b in range(B):
                pe.wait_ge(S["n1_ready"], b + 1)
                turn(4 * b + 1, x2[:, b], S["xn1_ps"])
            pe.wait_ge(S["ld_f1"], 112)
            for b in range(B):
                pe.wait_ge(S["xn1_ready"], b + 1)
                for t in range(NT):
                    r = mm(ps[:, 4 * b + 2, t * E1:(t + 1) * E1], xnT[:, b, tile(t)], gateT[:], start=True, stop=True)
                r.then_inc(S["gate_ps"], 1)
            pe.wait_ge(S["ld_f1"], 112)
            pe.wait_ge(S["ld_f0"], 112)
            pe.wait_ge(S["cw1_ready"], B)
            for b in range(B):
                for t in range(NT):
                    if t == 0 and b >= 1:
                        pe.wait_ge(S["cw1T_ready"], b)
                    r = nc.tensor.transpose(ps[0:PARTS * E1, 4, :].bitcast(BF16)[:, tile(t)],
                                            cwp1[:, b, t].rearrange("p i e -> p (i e)"), identb[:])
                r.then_inc(S["cw1T_ps"], 1)
                for c in range(C1 + 1):
                    n = b * (C1 + 1) + c
                    rows = P if c < C1 else I1
                    if n >= 2:
                        pe.wait_ge(S["gelu_ready"], n - 1)
                        pe.wait_ge(S["gu_ready"], n - 1)
                    mm(ps[0:rows, n % 2, :], wg[:, tile(c)] if c < C1 else swg[:], xnT[:, b, :],
                       start=True, stop=True).then_inc(S["g_ps"], 1)
                    mm(ps[0:rows, 2 + n % 2, :], wu[:, tile(c)] if c < C1 else swu[:], xnT[:, b, :],
                       start=True, stop=True).then_inc(S["uu_ps"], 1)
                    if c < C1:
                        m = b * C1 + c
                        if c == 0:
                            pe.wait_ge(S["cw1T_ready"], b + 1)
                        if m >= 2:
                            pe.wait_ge(S["hid1_ready"], m - 1 + (1 if m - 2 >= C1 else 0))
                        mm(bank(5 + m % 2), sel1[:, c, :], cwT[0:PARTS * E1, b, :], start=True, stop=True).then_inc(S["cs_ps"], 1)
                pe.wait_ge(S["hid1_ready"], (C1 + 1) * (b + 1))
                if b >= 1:
                    pe.wait_ge(S["out_ready"], b)
                for t in range(NT):
                    for c in range(C1 + 1):
                        rows = P if c < C1 else I1
                        r = mm(ps[:, 7, tile(t)], hid[0:rows, c, tile(t)], wd[:, c, :] if c < C1 else swd[:],
                               start=(c == 0), stop=(c == C1))
                r.then_inc(S["fin_ps"], 1)

        @block.vector
        def _(dve):
            v = nc.vector
            steps = [0]

            def step(ins):
                steps[0] += 1
                ins.then_inc(S["step_dve"], 1)
                dve.wait_ge(S["step_dve"], steps[0])

            v.memset(ones[:], 1.0).then_inc(S["const_ready"], 1)
            v.memset(V[:], 1.0).then_inc(S["const_ready"], 1)
            dve.wait_ge(S["ld_in"], 80)
            for b in range(B):
                dve.wait_ge(S["y0_ps"], b + 1)
                v.tensor_scalar(y0T[:, b, :], bank(5 + b), b0[:, b:b + 1], None, ALU.add).then_inc(S["y0_ready"], 1)
            dve.wait_ge(S["ld_qkv"], 96)

            def split(part_sem, res_sem, n, width):
                dve.wait_ge(S["part_a"], part_sem + n + 1)
                v.tensor_tensor(res[:, n % 2, 0:width], qk[:, n % 2, 0:width], parts[:, n, 0, 0:width],
                                ALU.subtract).then_inc(S["res_a"], 1)
                dve.wait_ge(S["part_b"], part_sem + n + 1)
                return v.tensor_tensor(parts[:, n, 2, 0:width], res[:, n % 2, 0:width], parts[:, n, 1, 0:width],
                                       ALU.subtract)

            for n in range(4):
                b = n // 2
                dve.wait_ge(S["qk_ps"], 2 * n + 2)
                bk = [(5 * b + 2 * (n % 2) + k) % 8 for k in range(2)]
                if n >= 2:
                    dve.wait_ge(S["part_c"], n - 1)
                v.tensor_tensor(rot[:, 0, :], bank(bk[0]), cos[:], ALU.mult).then_inc(S["rot_cos"], 1)
                v.tensor_tensor(rot[:, 1, :], bank(bk[1]), sin[:], ALU.mult).then_inc(S["rot_cos"], 1)
                dve.wait_ge(S["rot_cos"], 2 * n + 2)
                v.tensor_tensor(qk[:, n % 2, 0:T], rot[:, 0, :], rot[:, 1, :], ALU.add).then_inc(S["rot_done"], 1)
                if n >= 1:
                    split(0, 0, n - 1, T).then_inc(S["part_c"], 1)
                dve.wait_ge(S["rot_done"], n + 1)
            split(0, 0, 3, T).then_inc(S["part_c"], 1)
            dve.wait_ge(S["const_ready"], 2)
            for b in range(B):
                dve.wait_ge(S["v_ps"], b + 1)
                v.tensor_copy(V[:, b, :, :, 0:HD],
                              ps[:, (5 * b + 4) % 8, :].rearrange("p (n h d) -> p n h d", n=NT, h=H)).then_inc(S["vaug_ready"], 1)

            def split_rows(k, par, rows, done):
                src = ps[0:rows, k, 0:P]
                step(v.tensor_copy(negT[0:rows, par, 0, :], src))
                step(v.tensor_tensor(negR[0:rows, :], src, negT[0:rows, par, 0, :], ALU.subtract))
                step(v.tensor_copy(negT[0:rows, par, 1, :], negR[0:rows, :]))
                v.tensor_tensor(negT[0:rows, par, 2, :], negR[0:rows, :], negT[0:rows, par, 1, :],
                                ALU.subtract).then_inc(done, 1)

            def s_max(g, u):
                n = GH * NT * g + u
                dve.wait_ge(S["smax_ps"], n + 1)
                if u == 0 and g >= 2:
                    dve.wait_ge(S["negT_ps"], g - 1)
                v.tensor_reduce(negm[:, g % 2, u:u + 1], bank(n % 2), AX.X, ALU.max, negate=True).then_inc(S["smax_done"], 1)

            def neg_parts(g):
                dve.wait_ge(S["negT_ps"], g + 1)
                if g >= 2:
                    dve.wait_ge(S["neg_rows"][g % 2], 16 * PARTS * (g // 2))
                if g >= 1:
                    dve.wait_ge(S["neg_split"], g)
                split_rows(7, g % 2, GH * NT, S["neg_split"])

            def normalise(src, dst, ready, done):
                step(v.reciprocal(rden[:], src[:, :, :, HD]))
                v.tensor_tensor(dst, src[:, :, :, 0:HD],
                                rden[:].rearrange("p n (h o) -> p n h o", o=1).to_broadcast([P, NT, GH, HD]),
                                ALU.mult).then_inc(done, 1)

            heads4 = lambda k: ps[:, k, :].rearrange("p (n h d) -> p n h d", n=NT, h=GH)

            def outputs(g, tr, k, dst, done):
                dve.wait_ge(tr, g + 1)
                if g >= 1:
                    dve.wait_ge(done, g)
                b, gg = g // NG, g % NG
                normalise(heads4(k), dst[:, b, :, gg * 32:gg * 32 + 32].rearrange("p n (h d) -> p n h d", d=HD), None, done)

            for g in range(2):
                for u in range(GH * NT):
                    s_max(g, u)
                if g == 0:
                    neg_parts(0)
            for g in range(G):
                if g + 2 < G:
                    for u in range(4):
                        s_max(g + 2, u)
                if g + 1 < G:
                    neg_parts(g + 1)
                if g >= 1:
                    outputs(g - 1, S["otr_ps"], 7, O, S["o_ready"])
                if g + 2 < G:
                    for u in range(4, GH * NT):
                        s_max(g + 2, u)
            outputs(G - 1, S["otr_ps"], 7, O, S["o_ready"])

            dve.wait_ge(S["xbias_ready"], B)
            for b in range(B):
                dve.wait_ge(S["proj_ps"], b + 1)
                v.tensor_tensor(x1[:, b].rearrange("p n f -> p (n f)"), bank(4 * b + 1),
                                x[:, b].rearrange("p n f -> p (n f)"), ALU.add).then_inc(S["x1_ready"], 1)

            def norm(u_ps, base_ready, rows, done, first):
                for b in range(B):
                    dve.wait_ge(u_ps, b + 1)
                    dve.wait_ge(base_ready, b + 1)
                    yb = y[:, b].rearrange("p n f -> p (n f)")
                    step(v.tensor_tensor(yb, bank(4 * b), base[:, b].rearrange("p n f -> p (n f)"), ALU.add))
                    for t in range(NT):
                        r = v.bn_stats(stats[:, b, t, :], y[:, b, t, :])
                    step(r)
                    for t in range(NT):
                        r = v.bn_aggr(mv[:, b, t, :], stats[:, b, t, :])
                    step(r)
                    step(v.tensor_scalar(veps[:, b, :], mv[:, b, :, 1], EPS, None, ALU.add))
                    v.reciprocal(rinv[:, b, :], veps[:, b, :]).then_inc(S["mv_ready"], 1)
                    dve.wait_ge(S["rstd_ready"], first + b + 1)
                    step(v.tensor_tensor(rinv[:, b, :], root[:, b, :], root[:, b, :], ALU.mult))
                    step(v.tensor_tensor(rinv[:, b, :], rinv[:, b, :], veps[:, b, :], ALU.mult))
                    step(v.tensor_scalar(rinv[:, b, :], rinv[:, b, :], -0.5, 1.5, ALU.mult, ALU.add))
                    step(v.tensor_tensor(rstd[:, b, :], rinv[:, b, :], root[:, b, :], ALU.mult))
                    for t in range(NT):
                        r = v.tensor_scalar(x2[:, b, t, :], y[:, b, t, :], mv[:, b, t, 0:1], rstd[:, b, t:t + 1],
                                            ALU.subtract, ALU.mult)
                    step(r)
                    row = lambda k: rows[:, b, k:k + 1, :].to_broadcast([P, NT, P])
                    step(v.tensor_tensor(y[:, b], x2[:, b], row(1), ALU.mult))
                    v.tensor_tensor(x2[:, b], y[:, b], row(2), ALU.add).then_inc(done, 1)

            dve.wait_ge(S["ld_c0"], 192)
            norm(S["u0_ps"], S["base0_ready"], rows0, S["n0_ready"], 0)

            def to3(src, w, parts_out, tmp, done):
                step(v.tensor_copy(parts_out[:, :, 0, :], src))
                step(v.tensor_tensor(tmp, src, parts_out[:, :, 0, :], ALU.subtract))
                step(v.tensor_copy(parts_out[:, :, 1, :], tmp))
                v.tensor_tensor(parts_out[:, :, 2, :], tmp, parts_out[:, :, 1, :], ALU.subtract).then_inc(done, 1)

            def col(ap, n):
                return ap.rearrange("p (n o) -> p n o", o=1).to_broadcast([P, NT, n])

            for b in range(B):
                step(v.memset(sim[:, b, :, E0:E0 + 8], LOW))
                step(v.memset(pick[:, b], LOW))
            for b in range(B):
                dve.wait_ge(S["sim_ps"], b + 1)
                step(v.tensor_copy(sim[:, b, :, 0:E0], ps[:, 4 * b + 3, 0:NT * E0].rearrange("p (n e) -> p n e", n=NT)))
                for t in range(NT):
                    r = v.max(best[:, b, t, :], sim[:, b, t, :])
                step(r)
                step(v.tensor_copy(pick[:, b, :, 0:TOP0], best[:, b, :, 0:TOP0]))
                for t in range(NT):
                    r = v.match_replace(took[:, b, t, :], pick[:, b, t, :], sim[:, b, t, :], HIGH)
                step(r)
                v.tensor_tensor(ex[:, b], sim[:, b, :, 0:E0], best[:, b, :, 0:1].to_broadcast([P, NT, E0]),
                                ALU.subtract).then_inc(S["sc_sub"], 1)
                step(v.tensor_tensor(took[:, b, :, 0:E0], took[:, b, :, 0:E0], sim[:, b, :, 0:E0], ALU.not_equal))
                dve.wait_ge(S["sc_exp"], b + 1)
                step(v.tensor_tensor(ex[:, b], ex2[:, b], took[:, b, :, 0:E0], ALU.mult))
                step(v.tensor_reduce(tot[:, b, :], ex[:, b], AX.X, ALU.add))
                step(v.reciprocal(totr[:, b, :], tot[:, b, :]))
                step(v.tensor_tensor(cw[:, b], ex[:, b], col(totr[:, b, :], E0), ALU.mult))
                to3(cw[:, b], E0, cwp[:, b], cwr[:, b], S["cwp_ready"])
            for b in range(B):
                dve.wait_ge(S["cwT_ps"], b + 1)
                v.tensor_copy(cwT[:, b, :], ps[0:PARTS * E0, 4, :].bitcast(BF16)[:, 0:T]).then_inc(S["cwT_ready"], 1)
                for c in range(C0):
                    n = b * C0 + c
                    if b == 1 and c == 0:
                        dve.wait_ge(S["down_ps"], 1)
                    dve.wait_ge(S["silu_ready"], n + 1)
                    dve.wait_ge(S["sel_ps"], n + 1)
                    v.tensor_tensor(hid[:, c, :], act_sb[:, n % 2, :], bank(2 + n % 2), ALU.mult).then_inc(S["hid_ready"], 1)
                if b == 0:
                    dve.wait_ge(S["ld_f0"], 112)
                dve.wait_ge(S["x12_ready"], b + 1)
                dve.wait_ge(S["down_ps"], b + 1)
                v.scalar_tensor_tensor(out=x3[:, b].rearrange("p n f -> p (n f)"), in0=bank(5), scalar=scale[:, 0:1],
                                       in1=base[:, b].rearrange("p n f -> p (n f)"), op0=ALU.mult,
                                       op1=ALU.add).then_inc(S["x3_ready"], 1)

            dve.wait_ge(S["ld_c1"], 160)
            for b in range(B):
                dve.wait_ge(S["y1_ps"], b + 1)
                v.tensor_scalar(y1T[:, b, :], bank(4 + b), b2[:, b:b + 1], None, ALU.add).then_inc(S["y1_ready"], 1)
            dve.wait_ge(S["ld_l1"], 48)
            dve.wait_ge(S["y1_ps"], B)
            for n in range(4):
                b, k = n // 2, n % 2
                dve.wait_ge((S["l1q_ps"], S["l1k_ps"])[k], b + 1)
                if n >= 2:
                    dve.wait_ge(S["l1_parts"], n - 1)
                v.tensor_scalar(qk[:, k, 0:T], bank(2 * k + b), bl1[:, k:k + 1], QSCALE, ALU.add,
                                ALU.mult).then_inc((S["l1q_ready"], S["l1k_ready"])[k], 1)
                dve.wait_ge((S["l1q_ready"], S["l1k_ready"])[k], b + 1)
                step(v.tensor_reduce(res[:, k, 0:LM], qk[:, k, 0:T].rearrange("p (m s) -> p m s", s=SEG), AX.X, ALU.add))
                v.tensor_scalar(qk[:, k, T:LW], res[:, k, 0:LM], 1.0 / SEG, None, ALU.mult).then_inc(S["lm_ready"], 1)
                dve.wait_ge(S["lm_ready"], n + 1)
                split(4, 4, n, LW).then_inc(S["l1_parts"], 1)
            for b in range(B):
                dve.wait_ge(S["l1v_ps"], b + 1)
                v.tensor_tensor(V[:, b, :, :, 0:HD], ps[:, 6 + b, :].rearrange("p (n h d) -> p n h d", n=NT, h=H),
                                bvb[:].rearrange("p (o h d) -> p o h d", o=1, h=H).to_broadcast([P, NT, H, HD]),
                                ALU.add).then_inc(S["v1_ready"], 1)

            def maxima(g):
                dve.wait_ge(S["k2_ps"], g + 1)
                if g >= 2:
                    dve.wait_ge(S["n_ps"], g - 1)
                if g >= 1:
                    dve.wait_ge(S["k2_exp"], GH * g)
                v.tensor_reduce(neg2[:], ps[:, 6, :].rearrange("p (h m) -> p h m", h=GH), AX.X, ALU.max,
                                negate=True).then_inc(S["k2_max"], 1)
                for u in range(2 * GH):
                    n = 2 * GH * g + u
                    dve.wait_ge(S["m_ps"], n + 1)
                    c = u // 2 * 5
                    if u % 2 == 0:
                        r = v.tensor_reduce(negm[:, g % 2, c + 4:c + 5], bank(n % 2), AX.X, ALU.max, negate=True)
                    else:
                        r = v.tensor_reduce(negm[:, g % 2, c:c + 4], ps[:, n % 2, :].rearrange("p (n m) -> p n m", n=NT),
                                            AX.X, ALU.max, negate=True)
                    r.then_inc(S["m_done"], 1)

            def max_parts(g):
                dve.wait_ge(S["n_ps"], g + 1)
                if g >= 2:
                    dve.wait_ge(S["n_rows"][g % 2], 16 * PARTS * (g // 2))
                if g == 0:
                    for k in range(2):
                        dve.wait_ge(S["neg_rows"][k], 16 * PARTS * G // 2)
                if g >= 1:
                    dve.wait_ge(S["n_split"], g)
                split_rows(5, g % 2, 20, S["n_split"])

            def landmarks(g):
                dve.wait_ge(S["k2_exp"], GH * (g + 1))
                if g >= 1:
                    dve.wait_ge(S["a_ready"], g)
                step(v.reciprocal(rsum[:], sums[:]))
                v.tensor_tensor(AY[:, GH * g:GH * g + GH, 0:P], ek2[:],
                                rsum[:].rearrange("p (h o) -> p h o", o=1).to_broadcast([P, GH, P]),
                                ALU.mult).then_inc(S["a_ready"], 1)

            def column_sums(g):
                dve.wait_ge(S["col_ps"], g + 1)
                v.tensor_reduce(cmax[:, g:g + 1], ps[0:1, 7, :], AX.X, ALU.max).then_inc(S["col_done"], 1)
                dve.wait_ge(S["ytr_ps"], g + 1)
                src = ps[:, 5, 0:P].rearrange("p (h d) -> p h d", h=GH)
                if g >= 1:
                    dve.wait_ge(S["y_ready"], g)
                step(v.reciprocal(rden[:, 0, :], src[:, :, HD]))
                v.tensor_tensor(AY[:, GH * g:GH * g + GH, P:WA], src[:, :, 0:HD],
                                rden[:, 0, :].rearrange("p (h o) -> p h o", o=1).to_broadcast([P, GH, HD]),
                                ALU.mult).then_inc(S["y_ready"], 1)

            maxima(0)
            max_parts(0)
            landmarks(0)
            for g in range(G):
                if g + 1 < G:
                    maxima(g + 1)
                    max_parts(g + 1)
                    landmarks(g + 1)
                column_sums(g)

            dve.wait_ge(S["col_done"], G)
            step(v.tensor_reduce(rc[:, 0:1], cmax[:], AX.X, ALU.max))
            v.reciprocal(rc[:, 1:2], rc[:, 0:1]).then_inc(S["rc_ready"], 1)
            dve.wait_ge(S["rcb_ps"], 1)
            v.tensor_copy(rcb[:], ps[:, 7, 0:1]).then_inc(S["rcb_ready"], 1)
            v.memset(Gaug[:], 1.0).then_inc(S["gaug_ones"], 1)

            pair = lambda s: ps[:, 2 * s:2 * s + 2, 0:2 * WA]
            flat = lambda ap: ap.rearrange("p (k h) w -> p k (h w)", k=2)
            for q in range(G // 2):
                for it in range(ITERS):
                    for s in range(2):
                        n = (q * ITERS + it) * 2 + s
                        W = Wb[:, 2 * s + it % 2]
                        dve.wait_ge(S["w2_ready"], n + 1)
                        v.scalar_tensor_tensor(out=Db[:, s], in0=W, scalar=7.0, in1=W2[:, s],
                                               op0=ALU.mult, op1=ALU.subtract).then_inc(S["d_ready"], 1)
                        dve.wait_ge(S["f_ready"], n + 1)
                        step(v.scalar_tensor_tensor(out=Fb[:, s], in0=W, scalar=3.25, in1=Fb[:, s],
                                                    op0=ALU.mult, op1=ALU.subtract))
                    for s in range(2):
                        n = (q * ITERS + it) * 2 + s
                        dve.wait_ge(S["mm2_ps"], n + 1)
                        v.scalar_tensor_tensor(out=flat(Wb[:, 2 * s + (it + 1) % 2]), in0=pair(s), scalar=0.25,
                                               in1=flat(Fb[:, s]), op0=ALU.mult, op1=ALU.add).then_inc(S["wn_ready"], 1)
                dve.wait_ge(S["gaug_ones"], 1)
                for s in range(2):
                    g = 2 * q + s
                    dve.wait_ge(S["wn_ready"], (q * ITERS + ITERS - 1) * 2 + s + 1)
                    if g >= 2:
                        dve.wait_ge(S["x_ps"], g - 1)
                    v.tensor_copy(Gaug[:, s, :, 0:HD], Wb[:, 2 * s + ITERS % 2, :, P:WA]).then_inc(S["gaug_ready"], 1)
                for s in range(2):
                    outputs(2 * q + s, S["xtr_ps"], 7, O, S["xo_ready"])
            for b in range(B):
                dve.wait_ge(S["xo_ready"], NG * (b + 1))
                v.tensor_tensor(x4[:, b], O[:, b], x3[:, b], ALU.add).then_inc(S["x4_ready"], 1)

            dve.wait_ge(S["ld_ad"], 192)
            norm(S["u1_ps"], S["base1_ready"], rows1, S["n1_ready"], B)

            for b in range(B):
                step(v.memset(sim1[:, b, :, E1:16], LOW))
                step(v.memset(pick[:, b], LOW))
            for b in range(B):
                dve.wait_ge(S["gate_ps"], b + 1)
                lg = ps[:, 4 * b + 2, 0:NT * E1].rearrange("p (n e) -> p n e", n=NT)
                step(v.tensor_reduce(tot[:, b, :], lg, AX.X, ALU.max))
                v.tensor_tensor(ex[:, b, :, 0:E1], lg, col(tot[:, b, :], E1), ALU.subtract).then_inc(S["sc_sub"], 1)
                dve.wait_ge(S["sc_exp"], B + b + 1)
                step(v.tensor_reduce(tot[:, b, :], ex2[:, b, :, 0:E1], AX.X, ALU.add))
                step(v.reciprocal(totr[:, b, :], tot[:, b, :]))
                step(v.tensor_tensor(sim1[:, b, :, 0:E1], ex2[:, b, :, 0:E1], col(totr[:, b, :], E1), ALU.mult))
                for t in range(NT):
                    r = v.max(best[:, b, t, :], sim1[:, b, t, :])
                step(r)
                step(v.tensor_copy(pick[:, b, :, 0:TOP1], best[:, b, :, 0:TOP1]))
                for t in range(NT):
                    r = v.match_replace(took1[:, b, t, :], pick[:, b, t, :], sim1[:, b, t, :], HIGH)
                step(r)
                step(v.tensor_tensor(ex[:, b, :, 0:E1], took1[:, b, :, 0:E1], sim1[:, b, :, 0:E1], ALU.not_equal))
                step(v.tensor_reduce(tot[:, b, :], best[:, b, :, 0:TOP1], AX.X, ALU.add))
                step(v.tensor_scalar(tot[:, b, :], tot[:, b, :], 1e-20, None, ALU.add))
                step(v.reciprocal(totr[:, b, :], tot[:, b, :]))
                step(v.tensor_tensor(ex2[:, b, :, 0:E1], ex[:, b, :, 0:E1], sim1[:, b, :, 0:E1], ALU.mult))
                step(v.tensor_tensor(cw[:, b, :, 0:E1], ex2[:, b, :, 0:E1], col(totr[:, b, :], E1), ALU.mult))
                to3(cw[:, b, :, 0:E1], E1, cwp1[:, b], cwr[:, b, :, 0:E1], S["cw1_ready"])
            for b in range(B):
                dve.wait_ge(S["cw1T_ps"], b + 1)
                v.tensor_copy(cwT[0:PARTS * E1, b, :], ps[0:PARTS * E1, 4, :].bitcast(BF16)[:, 0:T]).then_inc(S["cw1T_ready"], 1)
                for c in range(C1 + 1):
                    n = b * (C1 + 1) + c
                    rows = P if c < C1 else I1
                    if b == 1 and c == 0:
                        dve.wait_ge(S["fin_ps"], 1)
                    dve.wait_ge(S["gelu_ready"], n + 1)
                    dve.wait_ge(S["uu_ps"], n + 1)
                    if c < C1:
                        if n >= 2:
                            dve.wait_ge(S["hid1_ready"], n - 1)
                        v.tensor_tensor(gu_sb[:, n % 2, :], act_sb[:, n % 2, :], bank(2 + n % 2), ALU.mult).then_inc(S["gu_ready"], 1)
                        m = b * C1 + c
                        dve.wait_ge(S["gu_ready"], n + 1)
                        dve.wait_ge(S["cs_ps"], m + 1)
                        v.tensor_tensor(hid[:, c, :], gu_sb[:, n % 2, :], bank(5 + m % 2), ALU.mult).then_inc(S["hid1_ready"], 1)
                    else:
                        v.tensor_tensor(hid[0:rows, c, :], act_sb[0:rows, n % 2, :], ps[0:rows, 2 + n % 2, :],
                                        ALU.mult).then_inc(S["hid1_ready"], 1)
                        dve.wait_ge(S["hid1_ready"], n + 1)
                        v.memset(gu_sb[0:1, n % 2, 0:1], 0.0).then_inc(S["gu_ready"], 1)
                dve.wait_ge(S["fin_ps"], b + 1)
                v.tensor_tensor(y[:, b].rearrange("p n f -> p (n f)"), bank(7),
                                x4[:, b].rearrange("p n f -> p (n f)"), ALU.add).then_inc(S["out_ready"], 1)

        @block.scalar
        def _(act):
            f = nc.scalar.activation

            def split(base_n, ready, n, width):
                act.wait_ge(*ready)
                f(parts[:, n, 0, 0:width], qk[:, n % 2, 0:width], ACT.Copy).then_inc(S["part_a"], 1)
                act.wait_ge(S["res_a"], base_n + n + 1)
                f(parts[:, n, 1, 0:width], res[:, n % 2, 0:width], ACT.Copy).then_inc(S["part_b"], 1)

            for n in range(4):
                split(0, (S["rot_done"], n + 1), n, T)

            for g in range(G):
                for p in range(8):
                    n, kb = 8 * g + p, 4 * g + p // 2
                    act.wait_ge(S["st_ps"], n + 1)
                    if kb >= 2:
                        act.wait_ge(S["av_ps"], kb - 1)
                    k = 2 + p % 2 * 2
                    f(PT[:, kb % 2 * 4 + p % 2 * 2:kb % 2 * 4 + p % 2 * 2 + 2, :], ps[:, k:k + 2, :], ACT.Exp,
                      scale=MAPS).then_inc(S["exp_done"], 1)
                    if p == 1 and g >= 1:
                        act.wait_ge(S["av_ps"], 4 * g)
                        if g >= 2:
                            act.wait_ge(S["otr_ps"], g - 1)
                        f(outT[:], bank(6), ACT.Copy).then_inc(S["outT_ready"], 1)
            act.wait_ge(S["av_ps"], 4 * G)
            act.wait_ge(S["otr_ps"], G - 1)
            f(outT[:], bank(6), ACT.Copy).then_inc(S["outT_ready"], 1)

            for b in range(B):
                act.wait_ge(S["oT_ps"], b + 1)
                f(featT[:, b, :], bank(4 * b), ACT.Copy).then_inc(S["oT_ready"], 1)

            def adapter(t_ps, t_ready, z_ps, z_ready, rows, bias, last):
                for b in range(B):
                    act.wait_ge(t_ps, b + 1)
                    act.wait_ge(*last[b])
                    f(featT[:, b, :], bank(4 * b + 2), ACT.Copy).then_inc(t_ready, 1)
                for b in range(B):
                    act.wait_ge(z_ps, b + 1)
                    f(zT[0:rows, b, :], ps[0:rows, 4 * b + 3, :], ACT.Relu, bias=bias[:, b:b + 1]).then_inc(z_ready, 1)

            def roots(first):
                for b in range(B):
                    act.wait_ge(S["mv_ready"], first + b + 1)
                    f(root[:, b, :], rinv[:, b, :], ACT.Sqrt).then_inc(S["rstd_ready"], 1)

            act.wait_ge(S["ld_c0"], 192)
            adapter(S["t0_ps"], S["t0_ready"], S["z0_ps"], S["z0_ready"], P, bdn, [(S["proj_ps"], 1), (S["proj_ps"], 2)])
            roots(0)
            for b in range(B):
                act.wait_ge(S["xn0_ps"], b + 1)
                f(xnT[:, b, :], bank(4 * b + 1), ACT.Copy).then_inc(S["xn0_ready"], 1)
            for b in range(B):
                act.wait_ge(S["hash_ps"], b + 1)
                f(hT[:, b, :], ps[0:PD, 4 * b + 2, :], ACT.Copy).then_inc(S["hash_ready"], 1)
            for b in range(B):
                act.wait_ge(S["sc_sub"], b + 1)
                f(ex2[:, b], ex[:, b], ACT.Exp).then_inc(S["sc_exp"], 1)
            for n in range(B * C0):
                act.wait_ge(S["up_proj_ps"], n + 1)
                if n >= 2:
                    act.wait_ge(S["hid_ready"], n - 1)
                f(act_sb[:, n % 2, :], bank(n % 2), ACT.Silu).then_inc(S["silu_ready"], 1)
            for b in range(B):
                act.wait_ge(S["x3T_ps"], b + 1)
                f(featT[:, b, :], bank(6 + b), ACT.Copy).then_inc(S["x3T_ready"], 1)
            act.wait_ge(S["ld_c1"], 160)
            act.wait_ge(S["down_ps"], B)
            for n in range(B * HC):
                act.wait_ge(S["h1_ps"], n + 1)
                f(hid[:, n, :], bank(n % 4), ACT.Gelu, bias=b1[:, n % HC:n % HC + 1]).then_inc(S["h1_ready"], 1)
            for n in range(4):
                if n == 0:
                    act.wait_ge(S["parts_out"], 16 * PARTS * 4)
                split(4, (S["lm_ready"], n + 1), n, LW)

            def landmark_exp(g):
                act.wait_ge(S["k2_max"], g + 1)
                if g >= 1:
                    act.wait_ge(S["a_ready"], g)
                for j in range(GH):
                    f(ek2[:, j, :], ps[:, 6, tile(j)], ACT.Exp, bias=neg2[:, j:j + 1],
                      accum_out=sums[:, j:j + 1]).then_inc(S["k2_exp"], 1)

            def value_exp(g):
                for j in range(GH):
                    n = GH * g + j
                    act.wait_ge(S["k3_ps"], n + 1)
                    if g >= 2:
                        act.wait_ge(S["yv_ps"], g - 1)
                    if g < 2:
                        act.wait_ge(S["y1_ps"], B)
                    f(PT[:, g % 2 * 4 + j, :], bank(2 + n % 2), ACT.Exp).then_inc(S["k3_exp"], 1)
                act.wait_ge(S["yv_ps"], g + 1)
                if g >= 1:
                    act.wait_ge(S["ytr_ps"], g)
                f(ysb[:], ps[:, 4, 0:P], ACT.Copy).then_inc(S["yv_sb"], 1)

            landmark_exp(0)
            for g in range(G):
                if g + 1 < G:
                    landmark_exp(g + 1)
                value_exp(g)

            act.wait_ge(S["rcb_ready"], 1)
            pair = lambda s: ps[:, 2 * s:2 * s + 2, 0:2 * WA]
            flat = lambda ap: ap.rearrange("p (k h) w -> p k (h w)", k=2)

            def k1_exp(g, j):
                n = GH * g + j
                act.wait_ge(S["k1_ps"], n + 1)
                if g >= 2:
                    act.wait_ge(S["x_ps"], g - 1)
                if g < 2:
                    act.wait_ge(S["yv_ps"], G)
                f(PT[:, g % 2 * 4 + j, :], bank(4 + n % 2), ACT.Exp).then_inc(S["k1_exp"], 1)

            for q in range(G // 2):
                for s in range(2):
                    g = 2 * q + s
                    act.wait_ge(S["sq_ps"], g + 1)
                    if g >= 2:
                        act.wait_ge(S["gaug_ready"], g - 1)
                    f(flat(Wb[:, 2 * s]), pair(s), ACT.Copy, scale=rcb[:, 0:1]).then_inc(S["w_ready"], 1)
                units = [(2 * q + k // GH, k % GH) for k in range(2 * GH)]
                for it in range(ITERS):
                    for s in range(2):
                        n = (q * ITERS + it) * 2 + s
                        act.wait_ge(S["mm1_ps"], n + 1)
                        f(flat(W2[:, s]), pair(s), ACT.Copy).then_inc(S["w2_ready"], 1)
                    for _ in range(2):
                        if units:
                            k1_exp(*units.pop(0))
                for s in range(2):
                    g = 2 * q + s
                    act.wait_ge(S["x_ps"], g + 1)
                    if g >= 1:
                        act.wait_ge(S["xtr_ps"], g)
                    f(outT[:], bank(6), ACT.Copy).then_inc(S["xo_sb"], 1)

            act.wait_ge(S["ld_ad"], 192)
            adapter(S["t1_ps"], S["t1_ready"], S["z1_ps"], S["z1_ready"], AD, ab1, [(S["h1_ps"], B * HC)] * 2)
            roots(B)
            for b in range(B):
                act.wait_ge(S["xn1_ps"], b + 1)
                f(xnT[:, b, :], bank(4 * b + 1), ACT.Copy).then_inc(S["xn1_ready"], 1)
            for b in range(B):
                act.wait_ge(S["sc_sub"], B + b + 1)
                f(ex2[:, b, :, 0:E1], ex[:, b, :, 0:E1], ACT.Exp).then_inc(S["sc_exp"], 1)
            for n in range(B * (C1 + 1)):
                rows = P if n % (C1 + 1) < C1 else I1
                act.wait_ge(S["g_ps"], n + 1)
                if n >= 2:
                    act.wait_ge(S["gu_ready"], n - 1)
                f(act_sb[0:rows, n % 2, :], ps[0:rows, n % 2, :], ACT.Gelu).then_inc(S["gelu_ready"], 1)

        @block.gpsimd
        def _(pool):
            g_ = nc.gpsimd
            two = float(np.array([0x3F803F80], np.uint32).view(np.float32)[0])
            g_.memset(KS[64:96, :, :].bitcast(F32), two).then_inc(S["ones_rows"], 1)
            pool.wait_ge(S["ones_rows"], 1)
            pool.wait_ge(S["ld_res"], 64)
            for b in range(B):
                r = g_.tensor_tensor(x[:, b], x[:, b], boutb[:].rearrange("p (o f) -> p o f", o=1).to_broadcast([P, NT, P]),
                                     ALU.add)
                r.then_inc(S["xbias_ready"], 1)
                pool.wait_ge(S["xbias_ready"], b + 1)
            pool.wait_ge(S["ld_c0"], 192)
            for b in range(B):
                pool.wait_ge(S["x1_ready"], b + 1)
                g_.tensor_tensor(base[:, b], x1[:, b], rows0[:, b, 0:1, :].to_broadcast([P, NT, P]),
                                 ALU.add).then_inc(S["base0_ready"], 1)
                pool.wait_ge(S["base0_ready"], b + 1)
            for b in range(B):
                pool.wait_ge(S["n0_ready"], b + 1)
                g_.tensor_tensor(base[:, b], x1[:, b], x2[:, b], ALU.add).then_inc(S["x12_ready"], 1)
                pool.wait_ge(S["x12_ready"], b + 1)
            for n in range(G // 2 * ITERS * 2):
                s = n % 2
                pool.wait_ge(S["w2_ready"], n + 1)
                if n >= 2:
                    pool.wait_ge(S["wn_ready"], n - 1)
                g_.tensor_scalar(Fb[:, s], W2[:, s], 3.75, None, ALU.mult).then_inc(S["f_ready"], 1)
                pool.wait_ge(S["f_ready"], n + 1)
            pool.wait_ge(S["ld_ad"], 192)
            for b in range(B):
                pool.wait_ge(S["x4_ready"], b + 1)
                g_.tensor_tensor(base[:, b], x4[:, b], rows1[:, b, 0:1, :].to_broadcast([P, NT, P]),
                                 ALU.add).then_inc(S["base1_ready"], 1)
                pool.wait_ge(S["base1_ready"], b + 1)


def tables():
    f = np.float32
    inv = (f(1.0) / np.power(f(10000.0), (np.arange(0, HD, 2, dtype=f) / f(HD)))).astype(f)
    fr = np.arange(T, dtype=f)[:, None] * inv[None, :]
    emb = np.concatenate((fr, fr), axis=-1)
    cos, sin = np.cos(emb).astype(f), np.sin(emb).astype(f)
    sign = np.where(np.arange(HD) < HD // 2, f(-1), f(1))
    spread = lambda m: np.ascontiguousarray(np.repeat(m.T, H, axis=0))
    ident = np.eye(P, dtype=f)
    bf = lambda m: (m * 0x3F80).astype(np.uint16)

    def select(experts, width, chunks):
        s = np.zeros((PARTS, experts, chunks, P), f)
        for c in range(chunks):
            for m in range(P):
                s[:, (c * P + m) // width, c, m] = 1
        return bf(s.reshape(PARTS * experts, chunks, P))

    return {"cos": spread(cos), "sin": spread(sin * sign), "ident": ident, "identb": bf(ident),
            "sel0": select(E0, PD, C0), "sel1": select(E1, I1, C1)}


def kernel(**inputs):
    import concourse.bacc as bacc
    from concourse.bass_utils import run_bass_kernel_spmd

    w = {k: np.asarray(v) for k, v in inputs.items()}
    c = np.ascontiguousarray
    dh = np.arange(H * HD).reshape(H, HD).T.reshape(-1)
    turned = [1, 3, 5, 7, 0, 2, 4, 6]
    dhr = np.arange(H * HD).reshape(H, HD)[:, turned].T.reshape(-1)
    q, k, v = np.split(w["L0_attn_w_qkv"], 3, axis=0)
    data = {
        "ids": np.concatenate([w["itok_B_0_7"], w["itok_B_0_6"], w["itok_B_0_8"]])[None, :],
        "x": w["x"], "xT": w["x"].transpose(0, 2, 1),
        "w0T": w["L0_cond_weight"].transpose(0, 2, 1), "b0": w["L0_cond_bias"],
        "wqkT": np.stack([q[dh].T, q[dhr].T, k[dh].T, k[dhr].T]), "wvT": v.T,
        "woutT": w["L0_attn_w_out"].T, "bout": w["L0_attn_b_out"][None, :],
        "down": w["L0_cond2_down_w"], "bd": w["L0_cond2_down_b"], "up": w["L0_cond2_up_w"],
        "bu": w["L0_cond2_up_b"], "ln_g": w["L0_cond2_ln_g"], "ln_b": w["L0_cond2_ln_b"],
        "hashT": w["L0_ffn_hasher_w"].T, "keysT": w["L0_ffn_keys"].T, "vd": w["L0_ffn_values_down"],
        "vu": w["L0_ffn_values_up"], "scale": w["L0_ffn_scale"][None, :],
        "w1": w["L1_cond_W1"], "b1": w["L1_cond_b1"].reshape(HC, P).T, "w2": w["L1_cond_W2"], "b2": w["L1_cond_b2"],
        "we": w["L1_cond_We"], "be": w["L1_cond_be"],
        "wl1T": np.stack([w["L1_attn_Wq"][dh].T, w["L1_attn_Wk"][dh].T, w["L1_attn_Wv"].T]),
        "bl1": np.stack([w["L1_attn_bq"][dh], w["L1_attn_bk"][dh]], axis=1), "bv": w["L1_attn_bv"][None, :],
        "a1": w["L1_cond2_W1"], "ab1": w["L1_cond2_b1"], "a2": w["L1_cond2_W2"], "ab2": w["L1_cond2_b2"],
        "gamma": w["L1_cond2_gamma"], "beta": w["L1_cond2_beta"],
        "gateT": w["L1_ffn_gate_w"].T, "wg": w["L1_ffn_Wg"], "wu": w["L1_ffn_Wu"], "wd": w["L1_ffn_Wd"],
        "swg": w["L1_ffn_sWg"], "swu": w["L1_ffn_sWu"], "swd": w["L1_ffn_sWd"],
        **tables(),
    }
    nc = bacc.Bacc("TRN2", target_bir_lowering=False, num_devices=1)
    arrays, aps = {}, {}
    for name, value in data.items():
        arrays[f"in_{name}"] = c(value)
        aps[name] = nc.dram_tensor(f"in_{name}", value.shape, mybir.dt.from_np(value.dtype), kind="ExternalInput").ap()
    out = nc.dram_tensor("out_0", (B, T, P), F32, kind="ExternalOutput").ap()
    build(nc, aps, out)
    r = run_bass_kernel_spmd(nc, [arrays], core_ids=[0])
    return r.results[0]["out_0"]
```

```python
from contextlib import ExitStack

import numpy as np

import concourse.bass as bass
from concourse import mybir

F32 = mybir.dt.float32
BF16 = mybir.dt.bfloat16
I32 = mybir.dt.int32
U16 = mybir.dt.uint16
ALU = mybir.AluOpType
ACT = mybir.ActivationFunctionType
AX = mybir.AxisListType

P = 128
B, T = 2, 512
NT = T // P
H, HD = 16, 8
GH = 4
NG = H // GH
G = B * NG
PARTS = 3
PROD = PARTS * PARTS * HD
KROWS = PROD + PARTS
LM = 128
SEG = T // LM
LW = T + LM
ITERS = 6
VW = 2 * HD
WA = P + HD
E0, PD, TOP0 = 32, 32, 4
C0 = E0 * PD // P
HC = 4
UN = GH * NT
LAG = 28
AD = 32
E1, I1, TOP1 = 8, 64, 2
C1 = E1 // 2
RING = (0, 1, 7)
WINDOW = 2 * PARTS - 1
STACK_DMAS = 2 * PARTS
EPS = 1e-5
LOW = -3.0e38
HIGH = 3.0e38

SEMAPHORES = """ld_ids ld_in ld_qkv ld_res ld_c0 ld_f0 ld_c1 ld_l1 ld_ad ld_f1
mv_ready rstd_ready const_ready step_dve stored
y0_ps y0_ready qk_ps v_ps rot_cos rot_done part_a res_a part_b part_c parts_out_0 parts_out_1 parts_out_2 parts_out_3 stacks_in_0 stacks_in_1 ones_rows vaug_ready
smax_ps smax_done negT_ps neg_copy neg_step neg_split neg_rows_0 neg_rows_1 st_ps exp_done av_ps outT_ready otr_ps o_ready
oT_ps oT_ready proj_ps x1_ready xbias_ready
t0_ps t0_ready t1_ps t1_ready z0_ps z0_ready z1_ps z1_ready u0_ps u1_ps n0_ready n1_ready base0_ready base1_ready
xn0_ps xn0_ready xn1_ps xn1_ready
hash_ps hash_ready sim_ps cwp_ready cwT_ps cwT_ready up_proj_ps silu_ready sel_ps hid_ready down_ps x3_ready x12_ready
x3T_ps x3T_ready h1_ps h1_ready y1_ps y1_ready
l1q_ps l1k_ps l1v_ps l1q_ready l1k_ready bl1_ready lm_ready v1_ready l1_parts
k2_ps k2_max k2_exp rs_ready a_ready col_ps col_done m_ps m_done n_ps n_copy n_split n_rows_0 n_rows_1 k3_ps k3_exp yv_ps yv_sb ytr_ps y_ready
rc_ready rcb_ps rcb_ready
sq_ps w_ready mm1_ps w2_ready e_ready f_ready d_ready mm2_ps wn_ready k1_ps k1_exp gaug_ready x_ps xo_sb xtr_ps xo_ready x4_ready gaug_ones
gate_ps sc_sub sc_exp cw1_ready cw1T_ps cw1T_ready g_ps gelu_ready uu_ps gu_ready cs_ps hid1_ready fin_ps out_ready"""


def build(nc, a, out):
    ctx = ExitStack()
    with ctx:
        def sb(name, shape, dt=F32):
            return ctx.enter_context(nc.sbuf_tensor(name, shape, dt))

        S = {}
        for n in SEMAPHORES.split():
            S[n] = ctx.enter_context(nc.semaphore(n))

        S["stacks_in"] = (S["stacks_in_0"], S["stacks_in_1"])
        S["parts_out"] = [S[f"parts_out_{n}"] for n in range(4)]
        S["neg_rows"] = (S["neg_rows_0"], S["neg_rows_1"])
        S["n_rows"] = (S["n_rows_0"], S["n_rows_1"])

        ids = sb("ids", [1, 8], I32)
        ident = sb("ident", [P, P])
        identb = sb("identb", [P, P], BF16)
        ones = sb("ones", [P, P])
        x = sb("x", [P, B, NT, P])
        xT = sb("xT", [P, B, T])
        w0T = sb("w0T", [P, B, P])
        b0 = sb("b0", [P, B])
        y0T = sb("y0T", [P, B, T])
        wqk = sb("wqk", [P, 4, P])
        wv = sb("wv", [P, P])
        QS = sb("QS", [P, B, H * LW], BF16)
        KS = sb("KS", [P, B, H * LW], BF16)
        V = sb("V", [P, B, NT, H, VW])
        woutT = sb("woutT", [P, P])
        boutb = sb("boutb", [P, P])
        negm = sb("negm", [P, 2, 20])
        negT = sb("negT", [32, 2, PARTS, P], BF16)
        negR = sb("negR", [32, 2, P])
        negS = sb("negS", [32, P])
        outT = sb("outT", [P, T])
        rden = sb("rden", [P, NT, GH])
        O = sb("O", [P, B, NT, P])
        featT = sb("featT", [P, B, T])
        stats = sb("stats", [P, B, NT, 6])
        mv = sb("mv", [P, B, NT, 2])
        rstd = sb("rstd", [P, B, NT])
        veps = sb("veps", [P, B, NT])
        rinv = sb("rinv", [P, B, NT])
        root = sb("root", [P, B, NT])
        wdn = sb("wdn", [P, B, P])
        bdn = sb("bdn", [P, B])
        wup = sb("wup", [P, B, P])
        rows0 = sb("rows0", [P, B, 3, P])
        rows1 = sb("rows1", [P, B, 3, P])
        hashT = sb("hashT", [P, PD])
        keysT = sb("keysT", [PD, E0])
        scale = sb("scale", [P, 1])
        sel0 = sb("sel0", [PARTS * E0, C0, P], BF16)
        sel1 = sb("sel1", [PARTS * E1, C1, P], BF16)
        sim = sb("sim", [P, B, NT, E0 + 8])
        took = sb("took", [P, B, NT, E0 + 8])
        best = sb("best", [P, B, NT, 8])
        pick = sb("pick", [P, B, NT, 8])
        ex = sb("ex", [P, B, NT, E0])
        ex2 = sb("ex2", [P, B, NT, E0])
        tot = sb("tot", [P, B, NT])
        totr = sb("totr", [P, B, NT])
        cw = sb("cw", [P, B, NT, E0])
        cwr = ex
        cwp = sb("cwp", [P, B, NT, PARTS, E0], BF16)
        cwT = sb("cwT", [PARTS * E0, B, T], BF16)
        sim1 = sim[:, :, :, 0:16]
        took1 = took[:, :, :, 0:16]
        cwp1 = sb("cwp1", [P, B, NT, PARTS, E1], BF16)
        b1 = sb("b1", [P, HC])
        b2 = sb("b2", [P, B])
        wl1 = sb("wl1", [P, 3, P])
        bl1 = sb("bl1", [P, 2])
        bl1s = sb("bl1s", [P, 2])
        bvb = sb("bvb", [P, P])
        sums = sb("sums", [P, GH])
        rsum = sb("rsum", [P, GH])
        cmax = sb("cmax", [1, G])
        rc = sb("rc", [1, 2])
        rcb = sb("rcb", [P, 1])
        Gaug = sb("Gaug", [P, 2, GH, VW])
        gateT = sb("gateT", [P, E1])
        a1 = sb("a1", [P, B, AD])
        ab1 = sb("ab1", [AD, B])
        a2 = sb("a2", [AD, B, P])

        PT = sb("PT", [P, 8, T])
        early = sb("early", [P, 6400])
        late = sb("late", [P, 5440])

        def view(buf, at, *shape):
            n = int(np.prod(shape))
            ap = buf[:, at:at + n]
            names = " ".join("abcd"[:len(shape)])
            return ap.rearrange(f"p ({names}) -> p {names}", **dict(zip("abcd", shape))) if len(shape) > 1 else ap

        PW = PARTS * LW * 4 // 2
        parts = early[:, 0:PW].bitcast(BF16).rearrange("p (n i t) -> p n i t", n=4, i=PARTS)
        qk = view(early, PW, 2, LW)
        res = view(early, PW + 2 * LW, 2, LW)
        vd = view(early, 0, E0 * PD)
        vu = view(early, 1024, C0, P)
        act_sb = view(early, 2048, 2, T)
        gu_sb = view(early, 3072, 2, T)
        w1 = view(early, 4096, HC, P)
        w2 = view(early, 4608, B, HC, P)
        AY = view(early, 0, B * H, WA)
        wg = view(early, 4352, E1 * I1)
        wu = view(early, 4864, E1 * I1)
        wd = view(early, 5376, C1, P)
        swg = view(early, 5888, I1)
        swu = view(early, 5952, I1)
        swd = early[0:I1, 6016:6016 + P]
        x1 = view(late, 0, B, NT, P)
        base = view(late, 1024, B, NT, P)
        y = view(late, 2048, B, NT, P)
        x2 = view(late, 3072, B, NT, P)
        zT = view(late, 4096, B, T)
        hT = late[0:PD, 4096:5120].rearrange("p (b t) -> p b t", b=B)
        Wb = view(late, 0, 2 * 2, GH, WA)
        W2 = view(late, 2176, 2, GH, WA)
        Fb = view(late, 3264, 2, GH, WA)
        Db = view(late, 4352, 2, GH, WA)
        cos, sin, rot = PT[:, 0, :], PT[:, 1, :], PT[:, 2:4, :]
        ek2 = featT[:, 0, :].rearrange("p (h m) -> p h m", h=GH)
        ysb = featT[:, 1, 0:P]
        neg2 = sb("neg2", [P, GH])
        x3 = x
        xnT = y0T
        y1T = xT
        x4 = O
        hid = PT

        ps = ctx.enter_context(nc.psum_tensor("ps", [P, 8, T], F32))
        bank = lambda i: ps[:, i, :]

        parts_dram = [nc.dram_tensor(f"parts_layer{n}", [4, WINDOW, HD, H, width], BF16, kind="Internal").ap()
                      for n, width in enumerate((T, LW))]

        QS0 = [QS[:, b, 0:H * T].rearrange("p (h t) -> p h t", h=H) for b in range(B)]
        KS0 = [KS[:, b, 0:H * T].rearrange("p (h t) -> p h t", h=H) for b in range(B)]
        QS1 = [QS[:, b, :].rearrange("p (h t) -> p h t", h=H) for b in range(B)]
        KS1 = [KS[:, b, :].rearrange("p (h t) -> p h t", h=H) for b in range(B)]
        MAPS = 0.5 ** 0.5 * 0.5
        QSCALE = float(1.0 / np.sqrt(np.sqrt(np.float64(HD))))

        block = ctx.enter_context(nc.Block())
        tile = lambda t: slice(t * P, (t + 1) * P)
        half = lambda s, k: ps[:, 2 * s + k, 0:2 * WA]
        two_heads = lambda ap, k: ap[:, 2 * k:2 * k + 2, :].rearrange("p h w -> p (h w)")
        parts_out = lambda n, layer: 16 * (PARTS if n % 2 == 0 else WINDOW) * (layer + 1)
        stack_in = lambda layer: 16 * STACK_DMAS * (layer + 1)
        C1W, C2 = 13.0 / 4, 15.0 / 4

        @block.sync
        def _(sp):
            def load(dst, src, sem):
                sp.dma_start(dst, src).then_inc(sem, 16)

            load(ids[0:1, 0:6], a["ids"], S["ld_ids"])
            load(xT[:], a["xT"].rearrange("b h t -> h b t"), S["ld_in"])
            sp.wait_ge(S["ld_ids"], 16)
            subj = [sp.value_load(ids[0:1, b:b + 1], min_val=0, max_val=7) for b in range(B)]
            prof = [sp.value_load(ids[0:1, 2 + b:3 + b], min_val=0, max_val=7) for b in range(B)]
            lang = [sp.value_load(ids[0:1, 4 + b:5 + b], min_val=0, max_val=9) for b in range(B)]
            one = lambda ap, i: ap[bass.ds(i, 1)]
            for b in range(B):
                load(w0T[:, b, :], one(a["w0T"], subj[b]).rearrange("s h o -> (s h) o"), S["ld_in"])
                load(b0[:, b:b + 1], one(a["b0"], subj[b]).rearrange("s h -> h s"), S["ld_in"])
            load(wqk[:], a["wqkT"].rearrange("n h o -> h n o"), S["ld_qkv"])
            load(wv[:], a["wvT"], S["ld_qkv"])
            load(cos[:], a["cos"], S["ld_qkv"])
            load(sin[:], a["sin"], S["ld_qkv"])
            load(ident[:], a["ident"], S["ld_qkv"])
            load(identb[:].bitcast(U16), a["identb"], S["ld_qkv"])
            for b in range(B):
                load(x[:, b], a["x"][b].rearrange("(n p) f -> p n f", p=P), S["ld_res"])
            load(boutb[:], a["bout"].to_broadcast([P, P]), S["ld_res"])
            load(woutT[:], a["woutT"], S["ld_res"])

            def send_parts(n, dram, split_done):
                sp.wait_ge(split_done, n + 1)
                for i in range(PARTS if n % 2 == 0 else WINDOW):
                    sp.dma_start(dram[n, i].rearrange("d h t -> (d h) t"), parts[:, n, i % PARTS, 0:dram.shape[-1]]
                                 ).then_inc(S["parts_out"][n], 16)

            def fetch_stack(n, dram, layer):
                b, width = n // 2, dram.shape[-1]
                sp.wait_ge(S["parts_out"][n], parts_out(n, layer))
                R = PARTS * HD
                for k in range(PARTS):
                    w = 0 if n % 2 == 0 else k
                    sp.dma_start((QS if n % 2 == 0 else KS)[k * R:(k + 1) * R, b, 0:H * width],
                                 dram[n, w:w + PARTS].rearrange("i d h t -> (i d) (h t)")).then_inc(S["stacks_in"][b], 16)

            sp.wait_ge(S["ones_rows"], 1)
            for n in range(5):
                if n < 4:
                    send_parts(n, parts_dram[0], S["part_c"])
                if n >= 1:
                    fetch_stack(n - 1, parts_dram[0], 0)

            for b in range(B):
                load(wdn[:, b, :], one(a["down"], prof[b]).rearrange("s h o -> (s h) o"), S["ld_c0"])
                load(bdn[:, b:b + 1], one(a["bd"], prof[b]).rearrange("s h -> h s"), S["ld_c0"])
                load(wup[:, b, :], one(a["up"], prof[b]).rearrange("s h o -> (s h) o"), S["ld_c0"])
                for k, n in enumerate(("bu", "ln_g", "ln_b")):
                    load(rows0[:, b, k, :], one(a[n], prof[b]).to_broadcast([P, P]), S["ld_c0"])
            load(hashT[:], a["hashT"], S["ld_f0"])
            load(keysT[:], a["keysT"], S["ld_f0"])
            load(vd[:].rearrange("p (e q) -> p e q", e=E0), a["vd"].rearrange("e d q -> d e q"), S["ld_f0"])
            load(vu[:], a["vu"].rearrange("e q d -> (e q) d").rearrange("(c p) d -> p c d", p=P), S["ld_f0"])
            load(scale[:], a["scale"].to_broadcast([P, 1]), S["ld_f0"])
            load(sel0[:].bitcast(U16), a["sel0"], S["ld_f0"])
            load(sel1[:].bitcast(U16), a["sel1"], S["ld_f0"])

            def neg_rows(g):
                sp.wait_ge(S["neg_split"], g + 1)
                b, h0 = g // NG, g % NG * GH
                for i in range(PARTS):
                    dst = QS0[b][PROD + i:PROD + i + 1, h0:h0 + GH, :].rearrange("p h (n t) -> p (h n) t", t=P)
                    sp.dma_start(dst, negT[0:GH * NT, g % 2, i, :]).then_inc(S["neg_rows"][g % 2], 16)

            for g in range(2):
                neg_rows(g)
            load(w1[:], a["w1"].rearrange("h (c n) -> h c n", c=HC), S["ld_c1"])
            load(b1[:], a["b1"], S["ld_c1"])
            PO = P - 32
            for b in range(B):
                load(w2[:, b, :, 0:PO], a["w2"].rearrange("(c n) o -> n c o", c=HC), S["ld_c1"])
                load(w2[:, b, :, PO:P], one(a["we"], subj[b]).rearrange("s (c n) o -> (s n) c o", c=HC), S["ld_c1"])
                load(b2[0:PO, b:b + 1], a["b2"].rearrange("(o s) -> o s", s=1), S["ld_c1"])
                load(b2[PO:P, b:b + 1], one(a["be"], subj[b]).rearrange("s o -> o s"), S["ld_c1"])
            for g in range(2, G):
                neg_rows(g)
            load(wl1[:], a["wl1T"].rearrange("n h o -> h n o"), S["ld_l1"])
            load(bl1[:], a["bl1"], S["ld_l1"])
            load(bvb[:], a["bv"].to_broadcast([P, P]), S["ld_l1"])
            for b in range(B):
                load(a1[:, b, :], one(a["a1"], lang[b]).rearrange("s h o -> (s h) o"), S["ld_ad"])
                load(ab1[:, b:b + 1], one(a["ab1"], lang[b]).rearrange("s h -> h s"), S["ld_ad"])
                load(a2[:, b, :], one(a["a2"], lang[b]).rearrange("s h o -> (s h) o"), S["ld_ad"])
                for k, n in enumerate(("ab2", "gamma", "beta")):
                    load(rows1[:, b, k, :], one(a[n], lang[b]).to_broadcast([P, P]), S["ld_ad"])
            load(gateT[:], a["gateT"], S["ld_f1"])
            for n in range(5):
                if n < 4:
                    send_parts(n, parts_dram[1], S["l1_parts"])
                if n >= 1:
                    if n % 2 == 1:
                        sp.wait_ge(S["st_ps"], UN * NG * (n // 2 + 1))
                    fetch_stack(n - 1, parts_dram[1], 1)
            load(wg[:].rearrange("p (e i) -> p e i", e=E1), a["wg"].rearrange("e h i -> h e i"), S["ld_f1"])
            load(wu[:].rearrange("p (e i) -> p e i", e=E1), a["wu"].rearrange("e h i -> h e i"), S["ld_f1"])
            load(wd[:], a["wd"].rearrange("e i h -> (e i) h").rearrange("(c p) h -> p c h", p=P), S["ld_f1"])
            load(swg[:], a["swg"], S["ld_f1"])
            load(swu[:], a["swu"], S["ld_f1"])
            load(swd[:], a["swd"], S["ld_f1"])

            for g in range(G):
                sp.wait_ge(S["n_split"], g + 1)
                b, h0 = g // NG, g % NG * GH
                for i in range(PARTS):
                    dst = QS1[b][PROD + i:PROD + i + 1, h0:h0 + GH, :].rearrange("p h (n t) -> p (h n) t", t=P)
                    sp.dma_start(dst, negT[0:20, g % 2, i, :]).then_inc(S["n_rows"][g % 2], 16)

            for b in range(B):
                sp.wait_ge(S["out_ready"], b + 1)
                sp.dma_start(out[b].rearrange("(n p) f -> p n f", p=P), y[:, b]).then_inc(S["stored"], 16)
            sp.wait_ge(S["stored"], 16 * B)
            for n in range(4):
                sp.wait_ge(S["parts_out"][n], parts_out(n, 1))

        @block.tensor
        def _(pe):
            mm = nc.tensor.matmul

            pe.wait_ge(S["ld_in"], 80)
            for b in range(B):
                mm(bank(5 + b), w0T[:, b, :], xT[:, b, :], start=True, stop=True).then_inc(S["y0_ps"], 1)
            pe.wait_ge(S["ld_qkv"], 96)
            for b in range(B):
                pe.wait_ge(S["y0_ready"], b + 1)
                for n in range(4):
                    if 5 * b + n == 8:
                        pe.wait_ge(S["rot_cos"], 2)
                    mm(bank((5 * b + n) % 8), wqk[:, n, :], y0T[:, b, :], start=True, stop=True).then_inc(S["qk_ps"], 1)
                if b == 1:
                    pe.wait_ge(S["rot_cos"], 2)
                for t in range(NT):
                    r = mm(ps[:, (5 * b + 4) % 8, tile(t)], y0T[:, b, tile(t)], wv[:], start=True, stop=True)
                r.then_inc(S["v_ps"], 1)

            def s_max(m):
                g, u = m // UN, m % UN
                b, h = g // NG, g % NG * GH + u // NT
                if u == 0:
                    pe.wait_ge(S["stacks_in"][b], stack_in(0))
                if m == 0:
                    pe.wait_ge(S["rot_cos"], 8)
                    pe.wait_ge(S["vaug_ready"], B)
                if m >= 3:
                    pe.wait_ge(S["smax_done"], m - 2)
                mm(bank(m % 3), QS0[b][0:PROD, h, tile(u % NT)], KS0[b][0:PROD, h, :],
                   start=True, stop=True).then_inc(S["smax_ps"], 1)

            def neg_t(g):
                pe.wait_ge(S["smax_done"], UN * (g + 1))
                if g >= 1:
                    pe.wait_ge(S["neg_copy"], g)
                if g >= 3:
                    pe.wait_ge(S["o_ready"], g - 2)
                nc.tensor.transpose(ps[0:UN, 7, 0:P], negm[:, g % 2, 0:UN], ident[:]).then_inc(S["negT_ps"], 1)

            def scores(n):
                g, kb, j = n // UN, n % UN // GH, n % GH
                b, h = g // NG, g % NG * GH + j
                if n % UN == 0:
                    pe.wait_ge(S["neg_rows"][g % 2], 16 * PARTS * (g // 2 + 1))
                if n >= 3:
                    pe.wait_ge(S["exp_done"], n - 2)
                mm(bank(3 + n % 3), KS0[b][0:KROWS, h, tile(kb)], QS0[b][0:KROWS, h, :],
                   start=True, stop=True).then_inc(S["st_ps"], 1)

            def av(k):
                g, kb = k // NT, k % NT
                b = g // NG
                pe.wait_ge(S["exp_done"], GH * (k + 1))
                if kb == 0 and g >= 1:
                    pe.wait_ge(S["outT_ready"], g)
                for j in range(GH):
                    r = mm(ps[32 * j:32 * j + VW, 6, :], V[:, b, kb, g % NG * GH + j, :],
                           PT[:, kb % 2 * 4 + j, :], start=(kb == 0), stop=(kb == NT - 1))
                r.then_inc(S["av_ps"], 1)

            def out_t(g):
                pe.wait_ge(S["outT_ready"], g + 1)
                pe.wait_ge(S["neg_copy"], min(g + 3, G))
                if g >= 1:
                    pe.wait_ge(S["o_ready"], g)
                for t in range(NT):
                    r = nc.tensor.transpose(ps[:, 7, tile(t)], outT[:, tile(t)], ident[:])
                r.then_inc(S["otr_ps"], 1)

            pe.wait_ge(S["ld_qkv"], 96)
            for m in range(LAG):
                s_max(m)
                if m == UN + 3:
                    neg_t(0)
            for n in range(G * UN + UN):
                g, u = n // UN, n % UN
                if n < G * UN:
                    scores(n)
                if n + LAG < G * UN:
                    s_max(n + LAG)
                if u == 6 and g + 1 < G:
                    neg_t(g + 1)
                if n >= 5 and (n - 5) % GH == 0 and (n - 5) // GH < G * NT:
                    av((n - 5) // GH)
                if u == 8 and 1 <= g:
                    out_t(g - 1)

            def turn(bk, src, done):
                for t in range(NT):
                    r = nc.tensor.transpose(ps[:, bk, tile(t)], src[:, t, :], ident[:])
                r.then_inc(done, 1)

            def token_mm(bk, lhs, rhs, done):
                for t in range(NT):
                    r = mm(ps[:, bk, tile(t)], lhs[:, tile(t)], rhs, start=True, stop=True)
                r.then_inc(done, 1)

            pe.wait_ge(S["o_ready"], G)
            for b in range(B):
                turn(4 * b, O[:, b], S["oT_ps"])
            pe.wait_ge(S["ld_res"], 64)
            for b in range(B):
                pe.wait_ge(S["oT_ready"], b + 1)
                token_mm(4 * b + 1, featT[:, b, :], woutT[:], S["proj_ps"])

            def adapter(ready, t_ps, t_ready, z_ps, z_ready, u_ps, src, wz, wu_, rows, loads):
                for b in range(B):
                    pe.wait_ge(ready, b + 1)
                    turn(4 * b + 2, src[:, b], t_ps)
                pe.wait_ge(*loads)
                for b in range(B):
                    pe.wait_ge(t_ready, b + 1)
                    mm(ps[0:rows, 4 * b + 3, :], wz[:, b, :], featT[:, b, :], start=True, stop=True).then_inc(z_ps, 1)
                for b in range(B):
                    pe.wait_ge(z_ready, b + 1)
                    token_mm(4 * b, zT[0:rows, b, :], wu_[:, b, :], u_ps)

            pe.wait_ge(S["ld_c0"], 192)
            adapter(S["x1_ready"], S["t0_ps"], S["t0_ready"], S["z0_ps"], S["z0_ready"], S["u0_ps"], x1, wdn, wup, P, (S["ld_c0"], 192))

            for b in range(B):
                pe.wait_ge(S["n0_ready"], b + 1)
                turn(4 * b + 1, x2[:, b], S["xn0_ps"])
            pe.wait_ge(S["ld_f0"], 112)
            for b in range(B):
                pe.wait_ge(S["xn0_ready"], b + 1)
                mm(ps[0:PD, 4 * b + 2, :], hashT[:], xnT[:, b, :], start=True, stop=True).then_inc(S["hash_ps"], 1)
            for b in range(B):
                pe.wait_ge(S["hash_ready"], b + 1)
                for t in range(NT):
                    r = mm(ps[:, 4 * b + 3, t * E0:(t + 1) * E0], hT[:, b, tile(t)], keysT[:], start=True, stop=True)
                r.then_inc(S["sim_ps"], 1)
            pe.wait_ge(S["ld_f0"], 112)
            for b in range(B):
                for c in range(C0):
                    n = b * C0 + c
                    if n >= 2:
                        pe.wait_ge(S["silu_ready"], n - 1)
                    if n == 0:
                        pe.wait_ge(S["n0_ready"], B)
                        pe.wait_ge(S["xn0_ready"], B)
                        pe.wait_ge(S["hash_ready"], B)
                    mm(bank(n % 2), vd[:, tile(c)], xnT[:, b, :], start=True, stop=True).then_inc(S["up_proj_ps"], 1)
                    if c == 0:
                        pe.wait_ge(S["cwp_ready"], b + 1)
                        for t in range(NT):
                            r = nc.tensor.transpose(ps[0:PARTS * E0, 4, :].bitcast(BF16)[:, tile(t)],
                                                    cwp[:, b, t].rearrange("p i e -> p (i e)"), identb[:])
                        r.then_inc(S["cwT_ps"], 1)
                        pe.wait_ge(S["cwT_ready"], b + 1)
                    if n == 0:
                        pe.wait_ge(S["cwp_ready"], B)
                    if n >= 2:
                        pe.wait_ge(S["hid_ready"], n - 1)
                    mm(bank(2 + n % 2), sel0[:, c, :], cwT[:, b, :], start=True, stop=True).then_inc(S["sel_ps"], 1)
                if b >= 1:
                    pe.wait_ge(S["x3_ready"], b)
                pe.wait_ge(S["hid_ready"], C0 * (b + 1))
                for t in range(NT):
                    for c in range(C0):
                        r = mm(ps[:, 5, tile(t)], hid[:, c, tile(t)], vu[:, c, :], start=(c == 0), stop=(c == C0 - 1))
                r.then_inc(S["down_ps"], 1)

            for b in range(B):
                pe.wait_ge(S["x3_ready"], b + 1)
                turn(6 + b, x3[:, b], S["x3T_ps"])
            pe.wait_ge(S["ld_c1"], 160)
            for b in range(B):
                pe.wait_ge(S["x3T_ready"], b + 1)
                for c in range(HC):
                    n = b * HC + c
                    if n >= 4:
                        pe.wait_ge(S["h1_ready"], n - 3)
                    mm(bank(n % 4), w1[:, c, :], featT[:, b, :], start=True, stop=True).then_inc(S["h1_ps"], 1)
            for b in range(B):
                pe.wait_ge(S["h1_ready"], HC * (b + 1))
                for c in range(HC):
                    r = mm(bank(4 + b), w2[:, b, c, :], hid[:, HC * b + c, :], start=(c == 0), stop=(c == HC - 1))
                r.then_inc(S["y1_ps"], 1)
            pe.wait_ge(S["ld_l1"], 48)
            for b in range(B):
                pe.wait_ge(S["y1_ready"], b + 1)
                mm(bank(b), wl1[:, 0, :], y1T[:, b, :], start=True, stop=True).then_inc(S["l1q_ps"], 1)
                mm(bank(2 + b), wl1[:, 1, :], y1T[:, b, :], start=True, stop=True).then_inc(S["l1k_ps"], 1)
                token_mm(6 + b, y1T[:, b, :], wl1[:, 2, :], S["l1v_ps"])

            QL = lambda b, h, k: QS1[b][0:k, h, T:LW]
            KL = lambda b, h, k: KS1[b][0:k, h, T:LW]

            def landmark_scores(g):
                b, h0 = g // NG, g % NG * GH
                if g % NG == 0:
                    pe.wait_ge(S["stacks_in"][b], stack_in(1))
                if g == 0:
                    pe.wait_ge(S["l1q_ready"], B)
                    pe.wait_ge(S["l1k_ready"], B)
                    pe.wait_ge(S["v1_ready"], B)
                if g >= 1:
                    pe.wait_ge(S["k2_exp"], GH * g)
                for j in range(GH):
                    r = mm(ps[:, 6, tile(j)], QL(b, h0 + j, PROD), KL(b, h0 + j, PROD), start=True, stop=True)
                r.then_inc(S["k2_ps"], 1)

            def maxima(g, u):
                b, n = g // NG, 2 * GH * g + u
                h = g % NG * GH + u // 2
                if n >= 3:
                    pe.wait_ge(S["m_done"], n - 2)
                if u % 2 == 0:
                    r = mm(bank(RING[n % 3]), QL(b, h, PROD), KS1[b][0:PROD, h, 0:T], start=True, stop=True)
                else:
                    for t in range(NT):
                        r = mm(ps[:, RING[n % 3], tile(t)], QS1[b][0:PROD, h, tile(t)], KL(b, h, PROD),
                               start=True, stop=True)
                r.then_inc(S["m_ps"], 1)

            def turn_maxima(g):
                pe.wait_ge(S["m_done"], 2 * GH * (g + 1))
                if g >= 2:
                    pe.wait_ge(S["y_ready"], g - 1)
                nc.tensor.transpose(ps[0:20, 5, 0:P], negm[:, g % 2, :], ident[:]).then_inc(S["n_ps"], 1)

            def value_scores(g, j):
                b, n = g // NG, GH * g + j
                h = g % NG * GH + j
                if j == 0:
                    pe.wait_ge(S["n_rows"][g % 2], 16 * PARTS * (g // 2 + 1))
                if n >= 2:
                    pe.wait_ge(S["k3_exp"], n - 1)
                for kb in range(NT):
                    r = mm(ps[:, 2 + n % 2, tile(kb)], KS1[b][0:KROWS, h, tile(kb)], QL(b, h, KROWS),
                           start=True, stop=True)
                r.then_inc(S["k3_ps"], 1)

            def landmark_values(g):
                b, h0 = g // NG, g % NG * GH
                if g >= 1:
                    pe.wait_ge(S["yv_sb"], g)
                pe.wait_ge(S["k3_exp"], GH * (g + 1))
                for kb in range(NT):
                    for j in range(GH):
                        r = mm(ps[32 * j:32 * j + VW, 4, 0:P], V[:, b, kb, h0 + j, :],
                               PT[:, g % 2 * 4 + j, tile(kb)], start=(kb == 0), stop=(kb == NT - 1))
                r.then_inc(S["yv_ps"], 1)

            def column_sums(g):
                pe.wait_ge(S["a_ready"], g + 1)
                pe.wait_ge(S["n_copy"], min(g + 2, G))
                if g >= 1:
                    pe.wait_ge(S["y_ready"], g)
                mm(ps[0:32, 5, :], ones[:, 0:32], AY[:, GH * g:GH * g + GH, 0:P], start=True, stop=True).then_inc(S["col_ps"], 1)

            def turn_values(g):
                pe.wait_ge(S["yv_sb"], g + 1)
                pe.wait_ge(S["col_done"], g + 1)
                nc.tensor.transpose(ps[:, 5, 0:P], ysb[:], ident[:]).then_inc(S["ytr_ps"], 1)

            for g in range(2):
                landmark_scores(g)
                for u in range(2 * GH):
                    maxima(g, u)
                    if g == 1 and u == 2:
                        turn_maxima(0)
            for g in range(G):
                ahead = g + 2 < G
                if ahead:
                    landmark_scores(g + 2)
                for u in range(2 * GH):
                    if ahead:
                        maxima(g + 2, u)
                    if u == 2 and g + 1 < G:
                        turn_maxima(g + 1)
                    if u < GH:
                        value_scores(g, u)
                    if u == 4:
                        column_sums(g)
                    if u == 5:
                        landmark_values(g)
                turn_values(g)

            pe.wait_ge(S["rc_ready"], 1)
            mm(ps[:, 7, 0:1], ones[0:1, :], rc[:, 1:2], start=True, stop=True).then_inc(S["rcb_ps"], 1)
            pe.wait_ge(S["y_ready"], G)

            def heads_mm(s, done, lhs, rhs):
                for j in range(GH):
                    r = mm(ps[:, 2 * s + j // 2, j % 2 * WA:(j % 2 + 1) * WA], lhs(j), rhs(j), start=True, stop=True)
                    if j % 2 == 1:
                        r.then_inc(done, 1)

            def k1_scores(g, j):
                b, h, n = g // NG, g % NG * GH + j, GH * g + j
                if n >= 2:
                    pe.wait_ge(S["k1_exp"], n - 1)
                mm(bank(4 + n % 2), KL(b, h, KROWS), QS1[b][0:KROWS, h, 0:T], start=True, stop=True).then_inc(S["k1_ps"], 1)

            def mix(g):
                pe.wait_ge(S["gaug_ready"], g + 1)
                pe.wait_ge(S["k1_exp"], GH * (g + 1))
                if g >= 1:
                    pe.wait_ge(S["xo_sb"], g)
                for j in range(GH):
                    r = mm(ps[32 * j:32 * j + VW, 6, :], Gaug[:, g % 2, j, :], PT[:, g % 2 * 4 + j, :],
                           start=True, stop=True)
                r.then_inc(S["x_ps"], 1)

            def turn_mix(g):
                pe.wait_ge(S["xo_sb"], g + 1)
                if g >= 1:
                    pe.wait_ge(S["xo_ready"], g)
                if g == 0:
                    pe.wait_ge(S["rcb_ready"], 1)
                for t in range(NT):
                    r = nc.tensor.transpose(ps[:, 7, tile(t)], outT[:, tile(t)], ident[:])
                r.then_inc(S["xtr_ps"], 1)

            for q in range(G // 2):
                for s in range(2):
                    g = 2 * q + s
                    if g >= 2:
                        pe.wait_ge(S["wn_ready"], 2 * ((q - 1) * 2 * ITERS + (ITERS - 1) * 2 + s + 1))
                    heads_mm(s, S["sq_ps"], lambda j: AY[:, GH * g + j, 0:P], lambda j: AY[:, GH * g + j, :])
                units = [(2 * q + k // GH, k % GH) for k in range(2 * GH)]
                for it in range(ITERS):
                    for s in range(2):
                        n = (q * ITERS + it) * 2 + s
                        W = Wb[:, 2 * s + it % 2]
                        for k in range(2):
                            if it == 0:
                                pe.wait_ge(S["w_ready"], 2 * (2 * q + s) + k + 1)
                            else:
                                pe.wait_ge(S["wn_ready"], 2 * (n - 2) + k + 1)
                            for j in (2 * k, 2 * k + 1):
                                r = mm(ps[:, 2 * s + k, j % 2 * WA:(j % 2 + 1) * WA], W[:, j, 0:P], W[:, j, :],
                                       start=True, stop=True)
                            r.then_inc(S["mm1_ps"], 1)
                    if it == 0 and q >= 1:
                        mix(2 * q - 2)
                    if it >= 1 and units:
                        k1_scores(*units.pop(0))
                    for s in range(2):
                        n = (q * ITERS + it) * 2 + s
                        for k in range(2):
                            pe.wait_ge(S["d_ready"], 2 * n + k + 1)
                            for j in (2 * k, 2 * k + 1):
                                r = mm(ps[:, 2 * s + k, j % 2 * WA:(j % 2 + 1) * WA], W2[:, s, j, 0:P], Db[:, s, j, :],
                                       start=True, stop=True)
                            r.then_inc(S["mm2_ps"], 1)
                    if it == 0 and q >= 1:
                        turn_mix(2 * q - 2)
                        mix(2 * q - 1)
                        turn_mix(2 * q - 1)
                    elif units:
                        k1_scores(*units.pop(0))
                        if it >= 4 and units:
                            k1_scores(*units.pop(0))
            for g in (G - 2, G - 1):
                mix(g)
                turn_mix(g)

            pe.wait_ge(S["ld_ad"], 192)
            adapter(S["x4_ready"], S["t1_ps"], S["t1_ready"], S["z1_ps"], S["z1_ready"], S["u1_ps"], x4, a1, a2, AD, (S["ld_ad"], 192))
            for b in range(B):
                pe.wait_ge(S["n1_ready"], b + 1)
                turn(4 * b + 1, x2[:, b], S["xn1_ps"])
            pe.wait_ge(S["ld_f1"], 112)
            for b in range(B):
                pe.wait_ge(S["xn1_ready"], b + 1)
                for t in range(NT):
                    r = mm(ps[:, 4 * b + 2, t * E1:(t + 1) * E1], xnT[:, b, tile(t)], gateT[:], start=True, stop=True)
                r.then_inc(S["gate_ps"], 1)
            pe.wait_ge(S["ld_f1"], 112)
            pe.wait_ge(S["ld_f0"], 112)
            pe.wait_ge(S["cw1_ready"], B)
            for b in range(B):
                for t in range(NT):
                    if t == 0 and b >= 1:
                        pe.wait_ge(S["cw1T_ready"], b)
                    r = nc.tensor.transpose(ps[0:PARTS * E1, 4, :].bitcast(BF16)[:, tile(t)],
                                            cwp1[:, b, t].rearrange("p i e -> p (i e)"), identb[:])
                r.then_inc(S["cw1T_ps"], 1)
                for c in range(C1 + 1):
                    n = b * (C1 + 1) + c
                    rows = P if c < C1 else I1
                    if n >= 2:
                        pe.wait_ge(S["gelu_ready"], n - 1)
                        pe.wait_ge(S["gu_ready"], n - 1)
                    mm(ps[0:rows, n % 2, :], wg[:, tile(c)] if c < C1 else swg[:], xnT[:, b, :],
                       start=True, stop=True).then_inc(S["g_ps"], 1)
                    mm(ps[0:rows, 2 + n % 2, :], wu[:, tile(c)] if c < C1 else swu[:], xnT[:, b, :],
                       start=True, stop=True).then_inc(S["uu_ps"], 1)
                    if c < C1:
                        m = b * C1 + c
                        if c == 0:
                            pe.wait_ge(S["cw1T_ready"], b + 1)
                        if m >= 2:
                            pe.wait_ge(S["hid1_ready"], m - 1 + (1 if m - 2 >= C1 else 0))
                        mm(bank(5 + m % 2), sel1[:, c, :], cwT[0:PARTS * E1, b, :], start=True, stop=True).then_inc(S["cs_ps"], 1)
                pe.wait_ge(S["hid1_ready"], (C1 + 1) * (b + 1))
                if b >= 1:
                    pe.wait_ge(S["out_ready"], b)
                for t in range(NT):
                    for c in range(C1 + 1):
                        rows = P if c < C1 else I1
                        r = mm(ps[:, 7, tile(t)], hid[0:rows, c, tile(t)], wd[:, c, :] if c < C1 else swd[:],
                               start=(c == 0), stop=(c == C1))
                r.then_inc(S["fin_ps"], 1)

        @block.vector
        def _(dve):
            v = nc.vector
            steps = [0]

            def step(ins):
                steps[0] += 1
                ins.then_inc(S["step_dve"], 1)
                dve.wait_ge(S["step_dve"], steps[0])

            v.memset(ones[:], 1.0).then_inc(S["const_ready"], 1)
            v.memset(V[:], 1.0).then_inc(S["const_ready"], 1)
            dve.wait_ge(S["ld_in"], 80)
            for b in range(B):
                dve.wait_ge(S["y0_ps"], b + 1)
                v.tensor_scalar(y0T[:, b, :], bank(5 + b), b0[:, b:b + 1], None, ALU.add).then_inc(S["y0_ready"], 1)
            dve.wait_ge(S["ld_qkv"], 96)

            def split(part_sem, res_sem, n, width):
                dve.wait_ge(S["part_a"], part_sem + n + 1)
                v.tensor_tensor(res[:, n % 2, 0:width], qk[:, n % 2, 0:width], parts[:, n, 0, 0:width],
                                ALU.subtract).then_inc(S["res_a"], 1)
                dve.wait_ge(S["part_b"], part_sem + n + 1)
                return v.tensor_tensor(parts[:, n, 2, 0:width], res[:, n % 2, 0:width], parts[:, n, 1, 0:width],
                                       ALU.subtract)

            for n in range(4):
                b = n // 2
                dve.wait_ge(S["qk_ps"], 2 * n + 2)
                bk = [(5 * b + 2 * (n % 2) + k) % 8 for k in range(2)]
                if n >= 2:
                    dve.wait_ge(S["part_c"], n - 1)
                v.tensor_tensor(rot[:, 0, :], bank(bk[0]), cos[:], ALU.mult).then_inc(S["rot_cos"], 1)
                v.tensor_tensor(rot[:, 1, :], bank(bk[1]), sin[:], ALU.mult).then_inc(S["rot_cos"], 1)
                dve.wait_ge(S["rot_cos"], 2 * n + 2)
                v.tensor_tensor(qk[:, n % 2, 0:T], rot[:, 0, :], rot[:, 1, :], ALU.add).then_inc(S["rot_done"], 1)
                if n >= 1:
                    split(0, 0, n - 1, T).then_inc(S["part_c"], 1)
                dve.wait_ge(S["rot_done"], n + 1)
            split(0, 0, 3, T).then_inc(S["part_c"], 1)
            dve.wait_ge(S["const_ready"], 2)
            for b in range(B):
                dve.wait_ge(S["v_ps"], b + 1)
                v.tensor_copy(V[:, b, :, :, 0:HD],
                              ps[:, (5 * b + 4) % 8, :].rearrange("p (n h d) -> p n h d", n=NT, h=H)).then_inc(S["vaug_ready"], 1)

            def s_max(m):
                g, u = m // UN, m % UN
                dve.wait_ge(S["smax_ps"], m + 1)
                if u == 0 and g >= 2:
                    dve.wait_ge(S["negT_ps"], g - 1)
                v.tensor_reduce(negm[:, g % 2, u:u + 1], bank(m % 3), AX.X, ALU.max, negate=True).then_inc(S["smax_done"], 1)

            def neg_copy(g):
                dve.wait_ge(S["negT_ps"], g + 1)
                if g >= 2:
                    dve.wait_ge(S["neg_split"], g - 1)
                v.tensor_copy(negR[0:UN, g % 2, :], ps[0:UN, 7, 0:P]).then_inc(S["neg_copy"], 1)

            def normalise(src, dst, ready, done):
                step(v.reciprocal(rden[:], src[:, :, :, HD]))
                v.tensor_tensor(dst, src[:, :, :, 0:HD],
                                rden[:].rearrange("p n (h o) -> p n h o", o=1).to_broadcast([P, NT, GH, HD]),
                                ALU.mult).then_inc(done, 1)

            heads4 = lambda k: ps[:, k, :].rearrange("p (n h d) -> p n h d", n=NT, h=GH)

            def outputs(g, tr, k, dst, done):
                dve.wait_ge(tr, g + 1)
                if g >= 1:
                    dve.wait_ge(done, g)
                b, gg = g // NG, g % NG
                normalise(heads4(k), dst[:, b, :, gg * 32:gg * 32 + 32].rearrange("p n (h d) -> p n h d", d=HD), None, done)

            for m in range(LAG):
                s_max(m)
                if m == UN + 4:
                    neg_copy(0)
            for n in range(G * UN + UN):
                g, u = n // UN, n % UN
                if n + LAG < G * UN:
                    s_max(n + LAG)
                if u == 7 and g + 1 < G:
                    neg_copy(g + 1)
                if u == 9 and g >= 1:
                    outputs(g - 1, S["otr_ps"], 7, O, S["o_ready"])

            dve.wait_ge(S["xbias_ready"], B)
            for b in range(B):
                dve.wait_ge(S["proj_ps"], b + 1)
                v.tensor_tensor(x1[:, b].rearrange("p n f -> p (n f)"), bank(4 * b + 1),
                                x[:, b].rearrange("p n f -> p (n f)"), ALU.add).then_inc(S["x1_ready"], 1)

            def norm(u_ps, base_ready, rows, done, first):
                for b in range(B):
                    dve.wait_ge(u_ps, b + 1)
                    dve.wait_ge(base_ready, b + 1)
                    yb = y[:, b].rearrange("p n f -> p (n f)")
                    step(v.tensor_tensor(yb, bank(4 * b), base[:, b].rearrange("p n f -> p (n f)"), ALU.add))
                    for t in range(NT):
                        r = v.bn_stats(stats[:, b, t, :], y[:, b, t, :])
                    step(r)
                    for t in range(NT):
                        r = v.bn_aggr(mv[:, b, t, :], stats[:, b, t, :])
                    step(r)
                    step(v.tensor_scalar(veps[:, b, :], mv[:, b, :, 1], EPS, None, ALU.add))
                    v.reciprocal(rinv[:, b, :], veps[:, b, :]).then_inc(S["mv_ready"], 1)
                    dve.wait_ge(S["rstd_ready"], first + b + 1)
                    step(v.tensor_tensor(rinv[:, b, :], root[:, b, :], root[:, b, :], ALU.mult))
                    step(v.tensor_tensor(rinv[:, b, :], rinv[:, b, :], veps[:, b, :], ALU.mult))
                    step(v.tensor_scalar(rinv[:, b, :], rinv[:, b, :], -0.5, 1.5, ALU.mult, ALU.add))
                    step(v.tensor_tensor(rstd[:, b, :], rinv[:, b, :], root[:, b, :], ALU.mult))
                    for t in range(NT):
                        r = v.tensor_scalar(x2[:, b, t, :], y[:, b, t, :], mv[:, b, t, 0:1], rstd[:, b, t:t + 1],
                                            ALU.subtract, ALU.mult)
                    step(r)
                    row = lambda k: rows[:, b, k:k + 1, :].to_broadcast([P, NT, P])
                    step(v.tensor_tensor(y[:, b], x2[:, b], row(1), ALU.mult))
                    v.tensor_tensor(x2[:, b], y[:, b], row(2), ALU.add).then_inc(done, 1)

            dve.wait_ge(S["ld_c0"], 192)
            norm(S["u0_ps"], S["base0_ready"], rows0, S["n0_ready"], 0)

            def to3(src, w, parts_out, tmp, done):
                step(v.tensor_copy(parts_out[:, :, 0, :], src))
                step(v.tensor_tensor(tmp, src, parts_out[:, :, 0, :], ALU.subtract))
                step(v.tensor_copy(parts_out[:, :, 1, :], tmp))
                v.tensor_tensor(parts_out[:, :, 2, :], tmp, parts_out[:, :, 1, :], ALU.subtract).then_inc(done, 1)

            def col(ap, n):
                return ap.rearrange("p (n o) -> p n o", o=1).to_broadcast([P, NT, n])

            for b in range(B):
                step(v.memset(sim[:, b, :, E0:E0 + 8], LOW))
                step(v.memset(pick[:, b], LOW))
            for b in range(B):
                dve.wait_ge(S["sim_ps"], b + 1)
                step(v.tensor_copy(sim[:, b, :, 0:E0], ps[:, 4 * b + 3, 0:NT * E0].rearrange("p (n e) -> p n e", n=NT)))
                for t in range(NT):
                    r = v.max(best[:, b, t, :], sim[:, b, t, :])
                step(r)
                step(v.tensor_copy(pick[:, b, :, 0:TOP0], best[:, b, :, 0:TOP0]))
                for t in range(NT):
                    r = v.match_replace(took[:, b, t, :], pick[:, b, t, :], sim[:, b, t, :], HIGH)
                step(r)
                v.tensor_tensor(ex[:, b], sim[:, b, :, 0:E0], best[:, b, :, 0:1].to_broadcast([P, NT, E0]),
                                ALU.subtract).then_inc(S["sc_sub"], 1)
                step(v.tensor_tensor(took[:, b, :, 0:E0], took[:, b, :, 0:E0], sim[:, b, :, 0:E0], ALU.not_equal))
                dve.wait_ge(S["sc_exp"], b + 1)
                step(v.tensor_tensor(ex[:, b], ex2[:, b], took[:, b, :, 0:E0], ALU.mult))
                step(v.tensor_reduce(tot[:, b, :], ex[:, b], AX.X, ALU.add))
                step(v.reciprocal(totr[:, b, :], tot[:, b, :]))
                step(v.tensor_tensor(cw[:, b], ex[:, b], col(totr[:, b, :], E0), ALU.mult))
                to3(cw[:, b], E0, cwp[:, b], cwr[:, b], S["cwp_ready"])
            for b in range(B):
                dve.wait_ge(S["cwT_ps"], b + 1)
                v.tensor_copy(cwT[:, b, :], ps[0:PARTS * E0, 4, :].bitcast(BF16)[:, 0:T]).then_inc(S["cwT_ready"], 1)
                for c in range(C0):
                    n = b * C0 + c
                    if b == 1 and c == 0:
                        dve.wait_ge(S["down_ps"], 1)
                    dve.wait_ge(S["silu_ready"], n + 1)
                    dve.wait_ge(S["sel_ps"], n + 1)
                    v.tensor_tensor(hid[:, c, :], act_sb[:, n % 2, :], bank(2 + n % 2), ALU.mult).then_inc(S["hid_ready"], 1)
                if b == 0:
                    dve.wait_ge(S["ld_f0"], 112)
                dve.wait_ge(S["x12_ready"], b + 1)
                dve.wait_ge(S["down_ps"], b + 1)
                v.scalar_tensor_tensor(out=x3[:, b].rearrange("p n f -> p (n f)"), in0=bank(5), scalar=scale[:, 0:1],
                                       in1=base[:, b].rearrange("p n f -> p (n f)"), op0=ALU.mult,
                                       op1=ALU.add).then_inc(S["x3_ready"], 1)

            dve.wait_ge(S["ld_c1"], 160)
            for b in range(B):
                dve.wait_ge(S["y1_ps"], b + 1)
                v.tensor_scalar(y1T[:, b, :], bank(4 + b), b2[:, b:b + 1], None, ALU.add).then_inc(S["y1_ready"], 1)
            dve.wait_ge(S["ld_l1"], 48)
            v.tensor_scalar(bl1s[:], bl1[:], QSCALE, None, ALU.mult).then_inc(S["bl1_ready"], 1)
            for n in range(4):
                b, k = n // 2, n % 2
                if n >= 2:
                    dve.wait_ge(S["l1_parts"], n - 1)
                dve.wait_ge((S["l1q_ready"], S["l1k_ready"])[k], b + 1)
                step(v.tensor_reduce(res[:, k, 0:LM], qk[:, k, 0:T].rearrange("p (m s) -> p m s", s=SEG), AX.X, ALU.add))
                v.tensor_scalar(qk[:, k, T:LW], res[:, k, 0:LM], 1.0 / SEG, None, ALU.mult).then_inc(S["lm_ready"], 1)
                dve.wait_ge(S["lm_ready"], n + 1)
                split(4, 4, n, LW).then_inc(S["l1_parts"], 1)
            for b in range(B):
                dve.wait_ge(S["l1v_ps"], b + 1)
                v.tensor_tensor(V[:, b, :, :, 0:HD], ps[:, 6 + b, :].rearrange("p (n h d) -> p n h d", n=NT, h=H),
                                bvb[:].rearrange("p (o h d) -> p o h d", o=1, h=H).to_broadcast([P, NT, H, HD]),
                                ALU.add).then_inc(S["v1_ready"], 1)

            def landmark_max(g):
                dve.wait_ge(S["k2_ps"], g + 1)
                if g >= 1:
                    dve.wait_ge(S["k2_exp"], GH * g)
                v.tensor_reduce(neg2[:], ps[:, 6, :].rearrange("p (h m) -> p h m", h=GH), AX.X, ALU.max,
                                negate=True).then_inc(S["k2_max"], 1)

            def maxima(g, u):
                n = 2 * GH * g + u
                dve.wait_ge(S["m_ps"], n + 1)
                if u == 0 and g >= 2:
                    dve.wait_ge(S["n_ps"], g - 1)
                c = u // 2 * 5
                src = bank(RING[n % 3])
                if u % 2 == 0:
                    r = v.tensor_reduce(negm[:, g % 2, c + 4:c + 5], src, AX.X, ALU.max, negate=True)
                else:
                    r = v.tensor_reduce(negm[:, g % 2, c:c + 4], src.rearrange("p (n m) -> p n m", n=NT),
                                        AX.X, ALU.max, negate=True)
                r.then_inc(S["m_done"], 1)

            def max_copy(g):
                dve.wait_ge(S["n_ps"], g + 1)
                if g >= 2:
                    dve.wait_ge(S["n_split"], g - 1)
                v.tensor_copy(negR[0:20, g % 2, :], ps[0:20, 5, 0:P]).then_inc(S["n_copy"], 1)

            def landmark_sums(g):
                dve.wait_ge(S["k2_exp"], GH * (g + 1))
                if g >= 1:
                    dve.wait_ge(S["a_ready"], g)
                v.reciprocal(rsum[:], sums[:]).then_inc(S["rs_ready"], 1)

            def column_max(g):
                dve.wait_ge(S["col_ps"], g + 1)
                v.tensor_reduce(cmax[:, g:g + 1], ps[0:1, 5, :], AX.X, ALU.max).then_inc(S["col_done"], 1)

            def values(g):
                dve.wait_ge(S["ytr_ps"], g + 1)
                src = ps[:, 5, 0:P].rearrange("p (h d) -> p h d", h=GH)
                if g >= 1:
                    dve.wait_ge(S["y_ready"], g)
                step(v.reciprocal(rden[:, 0, :], src[:, :, HD]))
                v.tensor_tensor(AY[:, GH * g:GH * g + GH, P:WA], src[:, :, 0:HD],
                                rden[:, 0, :].rearrange("p (h o) -> p h o", o=1).to_broadcast([P, GH, HD]),
                                ALU.mult).then_inc(S["y_ready"], 1)

            for g in range(2):
                landmark_max(g)
                for u in range(2 * GH):
                    maxima(g, u)
                    if g == 1 and u == 3:
                        max_copy(0)
                    if u == 4:
                        landmark_sums(g)
            for g in range(G):
                ahead = g + 2 < G
                if ahead:
                    landmark_max(g + 2)
                for u in range(2 * GH):
                    if ahead:
                        maxima(g + 2, u)
                    if u == 3 and g + 1 < G:
                        max_copy(g + 1)
                    if u == 4 and ahead:
                        landmark_sums(g + 2)
                    if u == 5:
                        column_max(g)
                values(g)

            dve.wait_ge(S["col_done"], G)
            step(v.tensor_reduce(rc[:, 0:1], cmax[:], AX.X, ALU.max))
            v.reciprocal(rc[:, 1:2], rc[:, 0:1]).then_inc(S["rc_ready"], 1)
            dve.wait_ge(S["rcb_ps"], 1)
            v.tensor_copy(rcb[:], ps[:, 7, 0:1]).then_inc(S["rcb_ready"], 1)
            v.memset(Gaug[:], 1.0).then_inc(S["gaug_ones"], 1)

            dve.wait_ge(S["gaug_ones"], 1)
            for q in range(G // 2):
                for it in range(ITERS):
                    for s in range(2):
                        n = (q * ITERS + it) * 2 + s
                        W = Wb[:, 2 * s + it % 2]
                        for k in range(2):
                            dve.wait_ge(S["w2_ready"], 2 * n + k + 1)
                            v.scalar_tensor_tensor(out=two_heads(Db[:, s], k), in0=two_heads(W, k), scalar=7 * C2,
                                                   in1=two_heads(W2[:, s], k), op0=ALU.mult,
                                                   op1=ALU.subtract).then_inc(S["d_ready"], 1)
                    for s in range(2):
                        n = (q * ITERS + it) * 2 + s
                        dve.wait_ge(S["f_ready"], n + 1)
                        for k in range(2):
                            dve.wait_ge(S["mm2_ps"], 2 * n + k + 1)
                            v.scalar_tensor_tensor(out=two_heads(Wb[:, 2 * s + (it + 1) % 2], k), in0=half(s, k),
                                                   scalar=0.25 / (C2 * C2), in1=two_heads(Fb[:, s], k), op0=ALU.mult,
                                                   op1=ALU.add).then_inc(S["wn_ready"], 1)
                    if it == 0 and q >= 1:
                        for s in range(2):
                            outputs(2 * q - 2 + s, S["xtr_ps"], 7, O, S["xo_ready"])
                for s in range(2):
                    g = 2 * q + s
                    dve.wait_ge(S["wn_ready"], 2 * ((q * ITERS + ITERS - 1) * 2 + s + 1))
                    if g >= 2:
                        dve.wait_ge(S["x_ps"], g - 1)
                    v.tensor_copy(Gaug[:, s, :, 0:HD], Wb[:, 2 * s + ITERS % 2, :, P:WA]).then_inc(S["gaug_ready"], 1)
            for g in (G - 2, G - 1):
                outputs(g, S["xtr_ps"], 7, O, S["xo_ready"])
            for b in range(B):
                dve.wait_ge(S["xo_ready"], NG * (b + 1))
                v.tensor_tensor(x4[:, b], O[:, b], x3[:, b], ALU.add).then_inc(S["x4_ready"], 1)

            dve.wait_ge(S["ld_ad"], 192)
            norm(S["u1_ps"], S["base1_ready"], rows1, S["n1_ready"], B)

            for b in range(B):
                step(v.memset(sim1[:, b, :, E1:16], LOW))
                step(v.memset(pick[:, b], LOW))
            for b in range(B):
                dve.wait_ge(S["gate_ps"], b + 1)
                lg = ps[:, 4 * b + 2, 0:NT * E1].rearrange("p (n e) -> p n e", n=NT)
                step(v.tensor_reduce(tot[:, b, :], lg, AX.X, ALU.max))
                v.tensor_tensor(ex[:, b, :, 0:E1], lg, col(tot[:, b, :], E1), ALU.subtract).then_inc(S["sc_sub"], 1)
                dve.wait_ge(S["sc_exp"], B + b + 1)
                step(v.tensor_reduce(tot[:, b, :], ex2[:, b, :, 0:E1], AX.X, ALU.add))
                step(v.reciprocal(totr[:, b, :], tot[:, b, :]))
                step(v.tensor_tensor(sim1[:, b, :, 0:E1], ex2[:, b, :, 0:E1], col(totr[:, b, :], E1), ALU.mult))
                for t in range(NT):
                    r = v.max(best[:, b, t, :], sim1[:, b, t, :])
                step(r)
                step(v.tensor_copy(pick[:, b, :, 0:TOP1], best[:, b, :, 0:TOP1]))
                for t in range(NT):
                    r = v.match_replace(took1[:, b, t, :], pick[:, b, t, :], sim1[:, b, t, :], HIGH)
                step(r)
                step(v.tensor_tensor(ex[:, b, :, 0:E1], took1[:, b, :, 0:E1], sim1[:, b, :, 0:E1], ALU.not_equal))
                step(v.tensor_reduce(tot[:, b, :], best[:, b, :, 0:TOP1], AX.X, ALU.add))
                step(v.tensor_scalar(tot[:, b, :], tot[:, b, :], 1e-20, None, ALU.add))
                step(v.reciprocal(totr[:, b, :], tot[:, b, :]))
                step(v.tensor_tensor(ex2[:, b, :, 0:E1], ex[:, b, :, 0:E1], sim1[:, b, :, 0:E1], ALU.mult))
                step(v.tensor_tensor(cw[:, b, :, 0:E1], ex2[:, b, :, 0:E1], col(totr[:, b, :], E1), ALU.mult))
                to3(cw[:, b, :, 0:E1], E1, cwp1[:, b], cwr[:, b, :, 0:E1], S["cw1_ready"])
            for b in range(B):
                dve.wait_ge(S["cw1T_ps"], b + 1)
                v.tensor_copy(cwT[0:PARTS * E1, b, :], ps[0:PARTS * E1, 4, :].bitcast(BF16)[:, 0:T]).then_inc(S["cw1T_ready"], 1)
                for c in range(C1 + 1):
                    n = b * (C1 + 1) + c
                    rows = P if c < C1 else I1
                    if b == 1 and c == 0:
                        dve.wait_ge(S["fin_ps"], 1)
                    dve.wait_ge(S["gelu_ready"], n + 1)
                    dve.wait_ge(S["uu_ps"], n + 1)
                    if c < C1:
                        if n >= 2:
                            dve.wait_ge(S["hid1_ready"], n - 1)
                        v.tensor_tensor(gu_sb[:, n % 2, :], act_sb[:, n % 2, :], bank(2 + n % 2), ALU.mult).then_inc(S["gu_ready"], 1)
                        m = b * C1 + c
                        dve.wait_ge(S["gu_ready"], n + 1)
                        dve.wait_ge(S["cs_ps"], m + 1)
                        v.tensor_tensor(hid[:, c, :], gu_sb[:, n % 2, :], bank(5 + m % 2), ALU.mult).then_inc(S["hid1_ready"], 1)
                    else:
                        v.tensor_tensor(hid[0:rows, c, :], act_sb[0:rows, n % 2, :], ps[0:rows, 2 + n % 2, :],
                                        ALU.mult).then_inc(S["hid1_ready"], 1)
                        dve.wait_ge(S["hid1_ready"], n + 1)
                        v.memset(gu_sb[0:1, n % 2, 0:1], 0.0).then_inc(S["gu_ready"], 1)
                dve.wait_ge(S["fin_ps"], b + 1)
                v.tensor_tensor(y[:, b].rearrange("p n f -> p (n f)"), bank(7),
                                x4[:, b].rearrange("p n f -> p (n f)"), ALU.add).then_inc(S["out_ready"], 1)

        @block.scalar
        def _(act):
            f = nc.scalar.activation

            def split(base_n, ready, n, width):
                act.wait_ge(*ready)
                f(parts[:, n, 0, 0:width], qk[:, n % 2, 0:width], ACT.Copy).then_inc(S["part_a"], 1)
                act.wait_ge(S["res_a"], base_n + n + 1)
                f(parts[:, n, 1, 0:width], res[:, n % 2, 0:width], ACT.Copy).then_inc(S["part_b"], 1)

            for n in range(4):
                split(0, (S["rot_done"], n + 1), n, T)

            for n in range(G * UN + UN):
                g, k, u = n // UN, n // GH, n % UN
                if n < G * UN:
                    act.wait_ge(S["st_ps"], n + 1)
                    if k >= 2:
                        act.wait_ge(S["av_ps"], k - 1)
                    f(PT[:, k % 2 * 4 + n % GH, :], bank(3 + n % 3), ACT.Exp, scale=MAPS).then_inc(S["exp_done"], 1)
                if u == 2 and g >= 1:
                    act.wait_ge(S["av_ps"], NT * g)
                    if g >= 2:
                        act.wait_ge(S["otr_ps"], g - 1)
                    f(outT[:], bank(6), ACT.Copy).then_inc(S["outT_ready"], 1)

            for b in range(B):
                act.wait_ge(S["oT_ps"], b + 1)
                f(featT[:, b, :], bank(4 * b), ACT.Copy).then_inc(S["oT_ready"], 1)

            def adapter(t_ps, t_ready, z_ps, z_ready, rows, bias, last):
                for b in range(B):
                    act.wait_ge(t_ps, b + 1)
                    act.wait_ge(*last[b])
                    f(featT[:, b, :], bank(4 * b + 2), ACT.Copy).then_inc(t_ready, 1)
                for b in range(B):
                    act.wait_ge(z_ps, b + 1)
                    f(zT[0:rows, b, :], ps[0:rows, 4 * b + 3, :], ACT.Relu, bias=bias[:, b:b + 1]).then_inc(z_ready, 1)

            def roots(first):
                for b in range(B):
                    act.wait_ge(S["mv_ready"], first + b + 1)
                    f(root[:, b, :], rinv[:, b, :], ACT.Sqrt).then_inc(S["rstd_ready"], 1)

            act.wait_ge(S["ld_c0"], 192)
            adapter(S["t0_ps"], S["t0_ready"], S["z0_ps"], S["z0_ready"], P, bdn, [(S["proj_ps"], 1), (S["proj_ps"], 2)])
            roots(0)
            for b in range(B):
                act.wait_ge(S["xn0_ps"], b + 1)
                f(xnT[:, b, :], bank(4 * b + 1), ACT.Copy).then_inc(S["xn0_ready"], 1)
            for b in range(B):
                act.wait_ge(S["hash_ps"], b + 1)
                f(hT[:, b, :], ps[0:PD, 4 * b + 2, :], ACT.Copy).then_inc(S["hash_ready"], 1)
            for b in range(B):
                act.wait_ge(S["sc_sub"], b + 1)
                f(ex2[:, b], ex[:, b], ACT.Exp).then_inc(S["sc_exp"], 1)
            for n in range(B * C0):
                act.wait_ge(S["up_proj_ps"], n + 1)
                if n >= 2:
                    act.wait_ge(S["hid_ready"], n - 1)
                f(act_sb[:, n % 2, :], bank(n % 2), ACT.Silu).then_inc(S["silu_ready"], 1)
            for b in range(B):
                act.wait_ge(S["x3T_ps"], b + 1)
                f(featT[:, b, :], bank(6 + b), ACT.Copy).then_inc(S["x3T_ready"], 1)
            act.wait_ge(S["ld_c1"], 160)
            act.wait_ge(S["down_ps"], B)
            for n in range(B * HC):
                act.wait_ge(S["h1_ps"], n + 1)
                f(hid[:, n, :], bank(n % 4), ACT.Gelu, bias=b1[:, n % HC:n % HC + 1]).then_inc(S["h1_ready"], 1)
            for k in range(4):
                act.wait_ge(S["parts_out"][k], parts_out(k, 0))
            act.wait_ge(S["bl1_ready"], 1)
            act.wait_ge(S["y1_ps"], B)

            def project(n):
                b, k = n // 2, n % 2
                act.wait_ge((S["l1q_ps"], S["l1k_ps"])[k], b + 1)
                if n >= 2:
                    act.wait_ge(S["l1_parts"], n - 1)
                f(qk[:, k, 0:T], bank(2 * k + b), ACT.Identity, bias=bl1s[:, k:k + 1],
                  scale=QSCALE).then_inc((S["l1q_ready"], S["l1k_ready"])[k], 1)

            project(0)
            project(1)
            for n in range(4):
                split(4, (S["lm_ready"], n + 1), n, LW)
                if n + 2 < 4:
                    project(n + 2)

            def landmark_exp(g):
                act.wait_ge(S["k2_max"], g + 1)
                if g >= 1:
                    act.wait_ge(S["a_ready"], g)
                for j in range(GH):
                    f(ek2[:, j, :], ps[:, 6, tile(j)], ACT.Exp, bias=neg2[:, j:j + 1],
                      accum_out=sums[:, j:j + 1]).then_inc(S["k2_exp"], 1)

            def value_exp(g):
                for j in range(GH):
                    n = GH * g + j
                    act.wait_ge(S["k3_ps"], n + 1)
                    if g >= 2:
                        act.wait_ge(S["yv_ps"], g - 1)
                    if g < 2:
                        act.wait_ge(S["y1_ps"], B)
                    f(PT[:, g % 2 * 4 + j, :], bank(2 + n % 2), ACT.Exp).then_inc(S["k3_exp"], 1)
                act.wait_ge(S["yv_ps"], g + 1)
                if g >= 1:
                    act.wait_ge(S["ytr_ps"], g)
                f(ysb[:], ps[:, 4, 0:P], ACT.Copy).then_inc(S["yv_sb"], 1)

            landmark_exp(0)
            landmark_exp(1)
            for g in range(G):
                if g + 2 < G:
                    landmark_exp(g + 2)
                value_exp(g)

            act.wait_ge(S["rcb_ready"], 1)
            def k1_exp(g, j):
                n = GH * g + j
                act.wait_ge(S["k1_ps"], n + 1)
                if g >= 2:
                    act.wait_ge(S["x_ps"], g - 1)
                if g < 2:
                    act.wait_ge(S["yv_ps"], G)
                f(PT[:, g % 2 * 4 + j, :], bank(4 + n % 2), ACT.Exp).then_inc(S["k1_exp"], 1)

            def copy_mix(g):
                act.wait_ge(S["x_ps"], g + 1)
                if g >= 1:
                    act.wait_ge(S["xtr_ps"], g)
                f(outT[:], bank(6), ACT.Copy).then_inc(S["xo_sb"], 1)

            for q in range(G // 2):
                for s in range(2):
                    g = 2 * q + s
                    if g >= 2:
                        act.wait_ge(S["gaug_ready"], g - 1)
                    for k in range(2):
                        act.wait_ge(S["sq_ps"], 2 * g + k + 1)
                        f(two_heads(Wb[:, 2 * s], k), half(s, k), ACT.Copy, scale=rcb[:, 0:1]).then_inc(S["w_ready"], 1)
                units = [(2 * q + k // GH, k % GH) for k in range(2 * GH)]
                for it in range(ITERS):
                    for s in range(2):
                        n = (q * ITERS + it) * 2 + s
                        if it == 0:
                            act.wait_ge(S["w_ready"], 2 * (2 * q + s + 1))
                        if n >= 2:
                            act.wait_ge(S["wn_ready"], 2 * (n - 1))
                        f(Fb[:, s], Wb[:, 2 * s + it % 2], ACT.Copy, scale=C1W).then_inc(S["e_ready"], 1)
                        for k in range(2):
                            act.wait_ge(S["mm1_ps"], 2 * n + k + 1)
                            f(two_heads(W2[:, s], k), half(s, k), ACT.Copy, scale=C2).then_inc(S["w2_ready"], 1)
                    if it == 0:
                        if q >= 1:
                            copy_mix(2 * q - 2)
                            copy_mix(2 * q - 1)
                        else:
                            k1_exp(*units.pop(0))
                    else:
                        for _ in range(3 if it >= 4 else 2):
                            if units:
                                k1_exp(*units.pop(0))
            for g in (G - 2, G - 1):
                copy_mix(g)

            act.wait_ge(S["ld_ad"], 192)
            adapter(S["t1_ps"], S["t1_ready"], S["z1_ps"], S["z1_ready"], AD, ab1, [(S["h1_ps"], B * HC)] * 2)
            roots(B)
            for b in range(B):
                act.wait_ge(S["xn1_ps"], b + 1)
                f(xnT[:, b, :], bank(4 * b + 1), ACT.Copy).then_inc(S["xn1_ready"], 1)
            for b in range(B):
                act.wait_ge(S["sc_sub"], B + b + 1)
                f(ex2[:, b, :, 0:E1], ex[:, b, :, 0:E1], ACT.Exp).then_inc(S["sc_exp"], 1)
            for n in range(B * (C1 + 1)):
                rows = P if n % (C1 + 1) < C1 else I1
                act.wait_ge(S["g_ps"], n + 1)
                if n >= 2:
                    act.wait_ge(S["gu_ready"], n - 1)
                f(act_sb[0:rows, n % 2, :], ps[0:rows, n % 2, :], ACT.Gelu).then_inc(S["gelu_ready"], 1)

        @block.gpsimd
        def _(pool):
            g_ = nc.gpsimd
            two = float(np.array([0x3F803F80], np.uint32).view(np.float32)[0])
            g_.memset(KS[64:96, :, :].bitcast(F32), two).then_inc(S["ones_rows"], 1)
            pool.wait_ge(S["ones_rows"], 1)
            pool.wait_ge(S["ld_res"], 64)
            for b in range(B):
                r = g_.tensor_tensor(x[:, b], x[:, b], boutb[:].rearrange("p (o f) -> p o f", o=1).to_broadcast([P, NT, P]),
                                     ALU.add)
                r.then_inc(S["xbias_ready"], 1)
                pool.wait_ge(S["xbias_ready"], b + 1)
            negsteps = [0]

            def split_rows(copied, done, g, rows, sent, before):
                pool.wait_ge(copied, g + 1)
                if g >= 2:
                    pool.wait_ge(sent[g % 2], 16 * PARTS * (g // 2))
                elif before:
                    pool.wait_ge(S["neg_rows"][g % 2], 16 * PARTS * G // 2)
                src, part = negR[0:rows, g % 2, :], [negT[0:rows, g % 2, i, :] for i in range(PARTS)]
                left = negS[0:rows, :]

                def step(ins):
                    negsteps[0] += 1
                    ins.then_inc(S["neg_step"], 1)
                    pool.wait_ge(S["neg_step"], negsteps[0])

                step(g_.tensor_copy(part[0], src))
                step(g_.tensor_tensor(left, src, part[0], ALU.subtract))
                step(g_.tensor_copy(part[1], left))
                g_.tensor_tensor(part[2], left, part[1], ALU.subtract).then_inc(done, 1)
                pool.wait_ge(done, g + 1)

            for g in range(G):
                split_rows(S["neg_copy"], S["neg_split"], g, UN, S["neg_rows"], 0)
            pool.wait_ge(S["ld_c0"], 192)
            for b in range(B):
                pool.wait_ge(S["x1_ready"], b + 1)
                g_.tensor_tensor(base[:, b], x1[:, b], rows0[:, b, 0:1, :].to_broadcast([P, NT, P]),
                                 ALU.add).then_inc(S["base0_ready"], 1)
                pool.wait_ge(S["base0_ready"], b + 1)
            for b in range(B):
                pool.wait_ge(S["n0_ready"], b + 1)
                g_.tensor_tensor(base[:, b], x1[:, b], x2[:, b], ALU.add).then_inc(S["x12_ready"], 1)
                pool.wait_ge(S["x12_ready"], b + 1)
            def landmark_attention(g):
                pool.wait_ge(S["rs_ready"], g + 1)
                if g == 3:
                    pool.wait_ge(S["stacks_in"][1], stack_in(1))
                g_.tensor_tensor(AY[:, GH * g:GH * g + GH, 0:P], ek2[:],
                                 rsum[:].rearrange("p (h o) -> p h o", o=1).to_broadcast([P, GH, P]),
                                 ALU.mult).then_inc(S["a_ready"], 1)
                pool.wait_ge(S["a_ready"], g + 1)

            landmark_attention(0)
            split_rows(S["n_copy"], S["n_split"], 0, 20, S["n_rows"], G)
            landmark_attention(1)
            for g in range(G):
                if g + 1 < G:
                    split_rows(S["n_copy"], S["n_split"], g + 1, 20, S["n_rows"], G)
                if g + 2 < G:
                    landmark_attention(g + 2)
            for n in range(G // 2 * ITERS * 2):
                pool.wait_ge(S["w2_ready"], 2 * (n + 1))
                pool.wait_ge(S["e_ready"], n + 1)
                g_.tensor_tensor(Fb[:, n % 2], Fb[:, n % 2], W2[:, n % 2], ALU.subtract).then_inc(S["f_ready"], 1)
                pool.wait_ge(S["f_ready"], n + 1)
            pool.wait_ge(S["ld_ad"], 192)
            for b in range(B):
                pool.wait_ge(S["x4_ready"], b + 1)
                g_.tensor_tensor(base[:, b], x4[:, b], rows1[:, b, 0:1, :].to_broadcast([P, NT, P]),
                                 ALU.add).then_inc(S["base1_ready"], 1)
                pool.wait_ge(S["base1_ready"], b + 1)


def tables():
    f = np.float32
    inv = (f(1.0) / np.power(f(10000.0), (np.arange(0, HD, 2, dtype=f) / f(HD)))).astype(f)
    fr = np.arange(T, dtype=f)[:, None] * inv[None, :]
    emb = np.concatenate((fr, fr), axis=-1)
    cos, sin = np.cos(emb).astype(f), np.sin(emb).astype(f)
    sign = np.where(np.arange(HD) < HD // 2, f(-1), f(1))
    spread = lambda m: np.ascontiguousarray(np.repeat(m.T, H, axis=0))
    ident = np.eye(P, dtype=f)
    bf = lambda m: (m * 0x3F80).astype(np.uint16)

    def select(experts, width, chunks):
        s = np.zeros((PARTS, experts, chunks, P), f)
        for c in range(chunks):
            for m in range(P):
                s[:, (c * P + m) // width, c, m] = 1
        return bf(s.reshape(PARTS * experts, chunks, P))

    return {"cos": spread(cos), "sin": spread(sin * sign), "ident": ident, "identb": bf(ident),
            "sel0": select(E0, PD, C0), "sel1": select(E1, I1, C1)}


def kernel(**inputs):
    import concourse.bacc as bacc
    from concourse.bass_utils import run_bass_kernel_spmd

    w = {k: np.asarray(v) for k, v in inputs.items()}
    c = np.ascontiguousarray
    dh = np.arange(H * HD).reshape(H, HD).T.reshape(-1)
    turned = [1, 3, 5, 7, 0, 2, 4, 6]
    dhr = np.arange(H * HD).reshape(H, HD)[:, turned].T.reshape(-1)
    q, k, v = np.split(w["L0_attn_w_qkv"], 3, axis=0)
    data = {
        "ids": np.concatenate([w["itok_B_0_7"], w["itok_B_0_6"], w["itok_B_0_8"]])[None, :],
        "x": w["x"], "xT": w["x"].transpose(0, 2, 1),
        "w0T": w["L0_cond_weight"].transpose(0, 2, 1), "b0": w["L0_cond_bias"],
        "wqkT": np.stack([q[dh].T, q[dhr].T, k[dh].T, k[dhr].T]), "wvT": v.T,
        "woutT": w["L0_attn_w_out"].T, "bout": w["L0_attn_b_out"][None, :],
        "down": w["L0_cond2_down_w"], "bd": w["L0_cond2_down_b"], "up": w["L0_cond2_up_w"],
        "bu": w["L0_cond2_up_b"], "ln_g": w["L0_cond2_ln_g"], "ln_b": w["L0_cond2_ln_b"],
        "hashT": w["L0_ffn_hasher_w"].T, "keysT": w["L0_ffn_keys"].T, "vd": w["L0_ffn_values_down"],
        "vu": w["L0_ffn_values_up"], "scale": w["L0_ffn_scale"][None, :],
        "w1": w["L1_cond_W1"], "b1": w["L1_cond_b1"].reshape(HC, P).T, "w2": w["L1_cond_W2"], "b2": w["L1_cond_b2"],
        "we": w["L1_cond_We"], "be": w["L1_cond_be"],
        "wl1T": np.stack([w["L1_attn_Wq"][dh].T, w["L1_attn_Wk"][dh].T, w["L1_attn_Wv"].T]),
        "bl1": np.stack([w["L1_attn_bq"][dh], w["L1_attn_bk"][dh]], axis=1), "bv": w["L1_attn_bv"][None, :],
        "a1": w["L1_cond2_W1"], "ab1": w["L1_cond2_b1"], "a2": w["L1_cond2_W2"], "ab2": w["L1_cond2_b2"],
        "gamma": w["L1_cond2_gamma"], "beta": w["L1_cond2_beta"],
        "gateT": w["L1_ffn_gate_w"].T, "wg": w["L1_ffn_Wg"], "wu": w["L1_ffn_Wu"], "wd": w["L1_ffn_Wd"],
        "swg": w["L1_ffn_sWg"], "swu": w["L1_ffn_sWu"], "swd": w["L1_ffn_sWd"],
        **tables(),
    }
    nc = bacc.Bacc("TRN2", target_bir_lowering=False, num_devices=1)
    arrays, aps = {}, {}
    for name, value in data.items():
        arrays[f"in_{name}"] = c(value)
        aps[name] = nc.dram_tensor(f"in_{name}", value.shape, mybir.dt.from_np(value.dtype), kind="ExternalInput").ap()
    out = nc.dram_tensor("out_0", (B, T, P), F32, kind="ExternalOutput").ap()
    build(nc, aps, out)
    r = run_bass_kernel_spmd(nc, [arrays], core_ids=[0])
    return r.results[0]["out_0"]
```

```python
from contextlib import ExitStack

import numpy as np

import concourse.bass as bass
from concourse import mybir

F32 = mybir.dt.float32
BF16 = mybir.dt.bfloat16
I32 = mybir.dt.int32
U16 = mybir.dt.uint16
ALU = mybir.AluOpType
ACT = mybir.ActivationFunctionType
AX = mybir.AxisListType

P = 128
B, T = 2, 512
NT = T // P
H, HD = 16, 8
GH = 4
NG = H // GH
G = B * NG
PARTS = 3
PROD = PARTS * PARTS * HD
KROWS = PROD + PARTS
LM = 128
SEG = T // LM
LW = T + LM
ITERS = 6
VW = 2 * HD
WA = P + HD
E0, PD, TOP0 = 32, 32, 4
C0 = E0 * PD // P
HC = 4
UN = GH * NT
LAG = 28
AD = 32
E1, I1, TOP1 = 8, 64, 2
C1 = E1 // 2
RING = (0, 1, 7)
WINDOW = 2 * PARTS - 1
STACK_DMAS = 2 * PARTS
EPS = 1e-5
LOW = -3.0e38
HIGH = 3.0e38

SEMAPHORES = """ld_ids ld_in ld_qkv ld_res ld_c0 ld_f0 ld_c1 ld_l1 ld_ad ld_f1
mv_ready rstd_ready const_ready step_dve stored
y0_ps y0_ready qk_ps v_ps rot_cos rot_done part_a res_a part_b part_c parts_out_0 parts_out_1 parts_out_2 parts_out_3 stacks_in_0 stacks_in_1 first_heads ones_rows vaug_ready
smax_ps smax_done negT_ps neg_copy neg_step neg_split neg_rows_0 neg_rows_1 st_ps exp_done av_ps outT_ready otr_ps o_ready
oT_ps oT_ready proj_ps x1_ready xbias_ready
t0_ps t0_ready t1_ps t1_ready z0_ps z0_ready z1_ps z1_ready u0_ps u1_ps u_read sim_read n0_ready n1_ready base0_ready base1_ready
xn0_ps xn0_ready xn1_ps xn1_ready
hash_ps hash_ready sim_ps cwp_ready cwT_ps cwT_ready up_proj_ps silu_ready sel_ps hid_ready down_ps x3_ready x12_ready
x3T_ps x3T_ready h1_ps h1_ready y1_ps y1_ready
l1q_ps l1k_ps l1v_ps l1q_ready l1k_ready bl1_ready lm_ready v1_ready l1_parts
k2_ps k2_max k2_exp rs_ready a_ready col_ps col_copy col_done m_ps m_done n_ps n_copy n_split n_rows_0 n_rows_1 k3_ps k3_exp yv_ps yv_sb ytr_ps y_ready
rc_ready rcb_ps rcb_ready
sq_ps w_ready mm1_ps w2_ready e_ready f_ready d_ready mm2_ps wn_ready k1_ps k1_exp gaug_ready x_ps xo_sb xtr_ps xo_ready x4_ready gaug_ones
gate_ps sc_sub sc_exp cw1_ready cw1T_ps cw1T_ready g_ps gelu_ready uu_ps gu_ready cs_ps hid1_ready fin_ps out_ready"""


def build(nc, a, out):
    ctx = ExitStack()
    with ctx:
        def sb(name, shape, dt=F32):
            return ctx.enter_context(nc.sbuf_tensor(name, shape, dt))

        S = {}
        for n in SEMAPHORES.split():
            S[n] = ctx.enter_context(nc.semaphore(n))

        S["stacks_in"] = (S["stacks_in_0"], S["stacks_in_1"])
        S["parts_out"] = [S[f"parts_out_{n}"] for n in range(4)]
        S["neg_rows"] = (S["neg_rows_0"], S["neg_rows_1"])
        S["n_rows"] = (S["n_rows_0"], S["n_rows_1"])

        ids = sb("ids", [1, 8], I32)
        ident = sb("ident", [P, P])
        identb = sb("identb", [P, P], BF16)
        ones = sb("ones", [P, P])
        x = sb("x", [P, B, NT, P])
        xT = sb("xT", [P, B, T])
        w0T = sb("w0T", [P, B, P])
        b0 = sb("b0", [P, B])
        y0T = sb("y0T", [P, B, T])
        wqk = sb("wqk", [P, 4, P])
        wv = sb("wv", [P, P])
        QS = sb("QS", [P, B, H * LW], BF16)
        KS = sb("KS", [P, B, H * LW], BF16)
        V = sb("V", [P, B, NT, H, VW])
        woutT = sb("woutT", [P, P])
        boutb = sb("boutb", [P, P])
        negm = sb("negm", [P, 2, 20])
        negT = sb("negT", [32, 2, PARTS, P], BF16)
        negR = sb("negR", [32, 2, P])
        negS = sb("negS", [32, P])
        outT = sb("outT", [P, T])
        rden = sb("rden", [P, NT, GH])
        O = sb("O", [P, B, NT, P])
        featT = sb("featT", [P, B, T])
        stats = sb("stats", [P, B, NT, 6])
        mv = sb("mv", [P, B, NT, 2])
        rstd = sb("rstd", [P, B, NT])
        veps = sb("veps", [P, B, NT])
        rinv = sb("rinv", [P, B, NT])
        root = sb("root", [P, B, NT])
        wdn = sb("wdn", [P, B, P])
        bdn = sb("bdn", [P, B])
        wup = sb("wup", [P, B, P])
        rows0 = sb("rows0", [P, B, 3, P])
        rows1 = sb("rows1", [P, B, 3, P])
        hashT = sb("hashT", [P, PD])
        keysT = sb("keysT", [PD, E0])
        scale = sb("scale", [P, 1])
        sel0 = sb("sel0", [PARTS * E0, C0, P], BF16)
        sel1 = sb("sel1", [PARTS * E1, C1, P], BF16)
        sim = sb("sim", [P, B, NT, E0 + 8])
        took = sb("took", [P, B, NT, E0 + 8])
        best = sb("best", [P, B, NT, 8])
        pick = sb("pick", [P, B, NT, 8])
        ex = sb("ex", [P, B, NT, E0])
        ex2 = sb("ex2", [P, B, NT, E0])
        tot = sb("tot", [P, B, NT])
        totr = sb("totr", [P, B, NT])
        cw = sb("cw", [P, B, NT, E0])
        cwr = ex
        cwp = sb("cwp", [P, B, NT, PARTS, E0], BF16)
        cwT = sb("cwT", [PARTS * E0, B, T], BF16)
        sim1 = sim[:, :, :, 0:16]
        took1 = took[:, :, :, 0:16]
        cwp1 = sb("cwp1", [P, B, NT, PARTS, E1], BF16)
        b1 = sb("b1", [P, HC])
        b2 = sb("b2", [P, B])
        wl1 = sb("wl1", [P, 3, P])
        bl1 = sb("bl1", [P, 2])
        bl1s = sb("bl1s", [P, 2])
        bvb = sb("bvb", [P, P])
        sums = sb("sums", [P, GH])
        rsum = sb("rsum", [P, GH])
        cmax = sb("cmax", [P, 3])
        rc = sb("rc", [1, 2])
        rcb = sb("rcb", [P, 1])
        Gaug = sb("Gaug", [P, 2, GH, VW])
        gateT = sb("gateT", [P, E1])
        a1 = sb("a1", [P, B, AD])
        ab1 = sb("ab1", [AD, B])
        a2 = sb("a2", [AD, B, P])

        PT = sb("PT", [P, 8, T])
        early = sb("early", [P, 6400])
        late = sb("late", [P, 5440])

        def view(buf, at, *shape):
            n = int(np.prod(shape))
            ap = buf[:, at:at + n]
            names = " ".join("abcd"[:len(shape)])
            return ap.rearrange(f"p ({names}) -> p {names}", **dict(zip("abcd", shape))) if len(shape) > 1 else ap

        PW = PARTS * LW * 4 // 2
        parts = early[:, 0:PW].bitcast(BF16).rearrange("p (n i t) -> p n i t", n=4, i=PARTS)
        qk = view(early, PW, 2, LW)
        res = view(early, PW + 2 * LW, 2, LW)
        vd = view(early, 0, E0 * PD)
        vu = view(early, 1024, C0, P)
        hc = view(early, 2048, HC, T)
        act_sb = view(early, 2048, 2, T)
        gu_sb = view(early, 3072, 2, T)
        w1 = view(early, 4096, HC, P)
        w2 = view(early, 4608, B, HC, P)
        room = QS[:, 1, :].bitcast(F32)
        parts1, qk1, res1 = [], [], []
        for n in range(4):
            k, words = n % 2, PARTS * LW // 2
            buf, at = ((room, (0, 2 * words, 2 * words + 2 * LW)), (early, (6400 - 2 * LW - 2 * words, None, 6400 - 2 * LW)))[n // 2]
            parts1.append(buf[:, at[0] + k * words:at[0] + (k + 1) * words].bitcast(BF16).rearrange("p (i t) -> p i t", i=PARTS))
            qk1.append(buf[:, at[1] + k * LW:at[1] + (k + 1) * LW] if n < 2 else view(late, 4096 + k * LW, LW))
            res1.append(buf[:, at[2] + k * LW:at[2] + (k + 1) * LW])
        AY = view(early, 0, B * H, WA)
        wg = view(early, 4352, E1 * I1)
        wu = view(early, 4864, E1 * I1)
        wd = view(early, 5376, C1, P)
        swg = view(early, 5888, I1)
        swu = view(early, 5952, I1)
        swd = early[0:I1, 6016:6016 + P]
        x1 = view(late, 0, B, NT, P)
        base = view(late, 1024, B, NT, P)
        y = view(late, 2048, B, NT, P)
        x2 = view(late, 3072, B, NT, P)
        zT = view(late, 4096, B, T)
        hT = late[0:PD, 4096:5120].rearrange("p (b t) -> p b t", b=B)
        room0 = QS[:, 0, :].bitcast(F32)
        base1 = [view(room0, 0, NT, P), base[:, 1]]
        y1 = [view(room0, 512, NT, P), y[:, 1]]
        n1 = [view(room0, 1024, NT, P), x2[:, 1]]
        z1T = [room0[:, 1536:1536 + T], zT[:, 1, :]]
        base_of, y_of, x2_of, zT_of = ([base[:, b] for b in range(B)], base1), ([y[:, b] for b in range(B)], y1), \
            ([x2[:, b] for b in range(B)], n1), ([zT[:, b, :] for b in range(B)], z1T)
        Wb = view(late, 0, 2 * 2, GH, WA)
        W2 = view(late, 2176, 2, GH, WA)
        Fb = view(late, 3264, 2, GH, WA)
        Db = view(late, 4352, 2, GH, WA)
        colsum = view(late, 0, 2, T)
        cos, sin, rot = PT[:, 0, :], PT[:, 1, :], PT[:, 2:4, :]
        ek2 = featT[:, 0, :].rearrange("p (h m) -> p h m", h=GH)
        ysb = featT[:, 1, 0:P]
        neg2 = sb("neg2", [P, GH])
        x3 = x
        xnT = y0T
        y1T = xT
        x4 = O
        hid = PT

        ps = ctx.enter_context(nc.psum_tensor("ps", [P, 8, T], F32))
        bank = lambda i: ps[:, i, :]

        parts_dram = [nc.dram_tensor(f"parts_layer{n}", [4, WINDOW, HD, H, width], BF16, kind="Internal").ap()
                      for n, width in enumerate((T, LW))]

        QS0 = [QS[:, b, 0:H * T].rearrange("p (h t) -> p h t", h=H) for b in range(B)]
        KS0 = [KS[:, b, 0:H * T].rearrange("p (h t) -> p h t", h=H) for b in range(B)]
        QS1 = [QS[:, b, :].rearrange("p (h t) -> p h t", h=H) for b in range(B)]
        KS1 = [KS[:, b, :].rearrange("p (h t) -> p h t", h=H) for b in range(B)]
        MAPS = 0.5 ** 0.5 * 0.5
        QSCALE = float(1.0 / np.sqrt(np.sqrt(np.float64(HD))))

        block = ctx.enter_context(nc.Block())
        tile = lambda t: slice(t * P, (t + 1) * P)
        half = lambda s, k: ps[:, 2 * s + k, 0:2 * WA]
        two_heads = lambda ap, k: ap[:, 2 * k:2 * k + 2, :].rearrange("p h w -> p (h w)")
        parts_out = lambda n, layer: 16 * (PARTS if n % 2 == 0 else WINDOW) * (layer + 1)
        stack_in = lambda layer: 16 * STACK_DMAS * (layer + 1)
        C1W, C2 = 13.0 / 4, 15.0 / 4

        @block.sync
        def _(sp):
            def load(dst, src, sem):
                sp.dma_start(dst, src).then_inc(sem, 16)

            load(ids[0:1, 0:6], a["ids"], S["ld_ids"])
            load(xT[:], a["xT"].rearrange("b h t -> h b t"), S["ld_in"])
            sp.wait_ge(S["ld_ids"], 16)
            subj = [sp.value_load(ids[0:1, b:b + 1], min_val=0, max_val=7) for b in range(B)]
            one = lambda ap, i: ap[bass.ds(i, 1)]
            def load_subject(b, sem):
                load(w0T[:, b, :], one(a["w0T"], subj[b]).rearrange("s h o -> (s h) o"), sem)
                load(b0[:, b:b + 1], one(a["b0"], subj[b]).rearrange("s h -> h s"), sem)

            load_subject(0, S["ld_in"])
            load(wqk[:], a["wqkT"].rearrange("n h o -> h n o"), S["ld_qkv"])
            load(cos[:], a["cos"], S["ld_qkv"])
            load(sin[:], a["sin"], S["ld_qkv"])
            load_subject(1, S["ld_qkv"])
            load(wv[:], a["wvT"], S["ld_qkv"])
            load(ident[:], a["ident"], S["ld_res"])
            load(identb[:].bitcast(U16), a["identb"], S["ld_res"])
            for b in range(B):
                load(x[:, b], a["x"][b].rearrange("(n p) f -> p n f", p=P), S["ld_res"])
            load(boutb[:], a["bout"].to_broadcast([P, P]), S["ld_res"])
            load(woutT[:], a["woutT"], S["ld_res"])
            prof = [sp.value_load(ids[0:1, 2 + b:3 + b], min_val=0, max_val=7) for b in range(B)]
            lang = [sp.value_load(ids[0:1, 4 + b:5 + b], min_val=0, max_val=9) for b in range(B)]

            def send_parts(n, layer, i, src):
                sp.wait_ge(S[("part_a", "part_b", ("part_c", "l1_parts")[layer])[i]], (n + 1) if i == 2 else 4 * layer + n + 1)
                dram = parts_dram[layer]
                for w in range(i, PARTS if n % 2 == 0 else WINDOW, PARTS):
                    sp.dma_start(dram[n, w].rearrange("d h t -> (d h) t"), src[:, i, 0:dram.shape[-1]]
                                 ).then_inc(S["parts_out"][n], 16)

            def fetch_stack(n, dram, layer, heads, done):
                b, width = n // 2, dram.shape[-1]
                sp.wait_ge(S["parts_out"][n], parts_out(n, layer))
                R = PARTS * HD
                for k in range(PARTS):
                    w = 0 if n % 2 == 0 else k
                    sp.dma_start((QS if n % 2 == 0 else KS)[k * R:(k + 1) * R, b, heads.start * width:heads.stop * width],
                                 dram[n, w:w + PARTS, :, heads].rearrange("i d h t -> (i d) h t").rearrange("r h t -> r (h t)")
                                 ).then_inc(done, 16)

            sp.wait_ge(S["ones_rows"], 1)
            def send(b, layer, src):
                for i in range(PARTS):
                    for n in (2 * b, 2 * b + 1):
                        send_parts(n, layer, i, src[n])

            def fetch(b, layer, heads, done):
                for n in (2 * b, 2 * b + 1):
                    fetch_stack(n, parts_dram[layer], layer, heads, done)

            parts0 = [parts[:, n] for n in range(4)]
            send(0, 0, parts0)
            fetch(0, 0, slice(0, GH), S["first_heads"])
            fetch(0, 0, slice(GH, H), S["stacks_in"][0])
            send(1, 0, parts0)
            def neg_rows(g):
                sp.wait_ge(S["neg_split"], g + 1)
                b, h0 = g // NG, g % NG * GH
                for i in range(PARTS):
                    dst = QS0[b][PROD + i:PROD + i + 1, h0:h0 + GH, :].rearrange("p h (n t) -> p (h n) t", t=P)
                    sp.dma_start(dst, negT[0:GH * NT, g % 2, i, :]).then_inc(S["neg_rows"][g % 2], 16)

            neg_rows(0)
            fetch(1, 0, slice(0, H), S["stacks_in"][1])
            neg_rows(1)
            for b in range(B):
                load(wdn[:, b, :], one(a["down"], prof[b]).rearrange("s h o -> (s h) o"), S["ld_c0"])
                load(bdn[:, b:b + 1], one(a["bd"], prof[b]).rearrange("s h -> h s"), S["ld_c0"])
                load(wup[:, b, :], one(a["up"], prof[b]).rearrange("s h o -> (s h) o"), S["ld_c0"])
                for k, n in enumerate(("bu", "ln_g", "ln_b")):
                    load(rows0[:, b, k, :], one(a[n], prof[b]).to_broadcast([P, P]), S["ld_c0"])
            neg_rows(2)
            load(hashT[:], a["hashT"], S["ld_f0"])
            load(keysT[:], a["keysT"], S["ld_f0"])
            load(vd[:].rearrange("p (e q) -> p e q", e=E0), a["vd"].rearrange("e d q -> d e q"), S["ld_f0"])
            load(vu[:], a["vu"].rearrange("e q d -> (e q) d").rearrange("(c p) d -> p c d", p=P), S["ld_f0"])
            load(scale[:], a["scale"].to_broadcast([P, 1]), S["ld_f0"])
            load(sel0[:].bitcast(U16), a["sel0"], S["ld_f0"])
            load(sel1[:].bitcast(U16), a["sel1"], S["ld_f0"])
            neg_rows(3)
            load(w1[:], a["w1"].rearrange("h (c n) -> h c n", c=HC), S["ld_c1"])
            load(b1[:], a["b1"], S["ld_c1"])
            PO = P - 32
            for b in range(B):
                load(w2[:, b, :, 0:PO], a["w2"].rearrange("(c n) o -> n c o", c=HC), S["ld_c1"])
                load(w2[:, b, :, PO:P], one(a["we"], subj[b]).rearrange("s (c n) o -> (s n) c o", c=HC), S["ld_c1"])
                load(b2[0:PO, b:b + 1], a["b2"].rearrange("(o s) -> o s", s=1), S["ld_c1"])
                load(b2[PO:P, b:b + 1], one(a["be"], subj[b]).rearrange("s o -> o s"), S["ld_c1"])
            for g in range(4, G):
                neg_rows(g)
            load(wl1[:], a["wl1T"].rearrange("n h o -> h n o"), S["ld_l1"])
            load(bl1[:], a["bl1"], S["ld_l1"])
            load(bvb[:], a["bv"].to_broadcast([P, P]), S["ld_l1"])
            for b in range(B):
                load(a1[:, b, :], one(a["a1"], lang[b]).rearrange("s h o -> (s h) o"), S["ld_ad"])
                load(ab1[:, b:b + 1], one(a["ab1"], lang[b]).rearrange("s h -> h s"), S["ld_ad"])
                load(a2[:, b, :], one(a["a2"], lang[b]).rearrange("s h o -> (s h) o"), S["ld_ad"])
                for k, n in enumerate(("ab2", "gamma", "beta")):
                    load(rows1[:, b, k, :], one(a[n], lang[b]).to_broadcast([P, P]), S["ld_ad"])
            load(gateT[:], a["gateT"], S["ld_f1"])
            def landmark_rows(g):
                sp.wait_ge(S["n_split"], g + 1)
                b, h0 = g // NG, g % NG * GH
                for i in range(PARTS):
                    dst = QS1[b][PROD + i:PROD + i + 1, h0:h0 + GH, :].rearrange("p h (n t) -> p (h n) t", t=P)
                    sp.dma_start(dst, negT[0:20, g % 2, i, :]).then_inc(S["n_rows"][g % 2], 16)

            send(0, 1, parts1)
            sp.wait_ge(S["st_ps"], UN * NG)
            fetch(0, 1, slice(0, GH), S["first_heads"])
            fetch(0, 1, slice(GH, H), S["stacks_in"][0])
            for g in range(2):
                landmark_rows(g)
            send(1, 1, parts1)
            sp.wait_ge(S["st_ps"], UN * G)
            fetch(1, 1, slice(0, GH), S["first_heads"])
            landmark_rows(2)
            fetch(1, 1, slice(GH, H), S["stacks_in"][1])
            landmark_rows(3)
            load(wg[:].rearrange("p (e i) -> p e i", e=E1), a["wg"].rearrange("e h i -> h e i"), S["ld_f1"])
            load(wu[:].rearrange("p (e i) -> p e i", e=E1), a["wu"].rearrange("e h i -> h e i"), S["ld_f1"])
            load(wd[:], a["wd"].rearrange("e i h -> (e i) h").rearrange("(c p) h -> p c h", p=P), S["ld_f1"])
            load(swg[:], a["swg"], S["ld_f1"])
            load(swu[:], a["swu"], S["ld_f1"])
            load(swd[:], a["swd"], S["ld_f1"])
            for g in range(4, G):
                landmark_rows(g)

            for b in range(B):
                sp.wait_ge(S["out_ready"], b + 1)
                sp.dma_start(out[b].rearrange("(n p) f -> p n f", p=P), y1[b]).then_inc(S["stored"], 16)
            sp.wait_ge(S["stored"], 16 * B)
            for n in range(4):
                sp.wait_ge(S["parts_out"][n], parts_out(n, 1))

        @block.tensor
        def _(pe):
            mm = nc.tensor.matmul

            def condition0(b):
                mm(bank(5 + b), w0T[:, b, :], xT[:, b, :], start=True, stop=True).then_inc(S["y0_ps"], 1)

            pe.wait_ge(S["ld_in"], 48)
            condition0(0)
            pe.wait_ge(S["ld_qkv"], 96)
            for b in range(B):
                pe.wait_ge(S["y0_ready"], b + 1)
                for n in range(4):
                    if 5 * b + n == 8:
                        pe.wait_ge(S["rot_cos"], 2)
                    mm(bank((5 * b + n) % 8), wqk[:, n, :], y0T[:, b, :], start=True, stop=True).then_inc(S["qk_ps"], 1)
                if b == 0:
                    condition0(1)
                if b == 1:
                    pe.wait_ge(S["rot_cos"], 2)
                for t in range(NT):
                    r = mm(ps[:, (5 * b + 4) % 8, tile(t)], y0T[:, b, tile(t)], wv[:], start=True, stop=True)
                r.then_inc(S["v_ps"], 1)

            def s_max(m):
                g, u = m // UN, m % UN
                b, h = g // NG, g % NG * GH + u // NT
                if m == 0:
                    pe.wait_ge(S["first_heads"], stack_in(0))
                elif u == 0 and g in (1, NG):
                    pe.wait_ge(S["stacks_in"][b], stack_in(0))
                if m == 0:
                    pe.wait_ge(S["rot_cos"], 8)
                    pe.wait_ge(S["vaug_ready"], B)
                if m >= 3:
                    pe.wait_ge(S["smax_done"], m - 2)
                mm(bank(m % 3), QS0[b][0:PROD, h, tile(u % NT)], KS0[b][0:PROD, h, :],
                   start=True, stop=True).then_inc(S["smax_ps"], 1)

            def neg_t(g):
                pe.wait_ge(S["smax_done"], UN * (g + 1))
                if g >= 1:
                    pe.wait_ge(S["neg_copy"], g)
                if g >= 3:
                    pe.wait_ge(S["o_ready"], g - 2)
                if g == 6:
                    pe.wait_ge(S["u_read"], 1)
                nc.tensor.transpose(ps[0:UN, 7, 0:P], negm[:, g % 2, 0:UN], ident[:]).then_inc(S["negT_ps"], 1)

            def scores(n):
                g, kb, j = n // UN, n % UN // GH, n % GH
                b, h = g // NG, g % NG * GH + j
                if n % UN == 0:
                    pe.wait_ge(S["neg_rows"][g % 2], 16 * PARTS * (g // 2 + 1))
                if n >= 3:
                    pe.wait_ge(S["exp_done"], n - 2)
                mm(bank(3 + n % 3), KS0[b][0:KROWS, h, tile(kb)], QS0[b][0:KROWS, h, :],
                   start=True, stop=True).then_inc(S["st_ps"], 1)

            def av(k):
                g, kb = k // NT, k % NT
                b = g // NG
                pe.wait_ge(S["exp_done"], GH * (k + 1))
                if kb == 0 and g >= 1:
                    pe.wait_ge(S["outT_ready"], g)
                for j in range(GH):
                    r = mm(ps[32 * j:32 * j + VW, 6, :], V[:, b, kb, g % NG * GH + j, :],
                           PT[:, kb % 2 * 4 + j, :], start=(kb == 0), stop=(kb == NT - 1))
                r.then_inc(S["av_ps"], 1)

            def out_t(g):
                pe.wait_ge(S["outT_ready"], g + 1)
                pe.wait_ge(S["neg_copy"], min(g + 3, G))
                if g >= 1:
                    pe.wait_ge(S["o_ready"], g)
                if g == 6:
                    pe.wait_ge(S["sim_read"], 1)
                if g == G - 1:
                    pe.wait_ge(S["cwT_ready"], 1)
                for t in range(NT):
                    r = nc.tensor.transpose(ps[:, 7, tile(t)], outT[:, tile(t)], ident[:])
                r.then_inc(S["otr_ps"], 1)

            def turn(bk, src, done):
                for t in range(NT):
                    r = nc.tensor.transpose(ps[:, bk, tile(t)], src[:, t, :], ident[:])
                r.then_inc(done, 1)

            def token_mm(bk, lhs, rhs, done):
                for t in range(NT):
                    r = mm(ps[:, bk, tile(t)], lhs[:, tile(t)], rhs, start=True, stop=True)
                r.then_inc(done, 1)

            def project_out(b, turned, projected):
                if turned is not None:
                    pe.wait_ge(S["o_ready"], NG * (b + 1))
                    turn(turned, O[:, b], S["oT_ps"])
                if projected is not None:
                    pe.wait_ge(S["ld_res"], 96)
                    pe.wait_ge(S["oT_ready"], b + 1)
                    token_mm(projected, featT[:, b, :], woutT[:], S["proj_ps"])

            def adapter_in(b, bk, layer, src):
                pe.wait_ge(S[("x1_ready", "x4_ready")[layer]], b + 1)
                turn(bk, src[:, b], S[("t0_ps", "t1_ps")[layer]])

            def adapter_down(b, bk, layer, w, rows):
                pe.wait_ge(S[("ld_c0", "ld_ad")[layer]], 192)
                pe.wait_ge(S[("t0_ready", "t1_ready")[layer]], b + 1)
                mm(ps[0:rows, bk, :], w[:, b, :], featT[:, b, :], start=True, stop=True).then_inc(S[("z0_ps", "z1_ps")[layer]], 1)

            def adapter_up(b, bk, layer, w, rows):
                pe.wait_ge(S[("z0_ready", "z1_ready")[layer]], b + 1)
                token_mm(bk, zT_of[layer][b][0:rows, :], w[:, b, :], S[("u0_ps", "u1_ps")[layer]])

            def turn_norm(b, bk, layer):
                pe.wait_ge(S[("n0_ready", "n1_ready")[layer]], b + 1)
                turn(bk, x2_of[layer][b], S[("xn0_ps", "xn1_ps")[layer]])

            def hash_mm(b, bk):
                pe.wait_ge(S["ld_f0"], 112)
                pe.wait_ge(S["xn0_ready"], b + 1)
                mm(ps[0:PD, bk, :], hashT[:], xnT[:, b, :], start=True, stop=True).then_inc(S["hash_ps"], 1)

            def similarity(b, bk):
                pe.wait_ge(S["hash_ready"], b + 1)
                for t in range(NT):
                    r = mm(ps[:, bk, t * E0:(t + 1) * E0], hT[:, b, tile(t)], keysT[:], start=True, stop=True)
                r.then_inc(S["sim_ps"], 1)

            def turn_weights(b, bk):
                pe.wait_ge(S["cwp_ready"], b + 1)
                for t in range(NT):
                    r = nc.tensor.transpose(ps[0:PARTS * E0, bk, :].bitcast(BF16)[:, tile(t)],
                                            cwp[:, b, t].rearrange("p i e -> p (i e)"), identb[:])
                r.then_inc(S["cwT_ps"], 1)

            pe.wait_ge(S["ld_res"], 96)
            for m in range(LAG):
                s_max(m)
                if m == UN + 1:
                    neg_t(0)
            for n in range(G * UN + UN):
                g, u = n // UN, n % UN
                if n < G * UN:
                    scores(n)
                if n + LAG < G * UN:
                    s_max(n + LAG)
                if u == 6 and g + 1 < G:
                    neg_t(g + 1)
                if n >= 5 and (n - 5) % GH == 0 and (n - 5) // GH < G * NT:
                    av((n - 5) // GH)
                if u == 8 and 1 <= g:
                    out_t(g - 1)
                if (g, u) == (4, 11):
                    project_out(0, 7, None)
                if (g, u) == (4, 13):
                    project_out(0, None, 7)
                if (g, u) == (5, 0):
                    adapter_in(0, 7, 0, x1)
                if (g, u) == (5, 2):
                    adapter_down(0, 7, 0, wdn, P)
                if (g, u) == (5, 4):
                    adapter_up(0, 7, 0, wup, P)
                if (g, u) == (6, 10):
                    pe.wait_ge(S["o_ready"], 6)
                    turn_norm(0, 7, 0)
                if (g, u) == (6, 12):
                    hash_mm(0, 7)
                if (g, u) == (6, 14):
                    similarity(0, 7)
                if (g, u) == (7, 14):
                    pe.wait_ge(S["o_ready"], 7)
                    turn_weights(0, 7)

            def up0(b, *chunks):
                for c in chunks:
                    n = b * C0 + c
                    if n >= 2:
                        pe.wait_ge(S["silu_ready"], n - 1)
                    mm(bank(n % 2), vd[:, tile(c)], xnT[:, b, :], start=True, stop=True).then_inc(S["up_proj_ps"], 1)

            def select0(b, *chunks):
                for c in chunks:
                    n = b * C0 + c
                    pe.wait_ge(S["cwT_ready"], b + 1)
                    if n >= 2:
                        pe.wait_ge(S["hid_ready"], n - 1)
                    mm(bank(2 + n % 2), sel0[:, c, :], cwT[:, b, :], start=True, stop=True).then_inc(S["sel_ps"], 1)

            def down0(b, bk, *tiles):
                pe.wait_ge(S["hid_ready"], C0 * (b + 1))
                for t in tiles:
                    for c in range(C0):
                        r = mm(ps[:, bk, tile(t)], hid[:, c, tile(t)], vu[:, c, :], start=(c == 0), stop=(c == C0 - 1))
                if t == NT - 1:
                    r.then_inc(S["down_ps"], 1)

            def turn_x3(b, bk):
                pe.wait_ge(S["x3_ready"], b + 1)
                turn(bk, x3[:, b], S["x3T_ps"])

            def condition_in(b, c, bk):
                pe.wait_ge(S["ld_c1"], 160)
                pe.wait_ge(S["x3T_ready"], b + 1)
                mm(bank(bk), w1[:, c, :], featT[:, b, :], start=True, stop=True).then_inc(S["h1_ps"], 1)

            def condition_out(b, bk):
                for c in range(HC):
                    pe.wait_ge(S["h1_ready"], HC * b + c + 1)
                    r = mm(bank(bk), w2[:, b, c, :], hc[:, c, :], start=(c == 0), stop=(c == HC - 1))
                r.then_inc(S["y1_ps"], 1)

            def project1(b, q, k, v):
                pe.wait_ge(S["ld_l1"], 48)
                pe.wait_ge(S["y1_ready"], b + 1)
                mm(bank(q), wl1[:, 0, :], y1T[:, b, :], start=True, stop=True).then_inc(S["l1q_ps"], 1)
                mm(bank(k), wl1[:, 1, :], y1T[:, b, :], start=True, stop=True).then_inc(S["l1k_ps"], 1)
                token_mm(v, y1T[:, b, :], wl1[:, 2, :], S["l1v_ps"])

            QL = lambda b, h, k: QS1[b][0:k, h, T:LW]
            KL = lambda b, h, k: KS1[b][0:k, h, T:LW]

            def landmark_scores(g):
                b, h0 = g // NG, g % NG * GH
                if g % NG == 0:
                    pe.wait_ge(S["first_heads"], stack_in(1 + b))
                elif g % NG == 1:
                    pe.wait_ge(S["stacks_in"][b], stack_in(1))
                if g >= 1:
                    pe.wait_ge(S["k2_exp"], GH * g)
                for j in range(GH):
                    r = mm(ps[:, 6, tile(j)], QL(b, h0 + j, PROD), KL(b, h0 + j, PROD), start=True, stop=True)
                r.then_inc(S["k2_ps"], 1)

            def maxima(g, u):
                b, n = g // NG, 2 * GH * g + u
                h = g % NG * GH + u // 2
                if n >= 3:
                    pe.wait_ge(S["m_done"], n - 2)
                if n == 2:
                    pe.wait_ge(S["v1_ready"], 1)
                if u % 2 == 0:
                    r = mm(bank(RING[n % 3]), QL(b, h, PROD), KS1[b][0:PROD, h, 0:T], start=True, stop=True)
                else:
                    for t in range(NT):
                        r = mm(ps[:, RING[n % 3], tile(t)], QS1[b][0:PROD, h, tile(t)], KL(b, h, PROD),
                               start=True, stop=True)
                r.then_inc(S["m_ps"], 1)

            def turn_maxima(g):
                pe.wait_ge(S["m_done"], 2 * GH * (g + 1))
                if g >= 2:
                    pe.wait_ge(S["col_copy"], g - 1)
                nc.tensor.transpose(ps[0:20, 5, 0:P], negm[:, g % 2, :], ident[:]).then_inc(S["n_ps"], 1)

            def value_scores(g, j):
                b, n = g // NG, GH * g + j
                h = g % NG * GH + j
                if j == 0:
                    pe.wait_ge(S["n_rows"][g % 2], 16 * PARTS * (g // 2 + 1))
                if n == 0:
                    pe.wait_ge(S["l1q_ready"], B)
                    pe.wait_ge(S["l1k_ready"], B)
                if n >= 2:
                    pe.wait_ge(S["k3_exp"], n - 1)
                for kb in range(NT):
                    r = mm(ps[:, 2 + n % 2, tile(kb)], KS1[b][0:KROWS, h, tile(kb)], QL(b, h, KROWS),
                           start=True, stop=True)
                r.then_inc(S["k3_ps"], 1)

            def landmark_values(g, *blocks):
                b, h0 = g // NG, g % NG * GH
                if g == 0:
                    pe.wait_ge(S["v1_ready"], B)
                if g >= 1:
                    pe.wait_ge(S["yv_sb"], g)
                pe.wait_ge(S["k3_exp"], GH * (g + 1))
                for kb in blocks:
                    for j in range(GH):
                        r = mm(ps[32 * j:32 * j + VW, 4, 0:P], V[:, b, kb, h0 + j, :],
                               PT[:, g % 2 * 4 + j, tile(kb)], start=(kb == 0), stop=(kb == NT - 1))
                if kb == NT - 1:
                    r.then_inc(S["yv_ps"], 1)

            def column_sums(g):
                pe.wait_ge(S["a_ready"], g + 1)
                pe.wait_ge(S["n_copy"], min(g + 2, G))
                if g >= 1:
                    pe.wait_ge(S["y_ready"], g)
                k = g % NG * 32
                mm(ps[k:k + 32, 5, :], ones[:, 0:32], AY[:, GH * g:GH * g + GH, 0:P], start=True, stop=True).then_inc(S["col_ps"], 1)

            def turn_values(g):
                pe.wait_ge(S["yv_sb"], g + 1)
                pe.wait_ge(S["col_copy"], g + 1)
                pe.wait_ge(S["n_copy"], min(g + 3, G))
                nc.tensor.transpose(ps[:, 5, 0:P], ysb[:], ident[:]).then_inc(S["ytr_ps"], 1)

            up0(0, 0)
            select0(0, 0)
            project_out(1, 4, None)
            up0(0, 1)
            select0(0, 1)
            project_out(1, None, 5)
            up0(0, 2)
            select0(0, 2)
            adapter_in(1, 4, 0, x1)
            up0(0, 3)
            select0(0, 3)
            adapter_down(1, 5, 0, wdn, P)
            up0(0, 4)
            select0(0, 4)
            adapter_up(1, 4, 0, wup, P)
            for c in range(5, C0):
                up0(0, c)
                select0(0, c)
            down0(0, 6, 0, 1, 2)
            turn_norm(1, 5, 0)
            down0(0, 6, 3)
            hash_mm(1, 4)
            turn_x3(0, 7)
            similarity(1, 5)
            for c in range(HC):
                condition_in(0, c, c)
            turn_weights(1, 4)
            condition_out(0, 6)
            project1(0, 1, 3, 7)
            up0(1, 0)
            pe.wait_ge(S["l1q_ready"], 1)
            up0(1, 1)
            select0(1, 0)
            pe.wait_ge(S["l1k_ready"], 1)
            select0(1, 1)
            for c in range(2, C0):
                up0(1, c)
                select0(1, c)

            for t in range(NT):
                down0(1, 4, t)
                if t == 1:
                    landmark_scores(0)
                for u in ((), (0, 1, 2), (3, 4, 5), (6, 7))[t]:
                    maxima(0, u)
            turn_x3(1, 3)
            landmark_scores(1)
            maxima(1, 0)
            condition_in(1, 0, 2)
            condition_in(1, 1, 4)
            maxima(1, 1)
            condition_in(1, 2, 3)
            maxima(1, 2)
            turn_maxima(0)
            pe.wait_ge(S["h1_ready"], HC + 1)
            condition_in(1, 3, 2)
            maxima(1, 3)
            maxima(1, 4)
            pe.wait_ge(S["h1_ready"], HC + 2)
            condition_out(1, 4)
            maxima(1, 5)
            maxima(1, 6)
            project1(1, 2, 3, 4)
            maxima(1, 7)
            turn_maxima(1)
            def heads_mm(s, done, lhs, rhs):
                for j in range(GH):
                    r = mm(ps[:, 2 * s + j // 2, j % 2 * WA:(j % 2 + 1) * WA], lhs(j), rhs(j), start=True, stop=True)
                    if j % 2 == 1:
                        r.then_inc(done, 1)

            def squares(g):
                heads_mm(g % 2, S["sq_ps"], lambda j: AY[:, GH * g + j, 0:P], lambda j: AY[:, GH * g + j, :])

            for g in range(G):
                ahead = g + 2 < G
                if ahead:
                    landmark_scores(g + 2)
                if 1 < g + 1 < G:
                    turn_maxima(g + 1)
                for u in range(2 * GH):
                    if ahead:
                        maxima(g + 2, u)
                    if u < GH:
                        value_scores(g, u)
                    if u == 2 and g >= 1:
                        turn_values(g - 1)
                    if u == 5:
                        landmark_values(g, 0)
                    if u == 6:
                        landmark_values(g, 1)
                if g == G - 2:
                    pe.wait_ge(S["m_done"], 2 * GH * G)
                    squares(0)
                column_sums(g)
                landmark_values(g, 2, 3)
                if g == G - 1:
                    pe.wait_ge(S["k3_exp"], GH * G)
                    squares(1)
            turn_values(G - 1)

            pe.wait_ge(S["col_done"], 1)
            nc.tensor.transpose(ps[0:1, 7, P:2 * P], cmax[:, 2:3], ident[:]).then_inc(S["rcb_ps"], 1)
            pe.wait_ge(S["rc_ready"], 1)
            mm(ps[:, 7, 0:1], ones[0:1, :], rc[:, 1:2], start=True, stop=True).then_inc(S["rcb_ps"], 1)
            pe.wait_ge(S["y_ready"], G)

            def k1_scores(g, j):
                b, h, n = g // NG, g % NG * GH + j, GH * g + j
                if n >= 2:
                    pe.wait_ge(S["k1_exp"], n - 1)
                mm(bank(4 + n % 2), KL(b, h, KROWS), QS1[b][0:KROWS, h, 0:T], start=True, stop=True).then_inc(S["k1_ps"], 1)

            def mix(g):
                pe.wait_ge(S["gaug_ready"], g + 1)
                pe.wait_ge(S["k1_exp"], GH * (g + 1))
                if g >= 1:
                    pe.wait_ge(S["xo_sb"], g)
                for j in range(GH):
                    r = mm(ps[32 * j:32 * j + VW, 6, :], Gaug[:, g % 2, j, :], PT[:, g % 2 * 4 + j, :],
                           start=True, stop=True)
                r.then_inc(S["x_ps"], 1)

            def turn_mix(g):
                pe.wait_ge(S["xo_sb"], g + 1)
                if g >= 1:
                    pe.wait_ge(S["xo_ready"], g)
                if g == 0:
                    pe.wait_ge(S["rcb_ready"], 1)
                for t in range(NT):
                    r = nc.tensor.transpose(ps[:, 7, tile(t)], outT[:, tile(t)], ident[:])
                r.then_inc(S["xtr_ps"], 1)

            def gates(b, bk):
                pe.wait_ge(S["ld_f1"], 112)
                pe.wait_ge(S["xn1_ready"], b + 1)
                for t in range(NT):
                    r = mm(ps[:, bk, t * E1:(t + 1) * E1], xnT[:, b, tile(t)], gateT[:], start=True, stop=True)
                r.then_inc(S["gate_ps"], 1)

            def turn_routing(b, bk):
                pe.wait_ge(S["cw1_ready"], b + 1)
                for t in range(NT):
                    r = nc.tensor.transpose(ps[0:PARTS * E1, bk, :].bitcast(BF16)[:, tile(t)],
                                            cwp1[:, b, t].rearrange("p i e -> p (i e)"), identb[:])
                r.then_inc(S["cw1T_ps"], 1)

            def up1(b, c):
                n = b * (C1 + 1) + c
                rows = P if c < C1 else I1
                if n >= 2:
                    last = n if c == 0 else n - 1
                    pe.wait_ge(S["gelu_ready"], last)
                    pe.wait_ge(S["gu_ready"], last)
                mm(ps[0:rows, c % 2, :], wg[:, tile(c)] if c < C1 else swg[:], xnT[:, b, :],
                   start=True, stop=True).then_inc(S["g_ps"], 1)
                mm(ps[0:rows, 2 + c % 2, :], wu[:, tile(c)] if c < C1 else swu[:], xnT[:, b, :],
                   start=True, stop=True).then_inc(S["uu_ps"], 1)

            def select1(b, c):
                m = b * C1 + c
                pe.wait_ge(S["cw1T_ready"], b + 1)
                if m >= 2:
                    pe.wait_ge(S["hid1_ready"], m - 1 + (1 if m - 2 >= C1 else 0))
                mm(bank(4 + m % 2), sel1[:, c, :], cwT[0:PARTS * E1, b, :], start=True, stop=True).then_inc(S["cs_ps"], 1)

            def down1(b, bk, *tiles):
                pe.wait_ge(S["hid1_ready"], (C1 + 1) * (b + 1))
                for t in tiles:
                    for c in range(C1 + 1):
                        rows = P if c < C1 else I1
                        r = mm(ps[:, bk, tile(t)], hid[0:rows, c, tile(t)], wd[:, c, :] if c < C1 else swd[:],
                               start=(c == 0), stop=(c == C1))
                if t == NT - 1:
                    r.then_inc(S["fin_ps"], 1)

            for q in range(G // 2):
                for s in range(2):
                    g = 2 * q + s
                    if g >= 2:
                        pe.wait_ge(S["wn_ready"], 2 * ((q - 1) * 2 * ITERS + (ITERS - 1) * 2 + s + 1))
                        squares(g)
                units = [(2 * q + k // GH, k % GH) for k in range(2 * GH)]
                for it in range(ITERS):
                    for s in range(2):
                        n = (q * ITERS + it) * 2 + s
                        W = Wb[:, 2 * s + it % 2]
                        for k in range(2):
                            if it == 0:
                                pe.wait_ge(S["w_ready"], 2 * (2 * q + s) + k + 1)
                            else:
                                pe.wait_ge(S["wn_ready"], 2 * (n - 2) + k + 1)
                            for j in (2 * k, 2 * k + 1):
                                r = mm(ps[:, 2 * s + k, j % 2 * WA:(j % 2 + 1) * WA], W[:, j, 0:P], W[:, j, :],
                                       start=True, stop=True)
                            r.then_inc(S["mm1_ps"], 1)
                    if it == 0 and q >= 1:
                        mix(2 * q - 2)
                    if it >= 1 and units:
                        k1_scores(*units.pop(0))
                    for s in range(2):
                        n = (q * ITERS + it) * 2 + s
                        for k in range(2):
                            pe.wait_ge(S["d_ready"], 2 * n + k + 1)
                            for j in (2 * k, 2 * k + 1):
                                r = mm(ps[:, 2 * s + k, j % 2 * WA:(j % 2 + 1) * WA], W2[:, s, j, 0:P], Db[:, s, j, :],
                                       start=True, stop=True)
                            r.then_inc(S["mm2_ps"], 1)
                    if it == 0 and q >= 1:
                        if q == 3:
                            pe.wait_ge(S["u_read"], B + 1)
                        turn_mix(2 * q - 2)
                        mix(2 * q - 1)
                        turn_mix(2 * q - 1)
                    elif units:
                        k1_scores(*units.pop(0))
                        if it >= 4 and units:
                            k1_scores(*units.pop(0))
                    if (q, it) == (2, 2):
                        adapter_in(0, 7, 1, x4)
                    if (q, it) == (2, 3):
                        adapter_down(0, 6, 1, a1, AD)
                    if (q, it) == (2, 4):
                        adapter_up(0, 7, 1, a2, AD)
                    if (q, it) == (3, 3):
                        turn_norm(0, 7, 1)
                    if (q, it) == (3, 4):
                        gates(0, 6)

            pe.wait_ge(S["wn_ready"], 2 * G * ITERS)
            up1(0, 0)
            mix(G - 2)
            up1(0, 1)
            turn_mix(G - 2)
            mix(G - 1)
            turn_mix(G - 1)
            turn_routing(0, 5)
            adapter_in(1, 6, 1, x4)
            select1(0, 0)
            pe.wait_ge(S["cw1T_ready"], 1)
            select1(0, 1)
            up1(0, 2)
            select1(0, 2)
            adapter_down(1, 7, 1, a1, AD)
            up1(0, 3)
            select1(0, 3)
            adapter_up(1, 6, 1, a2, AD)
            up1(0, 4)
            down1(0, 5, 0, 1, 2)
            turn_norm(1, 7, 1)
            gates(1, 6)
            up1(1, 0)
            up1(1, 1)
            down1(0, 5, 3)
            turn_routing(1, 7)
            up1(1, 2)
            select1(1, 0)
            pe.wait_ge(S["out_ready"], 1)
            select1(1, 1)
            up1(1, 3)
            select1(1, 2)
            select1(1, 3)
            up1(1, 4)
            down1(1, 6, *range(NT))

        @block.vector
        def _(dve):
            v = nc.vector
            steps = [0]

            def step(ins):
                steps[0] += 1
                ins.then_inc(S["step_dve"], 1)
                dve.wait_ge(S["step_dve"], steps[0])

            v.memset(ones[:], 1.0).then_inc(S["const_ready"], 1)
            v.memset(V[:], 1.0).then_inc(S["const_ready"], 1)
            dve.wait_ge(S["ld_qkv"], 96)

            def rest(m, src, dst, part):
                dve.wait_ge(S["part_a"], m + 1)
                v.tensor_tensor(dst, src, part[:, 0, :], ALU.subtract).then_inc(S["res_a"], 1)

            def last_part(m, src, part, done):
                dve.wait_ge(S["part_b"], m + 1)
                v.tensor_tensor(part[:, 2, :], src, part[:, 1, :], ALU.subtract).then_inc(done, 1)


            for n in range(4):
                b = n // 2
                dve.wait_ge(S["qk_ps"], 2 * n + 2)
                bk = [(5 * b + 2 * (n % 2) + k) % 8 for k in range(2)]
                if n >= 1:
                    dve.wait_ge(S["rot_done"], n)
                if n >= 2:
                    dve.wait_ge(S["part_c"], n - 1)
                v.tensor_tensor(rot[:, 0, :], bank(bk[0]), cos[:], ALU.mult).then_inc(S["rot_cos"], 1)
                v.tensor_tensor(rot[:, 1, :], bank(bk[1]), sin[:], ALU.mult).then_inc(S["rot_cos"], 1)
                dve.wait_ge(S["rot_cos"], 2 * n + 2)
                v.tensor_tensor(qk[:, n % 2, 0:T], rot[:, 0, :], rot[:, 1, :], ALU.add).then_inc(S["rot_done"], 1)
                if n % 2 == 1:
                    for m in (n - 1, n):
                        rest(m, qk[:, m % 2, 0:T], res[:, m % 2, 0:T], parts[:, m, :, 0:T])
                    for m in (n - 1, n):
                        last_part(m, res[:, m % 2, 0:T], parts[:, m, :, 0:T], S["part_c"])
            def s_max(m):
                g, u = m // UN, m % UN
                dve.wait_ge(S["smax_ps"], m + 1)
                if u == 0 and g >= 2:
                    dve.wait_ge(S["negT_ps"], g - 1)
                v.tensor_reduce(negm[:, g % 2, u:u + 1], bank(m % 3), AX.X, ALU.max, negate=True).then_inc(S["smax_done"], 1)

            def neg_copy(g):
                dve.wait_ge(S["negT_ps"], g + 1)
                if g >= 2:
                    dve.wait_ge(S["neg_split"], g - 1)
                v.tensor_copy(negR[0:UN, g % 2, :], ps[0:UN, 7, 0:P]).then_inc(S["neg_copy"], 1)

            def normalise(src, dst, ready, done):
                step(v.reciprocal(rden[:], src[:, :, :, HD]))
                v.tensor_tensor(dst, src[:, :, :, 0:HD],
                                rden[:].rearrange("p n (h o) -> p n h o", o=1).to_broadcast([P, NT, GH, HD]),
                                ALU.mult).then_inc(done, 1)

            heads4 = lambda k: ps[:, k, :].rearrange("p (n h d) -> p n h d", n=NT, h=GH)

            def outputs(g, tr, k, dst, done):
                dve.wait_ge(tr, g + 1)
                if g >= 1:
                    dve.wait_ge(done, g)
                b, gg = g // NG, g % NG
                normalise(heads4(k), dst[:, b, :, gg * 32:gg * 32 + 32].rearrange("p n (h d) -> p n h d", d=HD), None, done)

            def add_x(b, bk):
                dve.wait_ge(S["xbias_ready"], B)
                dve.wait_ge(S["proj_ps"], b + 1)
                v.tensor_tensor(x1[:, b].rearrange("p n f -> p (n f)"), bank(bk),
                                x[:, b].rearrange("p n f -> p (n f)"), ALU.add).then_inc(S["x1_ready"], 1)

            def norm_sum(b, bk, layer):
                dve.wait_ge(S[("u0_ps", "u1_ps")[layer]], b + 1)
                dve.wait_ge(S[("base0_ready", "base1_ready")[layer]], b + 1)
                v.tensor_tensor(y_of[layer][b].rearrange("p n f -> p (n f)"), bank(bk),
                                base_of[layer][b].rearrange("p n f -> p (n f)"), ALU.add).then_inc(S["u_read"], 1)

            def norm_stats(b, layer):
                dve.wait_ge(S["u_read"], B * layer + b + 1)
                for t in range(NT):
                    r = v.bn_stats(stats[:, b, t, :], y_of[layer][b][:, t, :])
                step(r)
                for t in range(NT):
                    r = v.bn_aggr(mv[:, b, t, :], stats[:, b, t, :])
                step(r)
                step(v.tensor_scalar(veps[:, b, :], mv[:, b, :, 1], EPS, None, ALU.add))
                v.reciprocal(rinv[:, b, :], veps[:, b, :]).then_inc(S["mv_ready"], 1)

            def norm_gain(b, layer, rows):
                dve.wait_ge(S[("ld_c0", "ld_ad")[layer]], 192)
                for t in range(NT):
                    r = v.scalar_tensor_tensor(out=x2_of[layer][b][:, t, :], in0=y_of[layer][b][:, t, :], scalar=mv[:, b, t, 0:1],
                                               in1=rows[:, b, 1, :], op0=ALU.subtract, op1=ALU.mult)
                step(r)

            def norm_newton(b, layer):
                dve.wait_ge(S["rstd_ready"], B * layer + b + 1)
                step(v.tensor_tensor(rinv[:, b, :], root[:, b, :], root[:, b, :], ALU.mult))
                step(v.tensor_tensor(rinv[:, b, :], rinv[:, b, :], veps[:, b, :], ALU.mult))
                step(v.tensor_scalar(rinv[:, b, :], rinv[:, b, :], -0.5, 1.5, ALU.mult, ALU.add))
                step(v.tensor_tensor(rstd[:, b, :], rinv[:, b, :], root[:, b, :], ALU.mult))

            def norm_scale(b, layer, rows):
                for t in range(NT):
                    r = v.scalar_tensor_tensor(out=x2_of[layer][b][:, t, :], in0=x2_of[layer][b][:, t, :], scalar=rstd[:, b, t:t + 1],
                                               in1=rows[:, b, 2, :], op0=ALU.mult, op1=ALU.add)
                r.then_inc(S[("n0_ready", "n1_ready")[layer]], 1)

            def to3(src, w, parts_out, tmp, done):
                step(v.tensor_copy(parts_out[:, :, 0, :], src))
                step(v.tensor_tensor(tmp, src, parts_out[:, :, 0, :], ALU.subtract))
                step(v.tensor_copy(parts_out[:, :, 1, :], tmp))
                v.tensor_tensor(parts_out[:, :, 2, :], tmp, parts_out[:, :, 1, :], ALU.subtract).then_inc(done, 1)

            def col(ap, n):
                return ap.rearrange("p (n o) -> p n o", o=1).to_broadcast([P, NT, n])

            def take_keys(b, bk):
                dve.wait_ge(S["sim_ps"], b + 1)
                v.tensor_copy(sim[:, b, :, 0:E0], ps[:, bk, 0:NT * E0].rearrange("p (n e) -> p n e", n=NT)
                              ).then_inc(S["sim_read"], 1)
                dve.wait_ge(S["sim_read"], b + 1)
                for t in range(NT):
                    r = v.max(best[:, b, t, :], sim[:, b, t, :])
                step(r)
                v.tensor_tensor(ex[:, b], sim[:, b, :, 0:E0], best[:, b, :, 0:1].to_broadcast([P, NT, E0]),
                                ALU.subtract).then_inc(S["sc_sub"], 1)
                step(v.tensor_copy(pick[:, b, :, 0:TOP0], best[:, b, :, 0:TOP0]))
                for t in range(NT):
                    r = v.match_replace(took[:, b, t, :], pick[:, b, t, :], sim[:, b, t, :], HIGH)
                step(r)
                step(v.tensor_tensor(took[:, b, :, 0:E0], took[:, b, :, 0:E0], sim[:, b, :, 0:E0], ALU.not_equal))

            def weigh_keys(b):
                dve.wait_ge(S["sc_exp"], b + 1)
                step(v.tensor_tensor(ex[:, b], ex2[:, b], took[:, b, :, 0:E0], ALU.mult))
                step(v.tensor_reduce(tot[:, b, :], ex[:, b], AX.X, ALU.add))
                step(v.reciprocal(totr[:, b, :], tot[:, b, :]))
                step(v.tensor_tensor(cw[:, b], ex[:, b], col(totr[:, b, :], E0), ALU.mult))
                to3(cw[:, b], E0, cwp[:, b], cwr[:, b], S["cwp_ready"])

            def copy_weights(b, bk):
                dve.wait_ge(S["cwT_ps"], b + 1)
                v.tensor_copy(cwT[:, b, :], ps[0:PARTS * E0, bk, :].bitcast(BF16)[:, 0:T]).then_inc(S["cwT_ready"], 1)

            def gate_hidden(b, *chunks):
                for c in chunks:
                    n = b * C0 + c
                    dve.wait_ge(S["silu_ready"], n + 1)
                    dve.wait_ge(S["sel_ps"], n + 1)
                    v.tensor_tensor(hid[:, c, :], hid[:, c, :], bank(2 + n % 2), ALU.mult).then_inc(S["hid_ready"], 1)

            def experts_out(b, bk):
                dve.wait_ge(S["ld_f0"], 112)
                dve.wait_ge(S["x12_ready"], b + 1)
                dve.wait_ge(S["down_ps"], b + 1)
                v.scalar_tensor_tensor(out=x3[:, b].rearrange("p n f -> p (n f)"), in0=bank(bk), scalar=scale[:, 0:1],
                                       in1=base[:, b].rearrange("p n f -> p (n f)"), op0=ALU.mult,
                                       op1=ALU.add).then_inc(S["x3_ready"], 1)

            def conditioned(b, bk):
                dve.wait_ge(S["ld_c1"], 160)
                dve.wait_ge(S["y1_ps"], b + 1)
                v.tensor_scalar(y1T[:, b, :], bank(bk), b2[:, b:b + 1], None, ALU.add).then_inc(S["y1_ready"], 1)

            def landmarks(n):
                b, k = n // 2, n % 2
                dve.wait_ge((S["l1q_ready"], S["l1k_ready"])[k], b + 1)
                step(v.tensor_reduce(res1[n][:, 0:LM], qk1[n][:, 0:T].rearrange("p (m s) -> p m s", s=SEG), AX.X, ALU.add))
                v.tensor_scalar(qk1[n][:, T:LW], res1[n][:, 0:LM], 1.0 / SEG, None, ALU.mult).then_inc(S["lm_ready"], 1)
                dve.wait_ge(S["lm_ready"], n + 1)

            def values1(b, bk):
                dve.wait_ge(S["l1v_ps"], b + 1)
                v.tensor_tensor(V[:, b, :, :, 0:HD], ps[:, bk, :].rearrange("p (n h d) -> p n h d", n=NT, h=H),
                                bvb[:].rearrange("p (o h d) -> p o h d", o=1, h=H).to_broadcast([P, NT, H, HD]),
                                ALU.add).then_inc(S["v1_ready"], 1)

            for b in range(B):
                step(v.memset(sim[:, b, :, E0:E0 + 8], LOW))
                step(v.memset(pick[:, b], LOW))
            for m in range(LAG):
                s_max(m)
                if m == UN:
                    neg_copy(0)
            for n in range(G * UN + UN):
                g, u = n // UN, n % UN
                if n + LAG < G * UN:
                    s_max(n + LAG)
                if u == 6 and g + 1 < G:
                    neg_copy(g + 1)
                if u == 9 and g >= 1:
                    outputs(g - 1, S["otr_ps"], 7, O, S["o_ready"])
                if (g, u) == (4, 14):
                    add_x(0, 7)
                if (g, u) == (5, 5):
                    norm_sum(0, 7, 0)
                if (g, u) == (5, 8):
                    norm_stats(0, 0)
                if (g, u) == (5, 11):
                    norm_gain(0, 0, rows0)
                if (g, u) == (5, 13):
                    norm_newton(0, 0)
                if (g, u) == (5, 14):
                    norm_scale(0, 0, rows0)
                if (g, u) == (6, 15):
                    take_keys(0, 7)
                if (g, u) == (7, 2):
                    weigh_keys(0)
                if (g, u) == (7, 15):
                    copy_weights(0, 7)

            def landmark_max(g):
                dve.wait_ge(S["k2_ps"], g + 1)
                if g >= 1:
                    dve.wait_ge(S["k2_exp"], GH * g)
                v.tensor_reduce(neg2[:], ps[:, 6, :].rearrange("p (h m) -> p h m", h=GH), AX.X, ALU.max,
                                negate=True).then_inc(S["k2_max"], 1)

            def maxima(g, u):
                n = 2 * GH * g + u
                dve.wait_ge(S["m_ps"], n + 1)
                if u == 0 and g >= 2:
                    dve.wait_ge(S["n_ps"], g - 1)
                c = u // 2 * 5
                src = bank(RING[n % 3])
                if u % 2 == 0:
                    r = v.tensor_reduce(negm[:, g % 2, c + 4:c + 5], src, AX.X, ALU.max, negate=True)
                else:
                    r = v.tensor_reduce(negm[:, g % 2, c:c + 4], src.rearrange("p (n m) -> p n m", n=NT),
                                        AX.X, ALU.max, negate=True)
                r.then_inc(S["m_done"], 1)

            def max_copy(g):
                dve.wait_ge(S["n_ps"], g + 1)
                if g >= 2:
                    dve.wait_ge(S["n_split"], g - 1)
                v.tensor_copy(negR[0:20, g % 2, :], ps[0:20, 5, 0:P]).then_inc(S["n_copy"], 1)

            def landmark_sums(g):
                dve.wait_ge(S["k2_exp"], GH * (g + 1))
                if g >= 1:
                    dve.wait_ge(S["a_ready"], g)
                v.reciprocal(rsum[:], sums[:]).then_inc(S["rs_ready"], 1)

            def column_max(b):
                dve.wait_ge(S["col_copy"], NG * (b + 1))
                step(v.tensor_reduce(cmax[:, b:b + 1], colsum[:, b, :], AX.X, ALU.max))

            def values(g):
                dve.wait_ge(S["ytr_ps"], g + 1)
                src = ps[:, 5, 0:P].rearrange("p (h d) -> p h d", h=GH)
                if g >= 1:
                    dve.wait_ge(S["y_ready"], g)
                step(v.reciprocal(rden[:, 0, :], src[:, :, HD]))
                v.tensor_tensor(AY[:, GH * g:GH * g + GH, P:WA], src[:, :, 0:HD],
                                rden[:, 0, :].rearrange("p (h o) -> p h o", o=1).to_broadcast([P, GH, HD]),
                                ALU.mult).then_inc(S["y_ready"], 1)

            gate_hidden(0, 0, 1)
            add_x(1, 5)
            gate_hidden(0, 2, 3, 4)
            norm_sum(1, 4, 0)
            gate_hidden(0, 5, 6, 7)
            norm_stats(1, 0)
            norm_gain(1, 0, rows0)
            norm_newton(1, 0)
            norm_scale(1, 0, rows0)
            experts_out(0, 6)
            take_keys(1, 5)
            weigh_keys(1)
            dve.wait_ge(S["ld_l1"], 48)
            v.tensor_scalar(bl1s[:], bl1[:], QSCALE, None, ALU.mult).then_inc(S["bl1_ready"], 1)
            copy_weights(1, 4)
            conditioned(0, 6)

            def rest1(n):
                rest(4 + n, qk1[n], res1[n], parts1[n])

            def last1(n):
                last_part(4 + n, res1[n], parts1[n], S["l1_parts"])

            landmarks(0)
            landmarks(1)
            gate_hidden(1, 0)
            rest1(0)
            gate_hidden(1, 1)
            rest1(1)
            gate_hidden(1, 2)
            last1(0)
            gate_hidden(1, 3)
            last1(1)
            values1(0, 7)
            gate_hidden(1, *range(4, C0))
            landmark_max(0)
            for u in range(2 * GH):
                maxima(0, u)
                if u == 4:
                    landmark_sums(0)
                if u == 5:
                    experts_out(1, 4)
            landmark_max(1)
            for u in range(2 * GH):
                maxima(1, u)
                if u == 2:
                    max_copy(0)
                if u == 4:
                    conditioned(1, 4)
            landmark_sums(1)
            max_copy(1)
            landmarks(2)
            landmarks(3)
            for g in range(G):
                ahead = g + 2 < G
                if 1 < g + 1 < G:
                    max_copy(g + 1)
                if ahead:
                    landmark_max(g + 2)
                for u in range(2 * GH):
                    if ahead:
                        maxima(g + 2, u)
                    if u == 2 and g >= 1:
                        values(g - 1)
                    if u == 7 and ahead:
                        landmark_sums(g + 2)
                    if g == 0 and u == 2:
                        values1(1, 4)
                    if g == NG and u == 3:
                        column_max(0)
            values(G - 1)

            column_max(1)
            v.tensor_reduce(cmax[:, 2:3], cmax[:, 0:2], AX.X, ALU.max).then_inc(S["col_done"], 1)
            dve.wait_ge(S["rcb_ps"], 1)
            step(v.tensor_reduce(rc[:, 0:1], ps[0:1, 7, P:2 * P], AX.X, ALU.max))
            v.reciprocal(rc[:, 1:2], rc[:, 0:1]).then_inc(S["rc_ready"], 1)
            dve.wait_ge(S["rcb_ps"], 2)
            v.tensor_copy(rcb[:], ps[:, 7, 0:1]).then_inc(S["rcb_ready"], 1)
            v.memset(Gaug[:], 1.0).then_inc(S["gaug_ones"], 1)

            def add_x3(b):
                dve.wait_ge(S["xo_ready"], NG * (b + 1))
                v.tensor_tensor(x4[:, b], O[:, b], x3[:, b], ALU.add).then_inc(S["x4_ready"], 1)

            def gate_scores(b, bk):
                dve.wait_ge(S["gate_ps"], b + 1)
                lg = ps[:, bk, 0:NT * E1].rearrange("p (n e) -> p n e", n=NT)
                step(v.tensor_reduce(tot[:, b, :], lg, AX.X, ALU.max))
                v.tensor_tensor(ex[:, b, :, 0:E1], lg, col(tot[:, b, :], E1), ALU.subtract).then_inc(S["sc_sub"], 1)
                step(v.memset(sim1[:, b, :, E1:16], LOW))
                step(v.memset(pick[:, b], LOW))

            def take_experts(b):
                dve.wait_ge(S["sc_exp"], B + b + 1)
                step(v.tensor_reduce(tot[:, b, :], ex2[:, b, :, 0:E1], AX.X, ALU.add))
                step(v.reciprocal(totr[:, b, :], tot[:, b, :]))
                step(v.tensor_tensor(sim1[:, b, :, 0:E1], ex2[:, b, :, 0:E1], col(totr[:, b, :], E1), ALU.mult))
                for t in range(NT):
                    r = v.max(best[:, b, t, :], sim1[:, b, t, :])
                step(r)
                step(v.tensor_copy(pick[:, b, :, 0:TOP1], best[:, b, :, 0:TOP1]))
                for t in range(NT):
                    r = v.match_replace(took1[:, b, t, :], pick[:, b, t, :], sim1[:, b, t, :], HIGH)
                step(r)

            def weigh_experts(b):
                step(v.tensor_tensor(ex[:, b, :, 0:E1], took1[:, b, :, 0:E1], sim1[:, b, :, 0:E1], ALU.not_equal))
                step(v.tensor_reduce(tot[:, b, :], best[:, b, :, 0:TOP1], AX.X, ALU.add))
                step(v.tensor_scalar(tot[:, b, :], tot[:, b, :], 1e-20, None, ALU.add))
                step(v.reciprocal(totr[:, b, :], tot[:, b, :]))
                step(v.tensor_tensor(ex2[:, b, :, 0:E1], ex[:, b, :, 0:E1], sim1[:, b, :, 0:E1], ALU.mult))
                step(v.tensor_tensor(cw[:, b, :, 0:E1], ex2[:, b, :, 0:E1], col(totr[:, b, :], E1), ALU.mult))
                to3(cw[:, b, :, 0:E1], E1, cwp1[:, b], cwr[:, b, :, 0:E1], S["cw1_ready"])

            def copy_routing(b, bk):
                dve.wait_ge(S["cw1T_ps"], b + 1)
                v.tensor_copy(cwT[0:PARTS * E1, b, :], ps[0:PARTS * E1, bk, :].bitcast(BF16)[:, 0:T]).then_inc(S["cw1T_ready"], 1)

            def gate_up(b, c):
                n = b * (C1 + 1) + c
                dve.wait_ge(S["gelu_ready"], n + 1)
                dve.wait_ge(S["uu_ps"], n + 1)
                if n >= 2:
                    dve.wait_ge(S["hid1_ready"], n - 1)
                v.tensor_tensor(gu_sb[:, n % 2, :], act_sb[:, n % 2, :], bank(2 + c % 2), ALU.mult).then_inc(S["gu_ready"], 1)

            def weigh_hidden(b, c):
                n, m = b * (C1 + 1) + c, b * C1 + c
                if b == 1 and c == 0:
                    dve.wait_ge(S["fin_ps"], 1)
                dve.wait_ge(S["gu_ready"], n + 1)
                dve.wait_ge(S["cs_ps"], m + 1)
                v.tensor_tensor(hid[:, c, :], gu_sb[:, n % 2, :], bank(4 + m % 2), ALU.mult).then_inc(S["hid1_ready"], 1)

            def shared_hidden(b):
                n, c = b * (C1 + 1) + C1, C1
                dve.wait_ge(S["gelu_ready"], n + 1)
                dve.wait_ge(S["uu_ps"], n + 1)
                v.tensor_tensor(hid[0:I1, c, :], act_sb[0:I1, n % 2, :], ps[0:I1, 2 + c % 2, :],
                                ALU.mult).then_inc(S["hid1_ready"], 1)
                dve.wait_ge(S["hid1_ready"], n + 1)
                v.memset(gu_sb[0:1, n % 2, 0:1], 0.0).then_inc(S["gu_ready"], 1)

            def result(b, bk):
                dve.wait_ge(S["fin_ps"], b + 1)
                v.tensor_tensor(y1[b].rearrange("p n f -> p (n f)"), bank(bk),
                                x4[:, b].rearrange("p n f -> p (n f)"), ALU.add).then_inc(S["out_ready"], 1)

            dve.wait_ge(S["gaug_ones"], 1)
            for q in range(G // 2):
                for it in range(ITERS):
                    for s in range(2):
                        n = (q * ITERS + it) * 2 + s
                        W = Wb[:, 2 * s + it % 2]
                        for k in range(2):
                            dve.wait_ge(S["w2_ready"], 2 * n + k + 1)
                            v.scalar_tensor_tensor(out=two_heads(Db[:, s], k), in0=two_heads(W, k), scalar=7 * C2,
                                                   in1=two_heads(W2[:, s], k), op0=ALU.mult,
                                                   op1=ALU.subtract).then_inc(S["d_ready"], 1)
                    for s in range(2):
                        n = (q * ITERS + it) * 2 + s
                        dve.wait_ge(S["f_ready"], n + 1)
                        for k in range(2):
                            dve.wait_ge(S["mm2_ps"], 2 * n + k + 1)
                            v.scalar_tensor_tensor(out=two_heads(Wb[:, 2 * s + (it + 1) % 2], k), in0=half(s, k),
                                                   scalar=0.25 / (C2 * C2), in1=two_heads(Fb[:, s], k), op0=ALU.mult,
                                                   op1=ALU.add).then_inc(S["wn_ready"], 1)
                    if it == 0 and q >= 1:
                        for s in range(2):
                            outputs(2 * q - 2 + s, S["xtr_ps"], 7, O, S["xo_ready"])
                    if (q, it) == (2, 1):
                        add_x3(0)
                    if (q, it) == (2, 4):
                        norm_sum(0, 7, 1)
                    if (q, it) == (2, 5):
                        norm_stats(0, 1)
                    if (q, it) == (3, 0):
                        norm_gain(0, 1, rows1)
                    if (q, it) == (3, 1):
                        norm_newton(0, 1)
                    if (q, it) == (3, 2):
                        norm_scale(0, 1, rows1)
                    if (q, it) == (3, 4):
                        gate_scores(0, 6)
                for s in range(2):
                    g = 2 * q + s
                    dve.wait_ge(S["wn_ready"], 2 * ((q * ITERS + ITERS - 1) * 2 + s + 1))
                    if g >= 2:
                        dve.wait_ge(S["x_ps"], g - 1)
                    v.tensor_copy(Gaug[:, s, :, 0:HD], Wb[:, 2 * s + ITERS % 2, :, P:WA]).then_inc(S["gaug_ready"], 1)
            take_experts(0)
            weigh_experts(0)
            for g in (G - 2, G - 1):
                outputs(g, S["xtr_ps"], 7, O, S["xo_ready"])
            add_x3(1)
            copy_routing(0, 5)
            for c in range(C1):
                gate_up(0, c)
                weigh_hidden(0, c)
            norm_sum(1, 6, 1)
            norm_stats(1, 1)
            shared_hidden(0)
            norm_gain(1, 1, rows1)
            norm_newton(1, 1)
            norm_scale(1, 1, rows1)
            gate_scores(1, 6)
            take_experts(1)
            weigh_experts(1)
            gate_up(1, 0)
            copy_routing(1, 7)
            gate_up(1, 1)
            result(0, 5)
            weigh_hidden(1, 0)
            weigh_hidden(1, 1)
            for c in range(2, C1):
                gate_up(1, c)
                weigh_hidden(1, c)
            shared_hidden(1)
            result(1, 6)

        @block.scalar
        def _(act):
            f = nc.scalar.activation

            act.wait_ge(S["ld_in"], 48)
            for b in range(B):
                if b == 1:
                    act.wait_ge(S["ld_qkv"], 96)
                act.wait_ge(S["y0_ps"], b + 1)
                f(y0T[:, b, :], bank(5 + b), ACT.Identity, bias=b0[:, b:b + 1]).then_inc(S["y0_ready"], 1)

            for b in range(B):
                for n in (2 * b, 2 * b + 1):
                    act.wait_ge(S["rot_done"], n + 1)
                    f(parts[:, n, 0, 0:T], qk[:, n % 2, 0:T], ACT.Copy).then_inc(S["part_a"], 1)
                for n in (2 * b, 2 * b + 1):
                    act.wait_ge(S["res_a"], n + 1)
                    f(parts[:, n, 1, 0:T], res[:, n % 2, 0:T], ACT.Copy).then_inc(S["part_b"], 1)
                act.wait_ge(S["const_ready"], 2)
                act.wait_ge(S["v_ps"], b + 1)
                f(V[:, b, :, :, 0:HD], ps[:, (5 * b + 4) % 8, :].rearrange("p (n h d) -> p n h d", n=NT, h=H),
                  ACT.Copy).then_inc(S["vaug_ready"], 1)

            def copy_out(b, bk):
                act.wait_ge(S["oT_ps"], b + 1)
                f(featT[:, b, :], bank(bk), ACT.Copy).then_inc(S["oT_ready"], 1)

            def copy_in(b, bk, layer):
                act.wait_ge(S[("t0_ps", "t1_ps")[layer]], b + 1)
                f(featT[:, b, :], bank(bk), ACT.Copy).then_inc(S[("t0_ready", "t1_ready")[layer]], 1)

            def adapter_relu(b, bk, layer, rows, bias):
                act.wait_ge(S[("ld_c0", "ld_ad")[layer]], 192)
                act.wait_ge(S[("z0_ps", "z1_ps")[layer]], b + 1)
                f(zT_of[layer][b][0:rows, :], ps[0:rows, bk, :], ACT.Relu, bias=bias[:, b:b + 1]
                  ).then_inc(S[("z0_ready", "z1_ready")[layer]], 1)

            def norm_root(b, layer):
                act.wait_ge(S["mv_ready"], B * layer + b + 1)
                f(root[:, b, :], rinv[:, b, :], ACT.Sqrt).then_inc(S["rstd_ready"], 1)

            def copy_norm(b, bk, layer):
                act.wait_ge(S[("xn0_ps", "xn1_ps")[layer]], b + 1)
                f(xnT[:, b, :], bank(bk), ACT.Copy).then_inc(S[("xn0_ready", "xn1_ready")[layer]], 1)

            def copy_hash(b, bk):
                act.wait_ge(S["hash_ps"], b + 1)
                f(hT[:, b, :], ps[0:PD, bk, :], ACT.Copy).then_inc(S["hash_ready"], 1)

            def key_exp(b):
                act.wait_ge(S["sc_sub"], b + 1)
                f(ex2[:, b], ex[:, b], ACT.Exp).then_inc(S["sc_exp"], 1)

            def silu(b, *chunks):
                for c in chunks:
                    n = b * C0 + c
                    act.wait_ge(S["up_proj_ps"], n + 1)
                    if b >= 1:
                        act.wait_ge(S["down_ps"], b)
                    f(hid[:, c, :], bank(n % 2), ACT.Silu).then_inc(S["silu_ready"], 1)

            def copy_x3(b, bk):
                act.wait_ge(S["x3T_ps"], b + 1)
                f(featT[:, b, :], bank(bk), ACT.Copy).then_inc(S["x3T_ready"], 1)

            def gelu_hidden(b, *banks):
                act.wait_ge(S["ld_c1"], 160)
                if b >= 1:
                    act.wait_ge(S["y1_ps"], b)
                for c, bk in enumerate(banks):
                    act.wait_ge(S["h1_ps"], HC * b + c + 1)
                    f(hc[:, c, :], bank(bk), ACT.Gelu, bias=b1[:, c:c + 1]).then_inc(S["h1_ready"], 1)

            def project(n, bk):
                b, k = n // 2, n % 2
                act.wait_ge(S["bl1_ready"], 1)
                act.wait_ge((S["l1q_ps"], S["l1k_ps"])[k], b + 1)
                f(qk1[n][:, 0:T], bank(bk), ACT.Identity, bias=bl1s[:, k:k + 1],
                  scale=QSCALE).then_inc((S["l1q_ready"], S["l1k_ready"])[k], 1)

            def part1(n):
                act.wait_ge(S["lm_ready"], n + 1)
                f(parts1[n][:, 0, :], qk1[n], ACT.Copy).then_inc(S["part_a"], 1)

            def part2(n):
                act.wait_ge(S["res_a"], 4 + n + 1)
                f(parts1[n][:, 1, :], res1[n], ACT.Copy).then_inc(S["part_b"], 1)

            def landmark_exp(g):
                act.wait_ge(S["k2_max"], g + 1)
                if g >= 1:
                    act.wait_ge(S["a_ready"], g)
                for j in range(GH):
                    f(ek2[:, j, :], ps[:, 6, tile(j)], ACT.Exp, bias=neg2[:, j:j + 1],
                      accum_out=sums[:, j:j + 1]).then_inc(S["k2_exp"], 1)

            for n in range(G * UN + UN):
                g, k, u = n // UN, n // GH, n % UN
                if n < G * UN:
                    act.wait_ge(S["st_ps"], n + 1)
                    if k >= 2:
                        act.wait_ge(S["av_ps"], k - 1)
                    f(PT[:, k % 2 * 4 + n % GH, :], bank(3 + n % 3), ACT.Exp, scale=MAPS).then_inc(S["exp_done"], 1)
                if u == 2 and g >= 1:
                    act.wait_ge(S["av_ps"], NT * g)
                    if g >= 2:
                        act.wait_ge(S["otr_ps"], g - 1)
                    f(outT[:], bank(6), ACT.Copy).then_inc(S["outT_ready"], 1)
                if (g, u) == (4, 12):
                    copy_out(0, 7)
                if (g, u) == (5, 1):
                    copy_in(0, 7, 0)
                if (g, u) == (5, 3):
                    adapter_relu(0, 7, 0, P, bdn)
                if (g, u) == (5, 9):
                    norm_root(0, 0)
                if (g, u) == (6, 11):
                    copy_norm(0, 7, 0)
                if (g, u) == (6, 13):
                    copy_hash(0, 7)
                if (g, u) == (7, 0):
                    key_exp(0)

            silu(0, 0)
            copy_out(1, 4)
            silu(0, 1, 2)
            copy_in(1, 4, 0)
            silu(0, 3)
            adapter_relu(1, 5, 0, P, bdn)
            silu(0, 4, 5, 6, 7)
            norm_root(1, 0)
            copy_norm(1, 5, 0)
            copy_hash(1, 4)
            copy_x3(0, 7)
            key_exp(1)
            gelu_hidden(0, 0, 1, 2, 3)
            project(0, 1)
            project(1, 3)
            silu(1, 0)
            part1(0)
            silu(1, 1)
            part1(1)
            silu(1, 2)
            part2(0)
            silu(1, 3)
            part2(1)
            silu(1, *range(4, C0))
            landmark_exp(0)
            copy_x3(1, 3)
            gelu_hidden(1, 2, 4, 3, 2)
            landmark_exp(1)
            act.wait_ge(S["y1_ps"], B)
            project(2, 2)
            project(3, 3)

            def value_exp(g, *heads):
                for j in heads:
                    n = GH * g + j
                    act.wait_ge(S["k3_ps"], n + 1)
                    if g >= 2:
                        act.wait_ge(S["yv_ps"], g - 1)
                    f(PT[:, g % 2 * 4 + j, :], bank(2 + n % 2), ACT.Exp).then_inc(S["k3_exp"], 1)

            def copy_columns(g):
                act.wait_ge(S["col_ps"], g + 1)
                k = g % NG * 32
                f(colsum[k:k + 32, g // NG, :], ps[k:k + 32, 5, :], ACT.Copy).then_inc(S["col_copy"], 1)

            def copy_values(g):
                act.wait_ge(S["yv_ps"], g + 1)
                if g >= 1:
                    act.wait_ge(S["ytr_ps"], g)
                f(ysb[:], ps[:, 4, 0:P], ACT.Copy).then_inc(S["yv_sb"], 1)

            for g in range(G):
                value_exp(g, 0)
                if g == 0:
                    part1(2)
                value_exp(g, 1)
                if g == 0:
                    part1(3)
                value_exp(g, 2, 3)
                if g == 0:
                    part2(2)
                if g + 2 < G:
                    landmark_exp(g + 2)
                if g == 0:
                    part2(3)
                copy_columns(g)
                copy_values(g)

            act.wait_ge(S["rcb_ready"], 1)
            def k1_exp(g, j):
                n = GH * g + j
                act.wait_ge(S["k1_ps"], n + 1)
                if g >= 2:
                    act.wait_ge(S["x_ps"], g - 1)
                if g < 2:
                    act.wait_ge(S["yv_ps"], G)
                f(PT[:, g % 2 * 4 + j, :], bank(4 + n % 2), ACT.Exp).then_inc(S["k1_exp"], 1)

            def copy_mix(g):
                act.wait_ge(S["x_ps"], g + 1)
                if g >= 1:
                    act.wait_ge(S["xtr_ps"], g)
                f(outT[:], bank(6), ACT.Copy).then_inc(S["xo_sb"], 1)

            def gate_exp(b):
                act.wait_ge(S["sc_sub"], B + b + 1)
                f(ex2[:, b, :, 0:E1], ex[:, b, :, 0:E1], ACT.Exp).then_inc(S["sc_exp"], 1)

            def gelu(b, *chunks):
                for c in chunks:
                    n = b * (C1 + 1) + c
                    rows = P if c < C1 else I1
                    act.wait_ge(S["g_ps"], n + 1)
                    if n >= 2:
                        act.wait_ge(S["gu_ready"], n - 1)
                    f(act_sb[0:rows, n % 2, :], ps[0:rows, c % 2, :], ACT.Gelu).then_inc(S["gelu_ready"], 1)

            for q in range(G // 2):
                for s in range(2):
                    g = 2 * q + s
                    if g >= 2:
                        act.wait_ge(S["gaug_ready"], g - 1)
                    for k in range(2):
                        act.wait_ge(S["sq_ps"], 2 * g + k + 1)
                        f(two_heads(Wb[:, 2 * s], k), half(s, k), ACT.Copy, scale=rcb[:, 0:1]).then_inc(S["w_ready"], 1)
                units = [(2 * q + k // GH, k % GH) for k in range(2 * GH)]
                for it in range(ITERS):
                    for s in range(2):
                        n = (q * ITERS + it) * 2 + s
                        if it == 0:
                            act.wait_ge(S["w_ready"], 2 * (2 * q + s + 1))
                        if n >= 2:
                            act.wait_ge(S["wn_ready"], 2 * (n - 1))
                        f(Fb[:, s], Wb[:, 2 * s + it % 2], ACT.Copy, scale=C1W).then_inc(S["e_ready"], 1)
                        for k in range(2):
                            act.wait_ge(S["mm1_ps"], 2 * n + k + 1)
                            f(two_heads(W2[:, s], k), half(s, k), ACT.Copy, scale=C2).then_inc(S["w2_ready"], 1)
                    if it == 0:
                        if q >= 1:
                            copy_mix(2 * q - 2)
                            copy_mix(2 * q - 1)
                        else:
                            k1_exp(*units.pop(0))
                    else:
                        for _ in range(3 if it >= 4 else 2):
                            if units:
                                k1_exp(*units.pop(0))
                    if (q, it) == (2, 2):
                        copy_in(0, 7, 1)
                    if (q, it) == (2, 3):
                        adapter_relu(0, 6, 1, AD, ab1)
                    if (q, it) == (3, 0):
                        norm_root(0, 1)
                    if (q, it) == (3, 3):
                        copy_norm(0, 7, 1)
                    if (q, it) == (3, 4):
                        gate_exp(0)
            copy_mix(G - 2)
            gelu(0, 0)
            copy_mix(G - 1)
            gelu(0, 1)
            copy_in(1, 6, 1)
            gelu(0, 2)
            adapter_relu(1, 7, 1, AD, ab1)
            gelu(0, 3, 4)
            norm_root(1, 1)
            copy_norm(1, 7, 1)
            gate_exp(1)
            gelu(1, *range(C1 + 1))

        @block.gpsimd
        def _(pool):
            g_ = nc.gpsimd
            two = float(np.array([0x3F803F80], np.uint32).view(np.float32)[0])
            g_.memset(KS[64:96, :, :].bitcast(F32), two).then_inc(S["ones_rows"], 1)
            pool.wait_ge(S["ones_rows"], 1)
            pool.wait_ge(S["ld_res"], 96)
            for b in range(B):
                r = g_.tensor_tensor(x[:, b], x[:, b], boutb[:].rearrange("p (o f) -> p o f", o=1).to_broadcast([P, NT, P]),
                                     ALU.add)
                r.then_inc(S["xbias_ready"], 1)
                pool.wait_ge(S["xbias_ready"], b + 1)
            negsteps = [0]

            def split_rows(copied, done, g, rows, sent, before):
                pool.wait_ge(copied, g + 1)
                if g >= 2:
                    pool.wait_ge(sent[g % 2], 16 * PARTS * (g // 2))
                elif before:
                    pool.wait_ge(S["neg_rows"][g % 2], 16 * PARTS * G // 2)
                src, part = negR[0:rows, g % 2, :], [negT[0:rows, g % 2, i, :] for i in range(PARTS)]
                left = negS[0:rows, :]

                def step(ins):
                    negsteps[0] += 1
                    ins.then_inc(S["neg_step"], 1)
                    pool.wait_ge(S["neg_step"], negsteps[0])

                step(g_.tensor_copy(part[0], src))
                step(g_.tensor_tensor(left, src, part[0], ALU.subtract))
                step(g_.tensor_copy(part[1], left))
                g_.tensor_tensor(part[2], left, part[1], ALU.subtract).then_inc(done, 1)
                pool.wait_ge(done, g + 1)

            def add_bias(b):
                pool.wait_ge(S["ld_c0"], 192)
                pool.wait_ge(S["x1_ready"], b + 1)
                g_.tensor_tensor(base[:, b], x1[:, b], rows0[:, b, 0:1, :].to_broadcast([P, NT, P]),
                                 ALU.add).then_inc(S["base0_ready"], 1)
                pool.wait_ge(S["base0_ready"], b + 1)

            def add_norm(b):
                pool.wait_ge(S["n0_ready"], b + 1)
                g_.tensor_tensor(base[:, b], x1[:, b], x2[:, b], ALU.add).then_inc(S["x12_ready"], 1)
                pool.wait_ge(S["x12_ready"], b + 1)

            for g in range(G):
                split_rows(S["neg_copy"], S["neg_split"], g, UN, S["neg_rows"], 0)
                if g == 5:
                    add_bias(0)
                if g == 6:
                    add_norm(0)
            add_bias(1)
            add_norm(1)
            def landmark_attention(g):
                pool.wait_ge(S["rs_ready"], g + 1)
                if g == 4:
                    for n in (2, 3):
                        pool.wait_ge(S["parts_out"][n], parts_out(n, 1))
                g_.tensor_tensor(AY[:, GH * g:GH * g + GH, 0:P], ek2[:],
                                 rsum[:].rearrange("p (h o) -> p h o", o=1).to_broadcast([P, GH, P]),
                                 ALU.mult).then_inc(S["a_ready"], 1)
                pool.wait_ge(S["a_ready"], g + 1)

            landmark_attention(0)
            split_rows(S["n_copy"], S["n_split"], 0, 20, S["n_rows"], G)
            landmark_attention(1)
            split_rows(S["n_copy"], S["n_split"], 1, 20, S["n_rows"], G)
            for n in (2, 3):
                pool.wait_ge(S["part_a"], 4 + n + 1)
                g_.tensor_tensor(res1[n], qk1[n], parts1[n][:, 0, :], ALU.subtract).then_inc(S["res_a"], 1)
                pool.wait_ge(S["res_a"], 4 + n + 1)
            for n in (2, 3):
                pool.wait_ge(S["part_b"], 4 + n + 1)
                g_.tensor_tensor(parts1[n][:, 2, :], res1[n], parts1[n][:, 1, :], ALU.subtract).then_inc(S["l1_parts"], 1)
                pool.wait_ge(S["l1_parts"], n + 1)
            for g in range(G):
                if 1 < g + 1 < G:
                    split_rows(S["n_copy"], S["n_split"], g + 1, 20, S["n_rows"], G)
                if g + 2 < G:
                    landmark_attention(g + 2)
            def add_bias1(b):
                pool.wait_ge(S["ld_ad"], 192)
                pool.wait_ge(S["x4_ready"], b + 1)
                g_.tensor_tensor(base1[b], x4[:, b], rows1[:, b, 0:1, :].to_broadcast([P, NT, P]),
                                 ALU.add).then_inc(S["base1_ready"], 1)
                pool.wait_ge(S["base1_ready"], b + 1)

            for n in range(G // 2 * ITERS * 2):
                pool.wait_ge(S["w2_ready"], 2 * (n + 1))
                pool.wait_ge(S["e_ready"], n + 1)
                g_.tensor_tensor(Fb[:, n % 2], Fb[:, n % 2], W2[:, n % 2], ALU.subtract).then_inc(S["f_ready"], 1)
                pool.wait_ge(S["f_ready"], n + 1)
                if n == (2 * ITERS + 2) * 2 + 1:
                    add_bias1(0)
            add_bias1(1)


def tables():
    f = np.float32
    inv = (f(1.0) / np.power(f(10000.0), (np.arange(0, HD, 2, dtype=f) / f(HD)))).astype(f)
    fr = np.arange(T, dtype=f)[:, None] * inv[None, :]
    emb = np.concatenate((fr, fr), axis=-1)
    cos, sin = np.cos(emb).astype(f), np.sin(emb).astype(f)
    sign = np.where(np.arange(HD) < HD // 2, f(-1), f(1))
    spread = lambda m: np.ascontiguousarray(np.repeat(m.T, H, axis=0))
    ident = np.eye(P, dtype=f)
    bf = lambda m: (m * 0x3F80).astype(np.uint16)

    def select(experts, width, chunks):
        s = np.zeros((PARTS, experts, chunks, P), f)
        for c in range(chunks):
            for m in range(P):
                s[:, (c * P + m) // width, c, m] = 1
        return bf(s.reshape(PARTS * experts, chunks, P))

    return {"cos": spread(cos), "sin": spread(sin * sign), "ident": ident, "identb": bf(ident),
            "sel0": select(E0, PD, C0), "sel1": select(E1, I1, C1)}


def kernel(**inputs):
    import concourse.bacc as bacc
    from concourse.bass_utils import run_bass_kernel_spmd

    w = {k: np.asarray(v) for k, v in inputs.items()}
    c = np.ascontiguousarray
    dh = np.arange(H * HD).reshape(H, HD).T.reshape(-1)
    turned = [1, 3, 5, 7, 0, 2, 4, 6]
    dhr = np.arange(H * HD).reshape(H, HD)[:, turned].T.reshape(-1)
    q, k, v = np.split(w["L0_attn_w_qkv"], 3, axis=0)
    data = {
        "ids": np.concatenate([w["itok_B_0_7"], w["itok_B_0_6"], w["itok_B_0_8"]])[None, :],
        "x": w["x"], "xT": w["x"].transpose(0, 2, 1),
        "w0T": w["L0_cond_weight"].transpose(0, 2, 1), "b0": w["L0_cond_bias"],
        "wqkT": np.stack([q[dh].T, q[dhr].T, k[dh].T, k[dhr].T]), "wvT": v.T,
        "woutT": w["L0_attn_w_out"].T, "bout": w["L0_attn_b_out"][None, :],
        "down": w["L0_cond2_down_w"], "bd": w["L0_cond2_down_b"], "up": w["L0_cond2_up_w"],
        "bu": w["L0_cond2_up_b"], "ln_g": w["L0_cond2_ln_g"], "ln_b": w["L0_cond2_ln_b"],
        "hashT": w["L0_ffn_hasher_w"].T, "keysT": w["L0_ffn_keys"].T, "vd": w["L0_ffn_values_down"],
        "vu": w["L0_ffn_values_up"], "scale": w["L0_ffn_scale"][None, :],
        "w1": w["L1_cond_W1"], "b1": w["L1_cond_b1"].reshape(HC, P).T, "w2": w["L1_cond_W2"], "b2": w["L1_cond_b2"],
        "we": w["L1_cond_We"], "be": w["L1_cond_be"],
        "wl1T": np.stack([w["L1_attn_Wq"][dh].T, w["L1_attn_Wk"][dh].T, w["L1_attn_Wv"].T]),
        "bl1": np.stack([w["L1_attn_bq"][dh], w["L1_attn_bk"][dh]], axis=1), "bv": w["L1_attn_bv"][None, :],
        "a1": w["L1_cond2_W1"], "ab1": w["L1_cond2_b1"], "a2": w["L1_cond2_W2"], "ab2": w["L1_cond2_b2"],
        "gamma": w["L1_cond2_gamma"], "beta": w["L1_cond2_beta"],
        "gateT": w["L1_ffn_gate_w"].T, "wg": w["L1_ffn_Wg"], "wu": w["L1_ffn_Wu"], "wd": w["L1_ffn_Wd"],
        "swg": w["L1_ffn_sWg"], "swu": w["L1_ffn_sWu"], "swd": w["L1_ffn_sWd"],
        **tables(),
    }
    nc = bacc.Bacc("TRN2", target_bir_lowering=False, num_devices=1)
    arrays, aps = {}, {}
    for name, value in data.items():
        arrays[f"in_{name}"] = c(value)
        aps[name] = nc.dram_tensor(f"in_{name}", value.shape, mybir.dt.from_np(value.dtype), kind="ExternalInput").ap()
    out = nc.dram_tensor("out_0", (B, T, P), F32, kind="ExternalOutput").ap()
    build(nc, aps, out)
    r = run_bass_kernel_spmd(nc, [arrays], core_ids=[0])
    return r.results[0]["out_0"]
```
